# Optimizing a Trainium2 kernel written in Bass

```python
import numpy as np
import jax
import jax.numpy as jnp

def _softmax(x, axis=-1):
    return jax.nn.softmax(x, axis=axis)

def _gelu(x):
    return jax.nn.gelu(x, approximate=True)

def _silu(x):
    return jax.nn.silu(x)

def _sigmoid(x):
    return jax.nn.sigmoid(x)

def _layernorm(x, axis=-1, eps=1e-05):
    m = jnp.mean(x, axis=axis, keepdims=True)
    v = jnp.var(x, axis=axis, keepdims=True)
    return (x - m) / jnp.sqrt(v + eps)

def _scatter_add(tgt, idx, src, axis=0):
    return tgt.at[idx].add(src)

def _segment_sum(src, seg, n):
    return jax.ops.segment_sum(src, seg, n)
kernel_name = 'mk_cond_seq_d4_seqx_r8_96ba7b'

def setup_inputs(seed: int=0):
    np.random.seed(seed)
    _w = jnp.asarray

    def _rec_inputs():
        import jax
        import jax.numpy as jnp
        _rk = jax.random.key(seed)
        x = -0.0002928 + 1 * jax.random.normal(jax.random.fold_in(_rk, 1), (16, 128, 128), jnp.float32)
        _lenS = 128 - jax.random.randint(jax.random.fold_in(_rk, 7), (16,), 0, max(1, 128 // 4) + 1, jnp.int32)
        _lenS2 = 128 - jax.random.randint(jax.random.fold_in(_rk, 8), (16,), 0, max(1, 128 // 4) + 1, jnp.int32)
        itok_B_0_7 = jax.random.randint(jax.random.fold_in(_rk, 11), (16,), 0, 8, jnp.int32)
        itok_B_6_14 = jax.random.randint(jax.random.fold_in(_rk, 12), (16,), 6, 15, jnp.int32)
        condB_theta = jax.random.uniform(jax.random.fold_in(_rk, 13), (16,), jnp.float32, 0.0, 0.983423)
        condB_phi = jax.random.uniform(jax.random.fold_in(_rk, 14), (16,), jnp.float32, 0.0, 0.961312)
        itok_B_0_15 = jax.random.randint(jax.random.fold_in(_rk, 15), (16,), 0, 16, jnp.int32)
        return (x, itok_B_0_7, itok_B_6_14, condB_theta, condB_phi, itok_B_0_15)
    x, itok_B_0_7, itok_B_6_14, condB_theta, condB_phi, itok_B_0_15 = _rec_inputs()

    def _L0_cond_setup():
        import jax, jax.numpy as jnp
        import numpy as np
        E, H, I = (8, 128, 512)
        B, S = (4, 128)
        LN_EPS = 1e-12
        key = jax.random.key(seed)
        ks = jax.random.split(key, 8)
        x = jax.random.normal(ks[0], (B, S, H), dtype=jnp.float32)
        expert_idx = jax.random.randint(ks[1], (B,), 0, E, dtype=jnp.int64)
        Wi = jax.random.normal(ks[2], (E, H, I), dtype=jnp.float32) * 0.02
        bi = jnp.zeros((E, I), dtype=jnp.float32)
        Wo = jax.random.normal(ks[3], (E, I, H), dtype=jnp.float32) * 0.02
        bo = jnp.zeros((E, H), dtype=jnp.float32)
        gamma = jnp.ones((E, H), dtype=jnp.float32)
        beta = jnp.zeros((E, H), dtype=jnp.float32)
        return {'input_tensor': x, 'expert_idx': expert_idx, 'Wi': Wi, 'bi': bi, 'Wo': Wo, 'bo': bo, 'gamma': gamma, 'beta': beta}
    _L0_cond_all = _L0_cond_setup()
    _L0_cond_in = {k: v for k, v in _L0_cond_all.items() if k in ('Wi', 'bi', 'Wo', 'bo', 'gamma', 'beta')}
    del _L0_cond_all

    def _L1_cond_setup():
        import jax, jax.numpy as jnp
        import numpy as np
        D = 128
        E = 8
        FF = 512
        TOPK = 2
        S = 32
        SE = 64
        SH = 128
        B, T = (2, 256)

        def _forward(x, subject_ids, ln_g, ln_b, subj_emb, hyp_w1, hyp_b1, hyp_w2, hyp_b2, sty_w1, sty_b1, sty_w2, sty_b2, router_w, exp_w1, exp_b1, exp_w2, exp_b2):
            mu = x.mean(-1, keepdims=True)
            var = x.var(-1, keepdims=True)
            h = (x - mu) * jax.lax.rsqrt(var + 1e-05) * ln_g + ln_b
            m_t = h.mean(1, keepdims=True)
            v_t = h.var(1, keepdims=True)
            h_norm = (h - m_t) * jax.lax.rsqrt(v_t + 1e-08)
            se = subj_emb[subject_ids]
            hyp = jax.nn.relu(se @ hyp_w1 + hyp_b1) @ hyp_w2 + hyp_b2
            sty = jax.nn.relu(hyp @ sty_w1 + sty_b1) @ sty_w2 + sty_b2
            gamma, beta = jnp.split(sty, 2, axis=-1)
            gamma = jax.nn.softplus(gamma) + 1e-08
            h = h_norm * gamma[:, None, :] + beta[:, None, :]
            h_flat = h.reshape(-1, D)
            probs = jax.nn.softmax(h_flat @ router_w, axis=-1)
            gates, idx = jax.lax.top_k(probs, TOPK)
            gates = gates / gates.sum(-1, keepdims=True)
            N = h_flat.shape[0]
            combine = jnp.zeros((N, E), h_flat.dtype).at[jnp.arange(N)[:, None], idx].add(gates)
            hid = jax.nn.relu(jnp.einsum('nd,edf->nef', h_flat, exp_w1) + exp_b1)
            eout = jnp.einsum('nef,efd->ned', hid, exp_w2) + exp_b2
            y = jnp.einsum('ned,ne->nd', eout, combine)
            return x + y.reshape(x.shape)
        key = jax.random.key(seed)
        ks = jax.random.split(key, 16)
        n = lambda k, sh, s=0.02: jax.random.normal(k, sh, dtype=jnp.float32) * s
        return {'x': jax.random.normal(ks[0], (B, T, D), dtype=jnp.float32), 'subject_ids': jax.random.randint(ks[1], (B,), 0, S), 'ln_g': jnp.ones((D,), jnp.float32), 'ln_b': jnp.zeros((D,), jnp.float32), 'subj_emb': n(ks[2], (S, SE)), 'hyp_w1': n(ks[3], (SE, SH), 1.0 / np.sqrt(SE)), 'hyp_b1': jnp.zeros((SH,), jnp.float32), 'hyp_w2': n(ks[4], (SH, SH), 1.0 / np.sqrt(SH)), 'hyp_b2': jnp.zeros((SH,), jnp.float32), 'sty_w1': n(ks[5], (SH, SH // 2), 1.0 / np.sqrt(SH)), 'sty_b1': jnp.zeros((SH // 2,), jnp.float32), 'sty_w2': n(ks[6], (SH // 2, 2 * D), 1.0 / np.sqrt(SH // 2)), 'sty_b2': jnp.zeros((2 * D,), jnp.float32), 'router_w': n(ks[7], (D, E), 1.0 / np.sqrt(D)), 'exp_w1': n(ks[8], (E, D, FF), 1.0 / np.sqrt(D)), 'exp_b1': jnp.zeros((E, FF), jnp.float32), 'exp_w2': n(ks[9], (E, FF, D), 1.0 / np.sqrt(FF)), 'exp_b2': jnp.zeros((E, D), jnp.float32)}
    _L1_cond_all = _L1_cond_setup()
    _L1_cond_in = {k: v for k, v in _L1_cond_all.items() if k in ('ln_g', 'ln_b', 'subj_emb', 'hyp_w1', 'hyp_b1', 'hyp_w2', 'hyp_b2', 'sty_w1', 'sty_b1', 'sty_w2', 'sty_b2', 'router_w', 'exp_w1', 'exp_b1', 'exp_w2', 'exp_b2')}
    del _L1_cond_all

    def _L2_cond_setup():
        import jax, jax.numpy as jnp
        import numpy as np
        key = jax.random.key(seed)
        k1, k2, k3 = jax.random.split(key, 3)
        B, N, D = (16, 512, 128)
        embeddings = jax.random.normal(k1, (B, N, D), dtype=jnp.float32)
        theta = jax.random.uniform(k2, (B,), dtype=jnp.float32)
        phi = jax.random.uniform(k3, (B,), dtype=jnp.float32)
        return {'embeddings': embeddings, 'theta': theta, 'phi': phi}
    _L2_cond_all = _L2_cond_setup()
    _L2_cond_in = {k: v for k, v in _L2_cond_all.items() if k in ()}
    del _L2_cond_all

    def _L3_cond_setup():
        import jax, jax.numpy as jnp
        import numpy as np
        B, S, D = (32, 128, 128)
        A = 32
        E = 16
        LN_EPS = 1e-05
        key = jax.random.key(seed)
        ks = jax.random.split(key, 10)
        s = lambda fan_in: 1.0 / np.sqrt(fan_in)
        return {'hidden_states': jax.random.normal(ks[0], (B, S, D), dtype=jnp.float32), 'domain_id': jax.random.randint(ks[1], (B,), 0, E, dtype=jnp.int64), 'down_W': jax.random.uniform(ks[2], (A, D), jnp.float32, -s(D), s(D)), 'down_b': jax.random.uniform(ks[3], (A,), jnp.float32, -s(D), s(D)), 'up_W': jax.random.uniform(ks[4], (D, A), jnp.float32, -s(A), s(A)), 'up_b': jax.random.uniform(ks[5], (D,), jnp.float32, -s(A), s(A)), 'expert_W': jax.random.uniform(ks[6], (E, A, A), jnp.float32, -s(A), s(A)), 'expert_b': jax.random.uniform(ks[7], (E, A), jnp.float32, -s(A), s(A)), 'domain_emb': jax.random.normal(ks[8], (E, A), dtype=jnp.float32), 'ln_gamma': jnp.ones((D,), jnp.float32), 'ln_beta': jnp.zeros((D,), jnp.float32)}
    _L3_cond_all = _L3_cond_setup()
    _L3_cond_in = {k: v for k, v in _L3_cond_all.items() if k in ('down_W', 'down_b', 'up_W', 'up_b', 'expert_W', 'expert_b', 'domain_emb', 'ln_gamma', 'ln_beta')}
    del _L3_cond_all
    return {'x': x, 'itok_B_0_7': itok_B_0_7, 'itok_B_6_14': itok_B_6_14, 'condB_theta': condB_theta, 'condB_phi': condB_phi, 'itok_B_0_15': itok_B_0_15, 'L0_cond_Wi': _L0_cond_in['Wi'], 'L0_cond_bi': _L0_cond_in['bi'], 'L0_cond_Wo': _L0_cond_in['Wo'], 'L0_cond_bo': _L0_cond_in['bo'], 'L0_cond_gamma': _L0_cond_in['gamma'], 'L0_cond_beta': _L0_cond_in['beta'], 'L1_cond_ln_g': _L1_cond_in['ln_g'], 'L1_cond_ln_b': _L1_cond_in['ln_b'], 'L1_cond_subj_emb': _L1_cond_in['subj_emb'], 'L1_cond_hyp_w1': _L1_cond_in['hyp_w1'], 'L1_cond_hyp_b1': _L1_cond_in['hyp_b1'], 'L1_cond_hyp_w2': _L1_cond_in['hyp_w2'], 'L1_cond_hyp_b2': _L1_cond_in['hyp_b2'], 'L1_cond_sty_w1': _L1_cond_in['sty_w1'], 'L1_cond_sty_b1': _L1_cond_in['sty_b1'], 'L1_cond_sty_w2': _L1_cond_in['sty_w2'], 'L1_cond_sty_b2': _L1_cond_in['sty_b2'], 'L1_cond_router_w': _L1_cond_in['router_w'], 'L1_cond_exp_w1': _L1_cond_in['exp_w1'], 'L1_cond_exp_b1': _L1_cond_in['exp_b1'], 'L1_cond_exp_w2': _L1_cond_in['exp_w2'], 'L1_cond_exp_b2': _L1_cond_in['exp_b2'], 'L3_cond_down_W': _L3_cond_in['down_W'], 'L3_cond_down_b': _L3_cond_in['down_b'], 'L3_cond_up_W': _L3_cond_in['up_W'], 'L3_cond_up_b': _L3_cond_in['up_b'], 'L3_cond_expert_W': _L3_cond_in['expert_W'], 'L3_cond_expert_b': _L3_cond_in['expert_b'], 'L3_cond_domain_emb': _L3_cond_in['domain_emb'], 'L3_cond_ln_gamma': _L3_cond_in['ln_gamma'], 'L3_cond_ln_beta': _L3_cond_in['ln_beta']}

def reference(x, itok_B_0_7, itok_B_6_14, condB_theta, condB_phi, itok_B_0_15, L0_cond_Wi, L0_cond_bi, L0_cond_Wo, L0_cond_bo, L0_cond_gamma, L0_cond_beta, L1_cond_ln_g, L1_cond_ln_b, L1_cond_subj_emb, L1_cond_hyp_w1, L1_cond_hyp_b1, L1_cond_hyp_w2, L1_cond_hyp_b2, L1_cond_sty_w1, L1_cond_sty_b1, L1_cond_sty_w2, L1_cond_sty_b2, L1_cond_router_w, L1_cond_exp_w1, L1_cond_exp_b1, L1_cond_exp_w2, L1_cond_exp_b2, L3_cond_down_W, L3_cond_down_b, L3_cond_up_W, L3_cond_up_b, L3_cond_expert_W, L3_cond_expert_b, L3_cond_domain_emb, L3_cond_ln_gamma, L3_cond_ln_beta):
    import jax
    import jax.numpy as jnp

    def _L0_cond_ref(input_tensor, expert_idx, Wi, bi, Wo, bo, gamma, beta):
        import jax, jax.numpy as jnp
        import numpy as np
        E, H, I = (8, 128, 512)
        B, S = (4, 128)
        LN_EPS = 1e-12
        Wi_b = Wi[expert_idx]
        bi_b = bi[expert_idx]
        Wo_b = Wo[expert_idx]
        bo_b = bo[expert_idx]
        g_b = gamma[expert_idx]
        be_b = beta[expert_idx]
        h = jax.nn.gelu(jnp.einsum('bsh,bhi->bsi', input_tensor, Wi_b) + bi_b[:, None, :], approximate=False)
        o = jnp.einsum('bsi,bih->bsh', h, Wo_b) + bo_b[:, None, :]
        r = o + input_tensor
        mu = jnp.mean(r, axis=-1, keepdims=True)
        var = jnp.mean(jnp.square(r - mu), axis=-1, keepdims=True)
        y = (r - mu) * jax.lax.rsqrt(var + LN_EPS)
        return y * g_b[:, None, :] + be_b[:, None, :]

    def _L1_cond_ref(x, subject_ids, ln_g, ln_b, subj_emb, hyp_w1, hyp_b1, hyp_w2, hyp_b2, sty_w1, sty_b1, sty_w2, sty_b2, router_w, exp_w1, exp_b1, exp_w2, exp_b2):
        import jax, jax.numpy as jnp
        import numpy as np
        D = 128
        E = 8
        FF = 512
        TOPK = 2
        S = 32
        SE = 64
        SH = 128
        B, T = (2, 256)

        def _forward(x, subject_ids, ln_g, ln_b, subj_emb, hyp_w1, hyp_b1, hyp_w2, hyp_b2, sty_w1, sty_b1, sty_w2, sty_b2, router_w, exp_w1, exp_b1, exp_w2, exp_b2):
            mu = x.mean(-1, keepdims=True)
            var = x.var(-1, keepdims=True)
            h = (x - mu) * jax.lax.rsqrt(var + 1e-05) * ln_g + ln_b
            m_t = h.mean(1, keepdims=True)
            v_t = h.var(1, keepdims=True)
            h_norm = (h - m_t) * jax.lax.rsqrt(v_t + 1e-08)
            se = subj_emb[subject_ids]
            hyp = jax.nn.relu(se @ hyp_w1 + hyp_b1) @ hyp_w2 + hyp_b2
            sty = jax.nn.relu(hyp @ sty_w1 + sty_b1) @ sty_w2 + sty_b2
            gamma, beta = jnp.split(sty, 2, axis=-1)
            gamma = jax.nn.softplus(gamma) + 1e-08
            h = h_norm * gamma[:, None, :] + beta[:, None, :]
            h_flat = h.reshape(-1, D)
            probs = jax.nn.softmax(h_flat @ router_w, axis=-1)
            gates, idx = jax.lax.top_k(probs, TOPK)
            gates = gates / gates.sum(-1, keepdims=True)
            N = h_flat.shape[0]
            combine = jnp.zeros((N, E), h_flat.dtype).at[jnp.arange(N)[:, None], idx].add(gates)
            hid = jax.nn.relu(jnp.einsum('nd,edf->nef', h_flat, exp_w1) + exp_b1)
            eout = jnp.einsum('nef,efd->ned', hid, exp_w2) + exp_b2
            y = jnp.einsum('ned,ne->nd', eout, combine)
            return x + y.reshape(x.shape)
        return _forward(x, subject_ids, ln_g, ln_b, subj_emb, hyp_w1, hyp_b1, hyp_w2, hyp_b2, sty_w1, sty_b1, sty_w2, sty_b2, router_w, exp_w1, exp_b1, exp_w2, exp_b2)

    def _L2_cond_ref(embeddings, theta, phi):
        import jax, jax.numpy as jnp
        import numpy as np
        B, N, D = embeddings.shape
        e = embeddings.reshape(B, N, D // 4, 4)
        ct = jnp.cos(theta)[:, None, None]
        st = jnp.sin(theta)[:, None, None]
        cp = jnp.cos(phi)[:, None, None]
        sp = jnp.sin(phi)[:, None, None]
        x0, x1, x2, x3 = (e[..., 0], e[..., 1], e[..., 2], e[..., 3])
        out = jnp.stack([x0 * ct + x1 * st, -x0 * st + x1 * ct, x2 * cp + x3 * sp, -x2 * sp + x3 * cp], axis=-1)
        return out.reshape(B, N, D)

    def _L3_cond_ref(hidden_states, domain_id, down_W, down_b, up_W, up_b, expert_W, expert_b, domain_emb, ln_gamma, ln_beta):
        import jax, jax.numpy as jnp
        import numpy as np
        B, S, D = (32, 128, 128)
        A = 32
        E = 16
        LN_EPS = 1e-05
        residual = hidden_states
        hidden = jnp.einsum('bsd,ad->bsa', hidden_states, down_W) + down_b
        hidden = jax.nn.gelu(hidden, approximate=False)
        valid = (domain_id >= 0) & (domain_id < E)
        idx = jnp.clip(domain_id, 0, E - 1)
        Wsel = expert_W[idx]
        bsel = expert_b[idx]
        expert_out = jnp.einsum('bsa,boa->bso', hidden, Wsel) + bsel[:, None, :]
        domain_output = jnp.where(valid[:, None, None], expert_out, hidden)
        hidden = domain_output + domain_emb[idx][:, None, :]
        hidden = jnp.einsum('bsa,da->bsd', hidden, up_W) + up_b
        x = hidden + residual
        mu = jnp.mean(x, axis=-1, keepdims=True)
        var = jnp.mean(jnp.square(x - mu), axis=-1, keepdims=True)
        return (x - mu) * jax.lax.rsqrt(var + LN_EPS) * ln_gamma + ln_beta
    x = _L0_cond_ref(x, itok_B_0_7, L0_cond_Wi, L0_cond_bi, L0_cond_Wo, L0_cond_bo, L0_cond_gamma, L0_cond_beta)
    x = _L1_cond_ref(x, itok_B_6_14, L1_cond_ln_g, L1_cond_ln_b, L1_cond_subj_emb, L1_cond_hyp_w1, L1_cond_hyp_b1, L1_cond_hyp_w2, L1_cond_hyp_b2, L1_cond_sty_w1, L1_cond_sty_b1, L1_cond_sty_w2, L1_cond_sty_b2, L1_cond_router_w, L1_cond_exp_w1, L1_cond_exp_b1, L1_cond_exp_w2, L1_cond_exp_b2)
    x = _L2_cond_ref(x, condB_theta, condB_phi)
    x = _L3_cond_ref(x, itok_B_0_15, L3_cond_down_W, L3_cond_down_b, L3_cond_up_W, L3_cond_up_b, L3_cond_expert_W, L3_cond_expert_b, L3_cond_domain_emb, L3_cond_ln_gamma, L3_cond_ln_beta)
    return x

_drawn_inputs = setup_inputs


def setup_inputs(seed=0):
    import zlib

    import numpy as np

    out = dict(_drawn_inputs(seed))
    spreads = {'L0_cond_bi': (0.0, 0.274),
     'L0_cond_bo': (0.0, 0.1),
     'L0_cond_gamma': (1.0, 0.2),
     'L0_cond_beta': (0.0, 0.1),
     'L1_cond_ln_g': (1.0, 0.6),
     'L1_cond_ln_b': (0.0, 0.8),
     'L1_cond_hyp_b1': (0.0, 0.1),
     'L1_cond_hyp_b2': (0.0, 0.1),
     'L1_cond_sty_b1': (0.0, 0.1),
     'L1_cond_sty_b2': (0.0, 0.1),
     'L1_cond_exp_b1': (0.0, 0.1),
     'L1_cond_exp_b2': (0.0, 0.1),
     'L3_cond_ln_gamma': (1.0, 0.2),
     'L3_cond_ln_beta': (0.0, 0.1)}
    factors = {'L3_cond_down_b': 6.262}
    for name, (base, spread) in spreads.items():
        noise = np.random.default_rng([zlib.crc32(name.encode()), seed]).standard_normal(out[name].shape)
        drawn = base * np.exp(spread * noise) if base else spread * noise
        out[name] = jnp.asarray(drawn.astype(out[name].dtype))
    for name, factor in factors.items():
        out[name] = (out[name] * factor).astype(out[name].dtype)
    return out
```

```python
from contextlib import ExitStack

import concourse.bass as bass
from concourse import mybir

F32 = mybir.dt.float32
BF16 = mybir.dt.bfloat16
I32 = mybir.dt.int32
U32 = mybir.dt.uint32
ALU = mybir.AluOpType
ACT = mybir.ActivationFunctionType
AX = mybir.AxisListType

P = 128
ROUND = 12582912.0
TWO_PI_HI = 6.28125
TWO_PI_LO = 0.0019353071795864769
PI = 3.1415925
FAR = 1.0e6


def conditional_layers_kernel(nc, x, id_l0, id_l1, theta, phi, id_l3,
                              l0_wi, l0_bi, l0_wo, l0_bo, l0_gamma, l0_beta,
                              ln_g, ln_b, subj_emb, hyp_w1, hyp_b1, hyp_w2, hyp_b2,
                              sty_w1, sty_b1, sty_w2, sty_b2, router_w,
                              exp_w1, exp_b1, exp_w2, exp_b2,
                              down_w, down_b, up_w, up_b, l3_w, l3_b, l3_emb, l3_gamma, l3_beta,
                              out):
    NB, S, D = x.shape
    E0, _, FF = l0_wi.shape
    E1 = exp_w1.shape[0]
    NS, SE = subj_emb.shape
    SH = hyp_w1.shape[1]
    SM = sty_w1.shape[1]
    E3, A, _ = l3_w.shape
    FC = FF // P
    GS = 4
    NG = NB // GS
    GW = GS * D
    TOPK = 2
    NROW = NB * S
    BLOCKS = (TOPK * NROW + E1 * (P - 1)) // P
    KT = TOPK * NB
    assert S == P and D == P and GW == 512 and FC * P == 512

    h_dram = nc.dram_tensor("h_rows", (NROW, D), F32, kind="Internal").ap()
    y_dram = nc.dram_tensor("expert_rows", (TOPK * NROW, D), F32, kind="Internal").ap()

    with ExitStack() as ctx:
        def sb(name, shape, dt=F32):
            return ctx.enter_context(nc.sbuf_tensor(name, shape, dt))

        def sem(name):
            return ctx.enter_context(nc.semaphore(name))

        bank = [ctx.enter_context(nc.psum_tensor(f"bank{i}", [P, 512], F32)) for i in range(8)]

        ident = sb("ident", [P, P])
        upper = sb("upper", [P, P], BF16)
        ones_bf = sb("ones_bf", [P, P], BF16)
        ones_row = sb("ones_row", [1, NB])
        minus_half = sb("minus_half", [P, 16])
        col_i = sb("col_i", [P, P], I32)
        col_f = sb("col_f", [P, P])
        col_bf = sb("col_bf", [P, P], BF16)
        part_i = sb("part_i", [P, 1], I32)
        part_f = sb("part_f", [P, 1])
        scan_mask = sb("scan_mask", [P, E1, NB])

        ids = sb("ids", [NS, 3, NB], I32)
        ids_f = sb("ids_f", [NS, 3, NB])
        id3_clip = sb("id3_clip", [NS, NB])
        id3_clip_i = sb("id3_clip_i", [1, NB], I32)
        valid = sb("valid", [NS, NB])
        invalid = sb("invalid", [NS, NB])
        pick_subj = sb("pick_subj", [NS, NB])
        pick_l3 = sb("pick_l3", [E3, NB])
        pick_l3_valid = sb("pick_l3_valid", [E3, NB])
        R_BI, R_B1, R_H1, R_H2, R_S1, R_S2, R_LG, R_LB, R_DB = (
            0, E0 * FC, E0 * FC + E1 * FC, E0 * FC + E1 * FC + 1, E0 * FC + E1 * FC + 2,
            E0 * FC + E1 * FC + 3, E0 * FC + E1 * FC + 5, E0 * FC + E1 * FC + 6, E0 * FC + E1 * FC + 7)
        NR = R_DB + 1
        rows = sb("rows", [NR, P])
        cols = sb("cols", [P, NR])
        angle = sb("angle", [P, 2, NB])
        arg = sb("arg", [P, 4, NB])
        turns = sb("turns", [P, 4, NB])
        trig = sb("trig", [P, 4, NB])
        rot_same = sb("rot_same", [P, NB, 4])
        rot_swap = sb("rot_swap", [P, NB, 4])
        emb_sb = sb("emb_sb", [NS, SE])
        hw1 = sb("hw1", [SE, SH])
        hw2 = sb("hw2", [SH, SH])
        sw1 = sb("sw1", [SH, SM])
        sw2 = sb("sw2", [SM, 2 * D])
        hyp_a = sb("hyp_a", [SE, NB])
        hyp_b = sb("hyp_b", [SH, NB])
        hyp_c = sb("hyp_c", [SH, NB])
        hyp_d = sb("hyp_d", [SM, NB])
        g_pre = sb("g_pre", [P, NB])
        g_abs = sb("g_abs", [P, NB])
        g_exp = sb("g_exp", [P, NB])
        g_ln = sb("g_ln", [P, NB])
        g_pos = sb("g_pos", [P, NB])
        film_g = sb("film_g", [P, NB])
        film_b = sb("film_b", [P, NB])
        g_sq = sb("g_sq", [P, 1])
        rw = sb("rw", [P, E1])

        x_sb = sb("x_sb", [P, NB, D])
        xT = sb("xT", [P, 2, GW])
        w0_place = sb("w0_place", [P, 2, 4 * FF])
        wi = w0_place[:, 0].rearrange("p (s f) -> p s f", s=4)
        wo = w0_place[:, 1].rearrange("p (s c d) -> p s c d", s=4, c=FC)
        tab0 = sb("tab0", [P, 3, E0, D])
        act0 = sb("act0", [P, 2, FC, P])
        x_bo = sb("x_bo", [P, 2, GS, D])
        r0 = sb("r0", [P, 2, GS, D])
        z0 = sb("z0", [P, 2, GS, D])
        zg = sb("zg", [P, 2, GS, D])
        x1 = sb("x1", [P, NB, D])
        st = sb("st", [P, 4, GS, 6])
        mv = sb("mv", [P, 3, GS, 2])
        veps = sb("veps", [P, 3, GS])
        rstd = sb("rstd", [P, 3, GS])

        z1 = sb("z1", [P, 2, GS, D])
        film = sb("film", [P, 6, GS])
        hT = sb("hT", [P, 2, GW])
        h_row = sb("h_row", [P, 2, GS, D])
        top_v = sb("top_v", [P, NB, 8])
        top_i = sb("top_i", [P, GS, 8], U32)
        top_if = sb("top_if", [P, GS, 2])
        pick = sb("pick", [P, TOPK, E1, NB], BF16)
        both = sb("both", [P, E1, NB], BF16)
        logit_sb = sb("logit_sb", [P, GS, E1])
        tot = sb("tot", [P, E1, NB])
        run = sb("run", [P, E1, NB])
        pos = sb("pos", [P, E1, NB])
        blk = sb("blk", [P, E1])
        blk_end = sb("blk_end", [P, E1])
        blk_start = sb("blk_start", [P, E1])
        slot_e = sb("slot_e", [P, TOPK, E1, NB])
        slot = sb("slot", [P, KT])
        blk_of = sb("blk_of", [P, KT])
        in_blk = sb("in_blk", [P, KT])
        hot_in = sb("hot_in", [P, KT, P], BF16)
        hot_blk = sb("hot_blk", [P, KT, 2, BLOCKS], BF16)
        hot_tmp = sb("hot_tmp", [P, KT, BLOCKS], BF16)
        blk_of_bf = sb("blk_of_bf", [P, KT], BF16)
        dest = sb("dest", [P, BLOCKS])
        wrap = sb("wrap", [P, BLOCKS])
        src_f = sb("src_f", [P, BLOCKS])
        src_i = sb("src_i", [P, BLOCKS], I32)
        dest_i = sb("dest_i", [P, BLOCKS], I32)
        exp_cmp = sb("exp_cmp", [1, BLOCKS, E1])
        exp_f = sb("exp_f", [1, BLOCKS])
        exp_i = sb("exp_i", [1, BLOCKS], I32)
        soft = sb("soft", [P, NB, 8])
        soft_in = sb("soft_in", [P, NB, 8])
        soft_s = sb("soft_s", [P, 4, NB])
        gates = sb("gates", [P, TOPK, NB])
        w1 = sb("w1", [P, E1, FF])
        w2 = sb("w2", [P, E1, FC, D])
        b2_tab = sb("b2_tab", [P, E1, D])
        got = sb("got", [P, 4, D])
        gotT = sb("gotT", [P, 2, P])
        up_sb = sb("up_sb", [P, 2, FF])
        hid = sb("hid", [P, 2, FC, P])
        y_blk = sb("y_blk", [P, 4, D])

        dw = sb("dw", [A, D])
        dwT = sb("dwT", [P, A])
        uw = sb("uw", [P, A])
        uwT = sb("uwT", [A, D])
        ub = sb("ub", [1, D])
        w3 = sb("w3", [A, NB, A])
        w3v = sb("w3v", [A, NB, A])
        eye3 = sb("eye3", [A, NB, A])
        b3 = sb("b3", [E3, A])
        e3 = sb("e3", [E3, A])
        c3 = sb("c3", [A, NB])
        bias3 = sb("bias3", [NB, D])
        m3 = sb("m3", [A + 1, NB, D])
        g3 = sb("g3", [P, D])
        be3 = sb("be3", [P, D])
        assert NG * TOPK * GS * D == 2 * 4 * FF
        y_in = w0_place[:].rearrange("p a f -> p (a f)").rearrange("p (g k t d) -> p g k t d", g=NG, k=TOPK, t=GS)
        u_a, u_b, t_same, t_swap = x_bo, z0, zg, r0
        xr = sb("xr", [P, 2, GS, D])
        xrT = xT
        a3 = sb("a3", [A + 1, 2, GW])
        r3 = sb("r3", [P, 2, GS, D])
        z3 = sb("z3", [P, 2, GS, D])
        zg3 = sb("zg3", [P, 2, GS, D])
        o3 = sb("o3", [P, 2, GS, D])
        st3 = sb("st3", [P, GS, 6])
        mv3 = sb("mv3", [P, 2, GS, 2])
        ve3 = sb("ve3", [P, 2, GS])
        rs3 = sb("rs3", [P, 2, GS])

        l_ids = sem("l_ids")
        l_x = [sem(f"l_x{g}") for g in range(NG)]
        l_w0 = [sem(f"l_w0_{s}") for s in range(4)]
        l_tab0 = sem("l_tab0")
        l_rows = sem("l_rows")
        l_small = sem("l_small")
        l_ang = sem("l_ang")
        l_w1 = sem("l_w1")
        l_w3 = sem("l_w3")
        l_m3 = sem("l_m3")
        l_y = [sem(f"l_y{g}") for g in range(NG)]
        k_pool = sem("k_pool")
        k_dve = sem("k_dve")
        v_ids = sem("v_ids")
        p_pro = sem("p_pro")
        v_pro = sem("v_pro")
        v_soft_in = sem("v_soft_in")
        a_soft = sem("a_soft")
        v_arg = sem("v_arg")
        a_trig = sem("a_trig")
        v_rot = sem("v_rot")
        vc = sem("vc")
        gc = sem("gc")
        ac = sem("ac")
        p_xT = sem("p_xT")
        v_xT = sem("v_xT")
        p_up = sem("p_up")
        a_gelu = sem("a_gelu")
        p_down = sem("p_down")
        g_xbo = sem("g_xbo")
        v_r0 = sem("v_r0")
        v_var = sem("v_var")
        g_rstd = sem("g_rstd")
        v_z0 = sem("v_z0")
        g_x1 = sem("g_x1")
        v_z1 = sem("v_z1")
        p_zT = sem("p_zT")
        v_hT = sem("v_hT")
        p_rt = sem("p_rt")
        v_top = sem("v_top")
        a_hrow = sem("a_hrow")
        st_h = [sem(f"st_h{i}") for i in range(2)]
        p_rank = sem("p_rank")
        v_hot = sem("v_hot")
        p_inv = sem("p_inv")
        v_idx = sem("v_idx")
        v_exp = sem("v_exp")
        v_w3 = sem("v_w3")
        p_m3 = sem("p_m3")
        a_m3 = sem("a_m3")
        v_smax = sem("v_smax")
        a_sexp = sem("a_sexp")
        v_gate = sem("v_gate")
        gat = [sem(f"gat{i}") for i in range(4)]
        sca = [sem(f"sca{i}") for i in range(4)]
        p_gT = sem("p_gT")
        v_gT = sem("v_gT")
        p_u = sem("p_u")
        v_u = sem("v_u")
        p_t = sem("p_t")
        a_hid = sem("a_hid")
        p_y = sem("p_y")
        v_y = sem("v_y")
        v_u3 = sem("v_u3")
        g_swap = sem("g_swap")
        v_xr = sem("v_xr")
        p_xrT = sem("p_xrT")
        a_xrT = sem("a_xrT")
        p_dn3 = sem("p_dn3")
        a_gelu3 = sem("a_gelu3")
        p_up3 = sem("p_up3")
        v_r3 = sem("v_r3")
        v_var3 = sem("v_var3")
        g_rstd3 = sem("g_rstd3")
        v_zg3 = sem("v_zg3")
        g_o3 = sem("g_o3")
        s_out = [sem(f"s_out{i}") for i in range(2)]

        class Chain:

            def __init__(self, eng, s):
                self.eng, self.s, self.n = eng, s, 0

            def do(self, ins):
                self.n += 1
                return ins.then_inc(self.s, 1)

            def settle(self):
                self.eng.wait_ge(self.s, self.n)

        block = ctx.enter_context(nc.Block())

        row = lambda ap: ap.rearrange("(o n) -> o n", o=1)
        pro = bank[7]
        c0 = NR
        q_se, q_h1, q_h2, q_s1, q_ga, q_be = (pro[:, c0 + NB * i:c0 + NB * (i + 1)] for i in range(6))
        q_dwT = bank[5][:, 0:A]
        q_c3 = bank[5][:, A:A + NB]
        q_uwT = bank[5][:, A + NB:A + NB + D]
        q_bias3 = bank[0][0:NB, 0:D]

        @block.sync
        def _(sp):
            sp.dma_start(ids[:, 0, :], row(id_l0).to_broadcast([NS, NB])).then_inc(l_ids, 16)
            sp.dma_start(ids[:, 1, :], row(id_l1).to_broadcast([NS, NB])).then_inc(l_ids, 16)
            sp.dma_start(ids[:, 2, :], row(id_l3).to_broadcast([NS, NB])).then_inc(l_ids, 16)

            def load_x(g):
                sp.dma_start(x_sb[:, GS * g:GS * (g + 1), :],
                             x[GS * g:GS * (g + 1)].rearrange("b s d -> s b d")).then_inc(l_x[g], 16)

            load_x(0)
            sp.wait_ge(l_ids, 48)
            for b in range(NB):
                e = sp.value_load(ids[0:1, 0, b:b + 1], min_val=0, max_val=E0 - 1)
                if b >= 4:
                    sp.wait_ge(p_down, b - 3)
                sp.dma_start(wi[:, b % 4, :], l0_wi[bass.ds(e, 1)].rearrange("o h i -> h (o i)"))\
                    .then_inc(l_w0[b % 4], 16)
                sp.dma_start(wo[:, b % 4, :, :], l0_wo[bass.ds(e, 1)].rearrange("o (c p) h -> p (o c) h", p=P))\
                    .then_inc(l_w0[b % 4], 16)
                if b < NG - 1:
                    load_x(b + 1)
                if b == 0:
                    for i, t in enumerate((l0_bo, l0_gamma, l0_beta)):
                        sp.dma_start(tab0[:, i], t.rearrange("(o e) d -> o e d", o=1).to_broadcast([P, E0, D]))\
                            .then_inc(l_tab0, 16)
                if b >= NB - E1:
                    i = b - (NB - E1)
                    sp.dma_start(w1[:, i, :], exp_w1[i]).then_inc(l_w1, 16)
                    sp.dma_start(w2[:, i], exp_w2[i].rearrange("(c p) d -> p c d", p=P)).then_inc(l_w1, 16)
            sp.dma_start(b2_tab[:], exp_b2.rearrange("(o e) d -> o e d", o=1).to_broadcast([P, E1, D]))\
                .then_inc(l_w1, 16)
            sp.wait_ge(v_ids, 1)
            for b in range(NB):
                e = sp.value_load(id3_clip_i[0:1, b:b + 1], min_val=0, max_val=E3 - 1)
                sp.dma_start(w3[:, b, :], l3_w[bass.ds(e, 1)].rearrange("o p a -> p (o a)")).then_inc(l_w3, 16)
            sp.wait_ge(v_pro, 10)
            sp.dma_start(m3[A:A + 1, :, :], bias3[:]).then_inc(l_m3, 16)
            for i in range(4):
                sp.wait_ge(sca[i], 16 * len(range(i, BLOCKS, 4)))
            y_v = y_dram.rearrange("(k t p) d -> p k t d", k=TOPK, p=P)
            for g in range(NG):
                for k in range(TOPK):
                    sp.dma_start(y_in[:, g, k], y_v[:, k, GS * g:GS * (g + 1), :]).then_inc(l_y[g], 16)
            for g in range(NG):
                sp.wait_ge(g_o3, g + 1)
                sp.dma_start(out[GS * g:GS * (g + 1)].rearrange("b s d -> s b d"), o3[:, g % 2])\
                    .then_inc(s_out[g % 2], 16)
            for i in range(2):
                sp.wait_ge(s_out[i], 16 * NG // 2)

        @block.gpsimd
        def _(pool):
            g_ = nc.gpsimd
            ch = Chain(pool, gc)
            g_.memset(rows[:], 0.0).then_inc(k_pool, 1)
            g_.memset(ident[:], 0.0).then_inc(k_pool, 1)
            g_.iota(col_i[:], [[1, P]], base=0, channel_multiplier=0).then_inc(k_pool, 1)
            g_.iota(part_i[:], [[0, 1]], base=0, channel_multiplier=1).then_inc(k_pool, 1)
            pool.wait_ge(k_pool, 4)
            g_.affine_select(out=ident[:], in_=ident[:], compare_op=ALU.not_equal, fill=1.0, base=0,
                             pattern=[[-1, P]], channel_multiplier=1).then_inc(k_pool, 1)
            g_.memset(minus_half[:], -0.5).then_inc(k_pool, 1)
            g_.memset(ones_bf[:], 1.0).then_inc(k_pool, 1)
            g_.memset(ones_row[:], 1.0).then_inc(k_pool, 1)
            g_.memset(scan_mask[:], 1.0).then_inc(k_pool, 1)
            g_.memset(a3[:], 1.0).then_inc(k_pool, 1)
            pool.wait_ge(k_pool, 10)
            g_.affine_select(out=upper[:], in_=ones_bf[:], compare_op=ALU.is_gt, fill=0.0, base=0,
                             pattern=[[1, P]], channel_multiplier=-1).then_inc(k_pool, 1)
            g_.memset(scan_mask[:, :, 0:1], 0.0).then_inc(k_pool, 1)
            g_.memset(eye3[:], 0.0).then_inc(k_pool, 1)
            pool.wait_ge(k_pool, 13)
            g_.affine_select(out=eye3[:], in_=eye3[:], compare_op=ALU.not_equal, fill=1.0, base=0,
                             pattern=[[0, NB], [-1, A]], channel_multiplier=1).then_inc(k_pool, 1)

            pool.wait_ge(l_ids, 48)
            pool.wait_ge(l_tab0, 48)

            def expert_row(b):
                return pool.value_load(ids[0:1, 0, b:b + 1], min_val=0, max_val=E0 - 1)

            def add_bo(g):
                pool.wait_ge(l_x[g], 16)
                if g >= 2:
                    pool.wait_ge(v_r0, g - 1)
                for k in range(GS):
                    b = GS * g + k
                    e = expert_row(b)
                    last = g_.tensor_tensor(x_bo[:, g % 2, k, :], x_sb[:, b, :],
                                            tab0[:, 0, bass.ds(e, 1), :].rearrange("p o d -> p (o d)"), ALU.add)
                    last.then_inc(g_xbo, 1)

            turn = [0]

            def power(kind):
                turn[0] += 1
                pool.wait_ge(v_var, turn[0])
                g_.tensor_tensor(rstd[:, kind, :], veps[:, kind, :], minus_half[:, 0:GS], ALU.pow)\
                    .then_inc(g_rstd, 1)

            def scale_shift(g):
                for k in range(GS):
                    b = GS * g + k
                    e = expert_row(b)
                    pool.wait_ge(v_z0, b + 1)
                    ch.do(g_.tensor_tensor(zg[:, g % 2, k, :], z0[:, g % 2, k, :],
                                           tab0[:, 1, bass.ds(e, 1), :].rearrange("p o d -> p (o d)"), ALU.mult))
                    ch.settle()
                    g_.tensor_tensor(x1[:, b, :], zg[:, g % 2, k, :],
                                     tab0[:, 2, bass.ds(e, 1), :].rearrange("p o d -> p (o d)"), ALU.add)\
                        .then_inc(g_x1, 1)

            add_bo(0)
            for g in range(NG):
                if g >= 1:
                    power(2)
                power(0)
                if g + 1 < NG:
                    add_bo(g + 1)
                scale_shift(g)
                power(1)
            power(2)

            pool.wait_ge(v_idx, 1)
            for i in range(2):
                pool.wait_ge(st_h[i], 16 * NG // 2)

            def gather(n):
                if n >= 4:
                    pool.wait_ge(p_gT, n - 3)
                g_.indirect_dma_start(got[:, n % 4, :], None, h_dram,
                                      bass.IndirectOffsetOnAxis(ap=src_i[:, n:n + 1], axis=0))\
                    .then_inc(gat[n % 4], 16)

            def scatter(n):
                pool.wait_ge(v_y, n + 1)
                g_.indirect_dma_start(y_dram, bass.IndirectOffsetOnAxis(ap=dest_i[:, n:n + 1], axis=0),
                                      y_blk[:, n % 4, :], None,
                                      bounds_check=TOPK * NROW - 1, oob_is_err=False)\
                    .then_inc(sca[n % 4], 16)

            for n in range(3):
                gather(n)
            for n in range(BLOCKS):
                if n + 3 < BLOCKS:
                    gather(n + 3)
                if n >= 2:
                    scatter(n - 2)
            scatter(BLOCKS - 2)
            scatter(BLOCKS - 1)

            pool.wait_ge(v_rot, 1)

            def swap(g):
                for k in range(GS):
                    b = GS * g + k
                    pool.wait_ge(v_u3, b + 1)
                    if g >= 2:
                        pool.wait_ge(v_xr, g - 1)
                    g_.tensor_tensor(t_swap[:, g % 2, k, :].rearrange("p (q j) -> p q j", j=4),
                                     u_b[:, g % 2, k, :].rearrange("p (q j) -> p q j", j=4),
                                     rot_swap[:, b:b + 1, :].to_broadcast([P, D // 4, 4]), ALU.mult)\
                        .then_inc(g_swap, 1)

            def norm3(g):
                pool.wait_ge(v_var3, g + 1)
                g_.tensor_tensor(rs3[:, g % 2, :], ve3[:, g % 2, :], minus_half[:, 0:GS], ALU.pow)\
                    .then_inc(g_rstd3, 1)

            def shift3(g):
                pool.wait_ge(v_zg3, g + 1)
                if g >= 2:
                    pool.wait_ge(s_out[g % 2], 16 * (g // 2))
                g_.tensor_tensor(o3[:, g % 2], zg3[:, g % 2],
                                 be3[:].rearrange("p (o d) -> p o d", o=1).to_broadcast([P, GS, D]), ALU.add)\
                    .then_inc(g_o3, 1)

            pool.wait_ge(l_small, 16 * 13)
            for g in range(NG + 1):
                if g < NG:
                    swap(g)
                if g >= 1:
                    norm3(g - 1)
                    shift3(g - 1)

        @block.scalar
        def _(act):
            a_ = nc.scalar

            def store_rows(g):
                act.wait_ge(p_rt, g + 1)
                if g >= 2:
                    act.wait_ge(st_h[g % 2], 16 * (g // 2))
                a_.activation(h_row[:, g % 2], bank[7][:], ACT.Copy).then_inc(a_hrow, 1)
                act.wait_ge(a_hrow, g + 1)
                act.dma_start(h_dram.rearrange("(t p) d -> p t d", p=P)[:, GS * g:GS * (g + 1), :], h_row[:, g % 2])\
                    .then_inc(st_h[g % 2], 16)

            act.dma_start(angle[:, 0, :], row(theta).to_broadcast([P, NB])).then_inc(l_ang, 16)
            act.dma_start(angle[:, 1, :], row(phi).to_broadcast([P, NB])).then_inc(l_ang, 16)
            act.wait_ge(k_pool, 1)
            for at, v, n in ((R_BI, l0_bi.rearrange("e (c p) -> (e c) p", p=P), E0 * FC),
                             (R_B1, exp_b1.rearrange("e (c p) -> (e c) p", p=P), E1 * FC),
                             (R_S2, sty_b2.rearrange("(c p) -> c p", p=P), 2)):
                act.dma_start(rows[at:at + n, :], v).then_inc(l_rows, 16)
            for at, v, n in ((R_H1, hyp_b1, SH), (R_H2, hyp_b2, SH), (R_S1, sty_b1, SM),
                             (R_LG, ln_g, D), (R_LB, ln_b, D), (R_DB, down_b, A)):
                act.dma_start(rows[at:at + 1, 0:n], row(v)).then_inc(l_rows, 16)
            for dst, src in ((emb_sb[:], subj_emb), (hw1[:], hyp_w1), (hw2[:], hyp_w2), (sw1[:], sty_w1),
                             (sw2[:], sty_w2), (rw[:], router_w), (dw[:], down_w), (uw[:], up_w),
                             (ub[:], row(up_b)), (b3[:], l3_b), (e3[:], l3_emb),
                             (g3[:], row(l3_gamma).to_broadcast([P, D])),
                             (be3[:], row(l3_beta).to_broadcast([P, D]))):
                act.dma_start(dst, src).then_inc(l_small, 16)
            act.wait_ge(v_arg, 1)
            a_.activation(trig[:], arg[:], ACT.Sin).then_inc(a_trig, 1)
            act.wait_ge(v_soft_in, 1)
            a_.activation(g_exp[:], g_abs[:], ACT.Exp, scale=-1.0).then_inc(ac, 1)
            act.wait_ge(ac, 1)
            a_.activation(g_ln[:], g_exp[:], ACT.Ln, bias=1.0).then_inc(a_soft, 1)

            act.wait_ge(v_pro, 1)
            for b in range(NB):
                e = act.value_load(ids[0:1, 0, b:b + 1], min_val=0, max_val=E0 - 1)
                act.wait_ge(p_up, b + 1)
                if b >= 2:
                    act.wait_ge(p_down, b - 1)
                for c in range(FC):
                    last = a_.activation(act0[:, b % 2, c, :], bank[1 + b % 2][:, c * P:(c + 1) * P], ACT.Gelu,
                                         bias=cols[:, bass.ds(e * FC + (R_BI + c), 1)])
                last.then_inc(a_gelu, 1)
                if b % GS == 1 and b >= 2 * GS + 1:
                    store_rows(b // GS - 2)
            for g in range(NG - 2, NG):
                store_rows(g)

            act.wait_ge(v_smax, 1)
            a_.activation(soft[:], soft_in[:], ACT.Exp).then_inc(a_sexp, 1)
            for i in range(4):
                act.wait_ge(p_m3, i + 1)
                a_.activation(m3[0:A, GS * i:GS * (i + 1), :], bank[1 + i][0:A, :], ACT.Copy).then_inc(a_m3, 1)

            for n in range(BLOCKS):
                if n == 0:
                    act.wait_ge(v_exp, 1)
                e = act.value_load(exp_i[0:1, n:n + 1], min_val=0, max_val=E1 - 1)
                act.wait_ge(p_t, n + 1)
                if n >= 2:
                    act.wait_ge(p_y, n - 1)
                for c in range(FC):
                    last = a_.activation(hid[:, n % 2, c, :], bank[2 + n % 2][:, c * P:(c + 1) * P], ACT.Relu,
                                         bias=cols[:, bass.ds(e * FC + (R_B1 + c), 1)])
                last.then_inc(a_hid, 1)

            for g in range(NG):
                act.wait_ge(p_xrT, g + 1)
                if g >= 2:
                    act.wait_ge(p_dn3, g - 1)
                a_.activation(xrT[:, g % 2, :], bank[0 + g % 2][:], ACT.Copy).then_inc(a_xrT, 1)
                act.wait_ge(p_dn3, g + 1)
                if g >= 2:
                    act.wait_ge(p_up3, g - 1)
                a_.activation(a3[0:A, g % 2, :], bank[2 + g % 2][0:A, :], ACT.Gelu,
                              bias=cols[0:A, R_DB:R_DB + 1]).then_inc(a_gelu3, 1)

        @block.tensor
        def _(pe):
            t_ = nc.tensor

            def mm(out_, lhsT, rhs, start=True, stop=True):
                return t_.matmul(out_, lhsT, rhs, start=start, stop=stop)

            def x_transposes(g):
                pe.wait_ge(l_x[g], 16)
                if g >= 1:
                    pe.wait_ge(v_xT, g)
                for k in range(GS):
                    last = t_.transpose(bank[0][:, k * P:(k + 1) * P], x_sb[:, GS * g + k, :], ident[:])
                last.then_inc(p_xT, 1)

            pe.wait_ge(k_pool, 5)
            pe.wait_ge(l_rows, 16 * 9)
            t_.transpose(pro[:, 0:NR], rows[:], ident[0:NR, 0:NR]).then_inc(p_pro, 1)
            x_transposes(0)
            pe.wait_ge(l_small, 16 * 13)
            pe.wait_ge(v_ids, 1)
            pe.wait_ge(v_pro, 1)
            mm(q_se[0:SE], emb_sb[:], pick_subj[:]).then_inc(p_pro, 1)
            pe.wait_ge(v_pro, 2)
            mm(q_h1[0:SH], hw1[:], hyp_a[:]).then_inc(p_pro, 1)
            pe.wait_ge(v_pro, 3)
            mm(q_h2[0:SH], hw2[:], hyp_b[:]).then_inc(p_pro, 1)
            pe.wait_ge(v_pro, 4)
            mm(q_s1[0:SM], sw1[:], hyp_c[:]).then_inc(p_pro, 1)
            pe.wait_ge(v_pro, 5)
            mm(q_ga, sw2[:, 0:D], hyp_d[:])
            mm(q_be, sw2[:, D:2 * D], hyp_d[:]).then_inc(p_pro, 1)
            t_.transpose(q_dwT, dw[:], ident[0:A, 0:A])
            t_.transpose(q_uwT[0:A], uw[:], ident[:])
            mm(q_c3[0:A], b3[:], pick_l3_valid[:], stop=False)
            mm(q_c3[0:A], e3[:], pick_l3[:], start=False).then_inc(p_pro, 1)

            def up(b):
                pe.wait_ge(v_xT, b // GS + 1)
                pe.wait_ge(l_w0[b % 4], 32 * (b // 4 + 1))
                if b >= 2:
                    pe.wait_ge(a_gelu, b - 1)
                for c in range(FC):
                    last = mm(bank[1 + b % 2][:, c * P:(c + 1) * P], wi[:, b % 4, c * P:(c + 1) * P],
                              xT[:, (b // GS) % 2, (b % GS) * P:(b % GS + 1) * P])
                last.then_inc(p_up, 1)

            def down(b):
                g, k = divmod(b, GS)
                pe.wait_ge(a_gelu, b + 1)
                if k == 0 and g >= 2:
                    pe.wait_ge(v_r0, g - 1)
                for c in range(FC):
                    last = mm(bank[3 + g % 2][:, k * P:(k + 1) * P], act0[:, b % 2, c, :], wo[:, b % 4, c, :],
                              start=(c == 0), stop=(c == FC - 1))
                last.then_inc(p_down, 1)

            def z_transposes(g):
                pe.wait_ge(v_z1, GS * (g + 1))
                if g >= 1:
                    pe.wait_ge(v_hT, g)
                else:
                    pe.wait_ge(v_pro, 9)
                for k in range(GS):
                    last = t_.transpose(bank[5][:, k * P:(k + 1) * P], z1[:, g % 2, k, :], ident[:])
                last.then_inc(p_zT, 1)

            def route(g):
                pe.wait_ge(v_hT, g + 1)
                if g >= 1:
                    pe.wait_ge(a_hrow, g)
                    pe.wait_ge(v_top, g)
                else:
                    pe.wait_ge(v_pro, 9)
                for k in range(GS):
                    mm(bank[6][:, k * E1:(k + 1) * E1], hT[:, g % 2, k * P:(k + 1) * P], rw[:])
                for k in range(GS):
                    last = t_.transpose(bank[7][:, k * P:(k + 1) * P], hT[:, g % 2, k * P:(k + 1) * P], ident[:])
                last.then_inc(p_rt, 1)

            for b in range(NB):
                if b % GS == 2 and b // GS + 1 < NG:
                    x_transposes(b // GS + 1)
                up(b)
                if b >= 1:
                    down(b - 1)
                if b % GS == 3 and b >= 2 * GS - 1:
                    z_transposes(b // GS - 1)
                if b % GS == 1 and b >= 2 * GS + 1:
                    route(b // GS - 2)
            down(NB - 1)
            route(NG - 2)
            pe.wait_ge(v_pro, 9)
            pe.wait_ge(v_xT, NG)
            mm(q_bias3, c3[:], uwT[:], stop=False)
            mm(q_bias3, ones_row[:], ub[:], start=False).then_inc(p_pro, 1)
            z_transposes(NG - 1)
            route(NG - 1)
            pe.wait_ge(v_top, NG)
            mm(bank[6][:, 128:256], upper[:], both[:].rearrange("p e t -> p (e t)"))
            mm(bank[6][:, 256:384], ones_bf[:], both[:].rearrange("p e t -> p (e t)")).then_inc(p_rank, 1)
            pe.wait_ge(v_w3, 1)
            pe.wait_ge(v_r0, NG)
            for b in range(NB):
                last = mm(bank[1 + b // GS][0:A, (b % GS) * D:(b % GS + 1) * D], w3v[:, b, :], uwT[:])
                if b % GS == GS - 1:
                    last.then_inc(p_m3, 1)
            pe.wait_ge(v_hot, 1)
            pe.wait_ge(v_pro, 10)
            for j in range(KT):
                if j % 8 == 0 and j:
                    pe.wait_ge(v_hot, j // 8 + 1)
                last = mm(bank[5][:, 0:2 * BLOCKS], hot_in[:, j, :],
                          hot_blk[:, j].rearrange("p a n -> p (a n)"), start=(j == 0), stop=(j == KT - 1))
            last.then_inc(p_inv, 1)

            pe.wait_ge(a_m3, 4)
            pe.wait_ge(v_idx, 1)
            pe.wait_ge(a_hrow, NG)
            pe.wait_ge(l_w1, 16 * (2 * E1 + 1))

            def rows_T(n):
                pe.wait_ge(gat[n % 4], 16 * (n // 4 + 1))
                if n >= 2:
                    pe.wait_ge(v_gT, n - 1)
                t_.transpose(bank[6 + n % 2][:, 0:P], got[:, n % 4, :], ident[:]).then_inc(p_gT, 1)

            def blk_up(n, e):
                pe.wait_ge(v_gT, n + 1)
                if n >= 2:
                    pe.wait_ge(v_u, n - 1)
                mm(bank[n % 2][:], gotT[:, n % 2, :], w1[:, bass.ds(e, 1), :].rearrange("p o f -> p (o f)"))\
                    .then_inc(p_u, 1)

            def blk_T(n):
                pe.wait_ge(v_u, n + 1)
                if n >= 2:
                    pe.wait_ge(a_hid, n - 1)
                for c in range(FC):
                    last = t_.transpose(bank[2 + n % 2][:, c * P:(c + 1) * P], up_sb[:, n % 2, c * P:(c + 1) * P],
                                        ident[:])
                last.then_inc(p_t, 1)

            def blk_down(n, e):
                pe.wait_ge(a_hid, n + 1)
                if n >= 2:
                    pe.wait_ge(v_y, n - 1)
                for c in range(FC):
                    last = mm(bank[4 + n % 2][:, 0:D], hid[:, n % 2, c, :],
                              w2[:, bass.ds(e, 1), c, :].rearrange("p o d -> p (o d)"),
                              start=(c == 0), stop=(c == FC - 1))
                last.then_inc(p_y, 1)

            ex = {}
            rows_T(0)
            for n in range(BLOCKS + 2):
                if n < BLOCKS:
                    ex[n] = pe.value_load(exp_i[0:1, n:n + 1], min_val=0, max_val=E1 - 1)
                    blk_up(n, ex[n])
                if n + 1 < BLOCKS:
                    rows_T(n + 1)
                if n >= 2:
                    blk_down(n - 2, ex.pop(n - 2))
                if 1 <= n <= BLOCKS:
                    blk_T(n - 1)

            def l3_T(g):
                pe.wait_ge(v_xr, g + 1)
                if g >= 2:
                    pe.wait_ge(a_xrT, g - 1)
                for k in range(GS):
                    last = t_.transpose(bank[g % 2][:, k * P:(k + 1) * P], xr[:, g % 2, k, :], ident[:])
                last.then_inc(p_xrT, 1)

            def l3_down(g):
                pe.wait_ge(a_xrT, g + 1)
                if g >= 2:
                    pe.wait_ge(a_gelu3, g - 1)
                mm(bank[2 + g % 2][0:A, :], dwT[:], xrT[:, g % 2, :]).then_inc(p_dn3, 1)

            def l3_up(g):
                pe.wait_ge(a_gelu3, g + 1)
                if g >= 2:
                    pe.wait_ge(v_r3, g - 1)
                for k in range(GS):
                    last = mm(bank[4 + g % 2][:, k * P:(k + 1) * P], a3[:, g % 2, k * P:(k + 1) * P],
                              m3[:, GS * g + k, :])
                last.then_inc(p_up3, 1)

            pe.wait_ge(l_m3, 16)
            pe.wait_ge(v_y, BLOCKS)
            for g in range(NG + 1):
                if g < NG:
                    l3_T(g)
                    l3_down(g)
                if g >= 1:
                    l3_up(g - 1)

        @block.vector
        def _(dve):
            v_ = nc.vector
            ch = Chain(dve, vc)
            do, settle = ch.do, ch.settle
            dve.wait_ge(k_pool, 4)
            v_.tensor_copy(col_f[:], col_i[:]).then_inc(k_dve, 1)
            v_.tensor_copy(col_bf[:], col_i[:]).then_inc(k_dve, 1)
            v_.tensor_copy(part_f[:], part_i[:]).then_inc(k_dve, 1)
            dve.wait_ge(l_ids, 48)
            do(v_.tensor_copy(ids_f[:], ids[:]))
            settle()
            dve.wait_ge(k_dve, 3)
            do(v_.tensor_scalar(id3_clip[:], ids_f[:, 2, :], 0.0, float(E3 - 1), ALU.max, ALU.min))
            do(v_.tensor_scalar(invalid[:], ids_f[:, 2, :], 0.0, None, ALU.is_ge))
            do(v_.tensor_scalar(pick_subj[:], ids_f[:, 1, :], part_f[0:NS, 0:1], None, ALU.is_equal))
            do(v_.tensor_scalar(pick_l3_valid[:], ids_f[0:E3, 2, :], part_f[0:E3, 0:1], None, ALU.is_equal))
            settle()
            do(v_.tensor_copy(id3_clip_i[:], id3_clip[0:1, :]))
            do(v_.tensor_scalar(pick_l3[:], id3_clip[0:E3, :], part_f[0:E3, 0:1], None, ALU.is_equal))
            do(v_.scalar_tensor_tensor(out=valid[:], in0=ids_f[:, 2, :], scalar=float(E3), in1=invalid[:],
                                       op0=ALU.is_lt, op1=ALU.mult))
            settle()
            v_.tensor_scalar(invalid[:], valid[:], -1.0, 1.0, ALU.mult, ALU.add).then_inc(v_ids, 1)
            dve.wait_ge(l_ang, 32)
            do(v_.tensor_copy(arg[:, 0:4:2, :], angle[:]))
            do(v_.tensor_scalar(arg[:, 1:4:2, :], angle[:], 1.5707963267948966, None, ALU.add))
            settle()
            do(v_.tensor_scalar(turns[:], arg[:], 0.15915494309189535, ROUND, ALU.mult, ALU.add))
            settle()
            do(v_.tensor_scalar(turns[:], turns[:], -ROUND, None, ALU.add))
            settle()
            do(v_.scalar_tensor_tensor(out=arg[:], in0=turns[:], scalar=-TWO_PI_HI, in1=arg[:],
                                       op0=ALU.mult, op1=ALU.add))
            settle()
            do(v_.scalar_tensor_tensor(out=arg[:], in0=turns[:], scalar=-TWO_PI_LO, in1=arg[:],
                                       op0=ALU.mult, op1=ALU.add))
            settle()
            v_.tensor_scalar(arg[:], arg[:], PI, -PI, ALU.min, ALU.max).then_inc(v_arg, 1)

            def evac_xT(g):
                dve.wait_ge(p_xT, g + 1)
                if g >= 2:
                    dve.wait_ge(p_up, GS * (g - 1))
                v_.tensor_copy(xT[:, g % 2, :], bank[0][:]).then_inc(v_xT, 1)

            dve.wait_ge(p_pro, 1)
            v_.tensor_copy(cols[:], pro[:, 0:NR]).then_inc(v_pro, 1)
            evac_xT(0)
            dve.wait_ge(p_pro, 2)
            v_.tensor_copy(hyp_a[:], q_se[0:SE]).then_inc(v_pro, 1)
            dve.wait_ge(p_pro, 3)
            dve.wait_ge(v_pro, 2)
            v_.tensor_scalar(hyp_b[:], q_h1, cols[:, R_H1:R_H1 + 1], 0.0, ALU.add, ALU.max).then_inc(v_pro, 1)
            dve.wait_ge(p_pro, 4)
            v_.tensor_scalar(hyp_c[:], q_h2, cols[:, R_H2:R_H2 + 1], None, ALU.add).then_inc(v_pro, 1)
            dve.wait_ge(p_pro, 5)
            v_.tensor_scalar(hyp_d[:], q_s1[0:SM], cols[0:SM, R_S1:R_S1 + 1], 0.0, ALU.add, ALU.max)\
                .then_inc(v_pro, 1)
            dve.wait_ge(p_pro, 6)
            do(v_.tensor_scalar(g_pre[:], q_ga, cols[:, R_S2:R_S2 + 1], None, ALU.add))
            v_.tensor_scalar(film_b[:], q_be, cols[:, R_S2 + 1:R_S2 + 2], None, ALU.add).then_inc(v_pro, 1)
            settle()
            v_.scalar_tensor_tensor(out=g_abs[:], in0=g_pre[:], scalar=-1.0, in1=g_pre[:],
                                    op0=ALU.mult, op1=ALU.max).then_inc(v_soft_in, 1)
            do(v_.tensor_scalar(g_pos[:], g_pre[:], 0.0, 1e-8, ALU.max, ALU.add))
            do(v_.tensor_tensor(g_sq[:], cols[:, R_LG:R_LG + 1], cols[:, R_LG:R_LG + 1], ALU.mult))
            dve.wait_ge(p_pro, 7)
            v_.tensor_copy(dwT[:], q_dwT).then_inc(v_pro, 1)
            v_.tensor_copy(uwT[:], q_uwT[0:A]).then_inc(v_pro, 1)
            v_.tensor_copy(c3[:], q_c3[0:A]).then_inc(v_pro, 1)
            settle()
            dve.wait_ge(a_soft, 1)
            do(v_.tensor_tensor(film_g[:], g_pos[:], g_ln[:], ALU.add))
            dve.wait_ge(a_trig, 1)
            for j in range(4):
                do(v_.tensor_copy(rot_same[:, :, j], trig[:, 2 * (j // 2) + 1, :]))
                last = v_.tensor_scalar(rot_swap[:, :, j], trig[:, 2 * (j // 2), :], 1.0 if j % 2 else -1.0,
                                        None, ALU.mult)
                if j < 3:
                    do(last)
            last.then_inc(v_rot, 1)
            settle()

            def stats(kind, src):
                for k in range(GS):
                    do(v_.bn_stats(st[:, kind, k, :], src(k)))
                settle()
                for k in range(GS):
                    do(v_.bn_aggr(mv[:, kind, k, :], st[:, kind, k, :]))
                settle()

            def l0_sum(g):
                dve.wait_ge(p_down, GS * (g + 1))
                dve.wait_ge(g_xbo, GS * (g + 1))
                v_.tensor_tensor(r0[:, g % 2].rearrange("p k d -> p (k d)"), bank[3 + g % 2][:],
                                 x_bo[:, g % 2].rearrange("p k d -> p (k d)"), ALU.add).then_inc(v_r0, 1)
                dve.wait_ge(v_r0, g + 1)
                stats(0, lambda k: r0[:, g % 2, k, :])
                v_.tensor_scalar(veps[:, 0, :], mv[:, 0, :, 1], 1e-12, None, ALU.add).then_inc(v_var, 1)

            power = [0]

            def normalise(dst, src, kind, s):
                power[0] += 1
                dve.wait_ge(g_rstd, power[0])
                for k in range(GS):
                    v_.tensor_scalar(dst[:, k, :], src(k), mv[:, kind, k, 0:1], rstd[:, kind, k:k + 1],
                                     ALU.subtract, ALU.mult).then_inc(s, 1)

            def l0_norm(g):
                if g >= 2:
                    dve.wait_ge(g_x1, GS * (g - 1))
                normalise(z0[:, g % 2], lambda k: r0[:, g % 2, k, :], 0, v_z0)

            def l1_stats(g):
                dve.wait_ge(g_x1, GS * (g + 1))
                stats(1, lambda k: x1[:, GS * g + k, :])
                v_.tensor_scalar(veps[:, 1, :], mv[:, 1, :, 1], 1e-5, None, ALU.add).then_inc(v_var, 1)

            def l1_norm(g):
                if g >= 2:
                    dve.wait_ge(p_zT, g - 1)
                normalise(z1[:, g % 2], lambda k: x1[:, GS * g + k, :], 1, v_z1)

            g_col, b_col = cols[:, R_LG:R_LG + 1], cols[:, R_LB:R_LB + 1]

            def row_stats(g):
                dve.wait_ge(p_zT, g + 1)
                stats(2, lambda k: bank[5][:, k * P:(k + 1) * P])
                v_.tensor_scalar(veps[:, 2, :], mv[:, 2, :, 1], g_sq[:], 1e-8, ALU.mult, ALU.add)\
                    .then_inc(v_var, 1)
                do(v_.tensor_scalar(film[:, 2, :], mv[:, 2, :, 0], g_col, b_col, ALU.mult, ALU.add))
                settle()
                do(v_.tensor_scalar(film[:, 3, :], film[:, 2, :], -1.0, b_col, ALU.mult, ALU.add))

            def film_h(g):
                power[0] += 1
                dve.wait_ge(g_rstd, power[0])
                bs = slice(GS * g, GS * (g + 1))
                do(v_.tensor_tensor(film[:, 4, :], rstd[:, 2, :], film_g[:, bs], ALU.mult))
                settle()
                do(v_.tensor_scalar(film[:, 0, :], film[:, 4, :], g_col, None, ALU.mult))
                do(v_.tensor_tensor(film[:, 5, :], film[:, 4, :], film[:, 3, :], ALU.mult))
                settle()
                do(v_.tensor_tensor(film[:, 1, :], film[:, 5, :], film_b[:, bs], ALU.add))
                settle()
                if g >= 2:
                    dve.wait_ge(p_rt, g - 1)
                for k in range(GS):
                    last = v_.tensor_scalar(hT[:, g % 2, k * P:(k + 1) * P], bank[5][:, k * P:(k + 1) * P],
                                            film[:, 0, k:k + 1], film[:, 1, k:k + 1], ALU.mult, ALU.add)
                last.then_inc(v_hT, 1)

            def top2(g):
                dve.wait_ge(p_rt, g + 1)
                ts = slice(GS * g, GS * (g + 1))
                do(v_.tensor_copy(logit_sb[:].rearrange("p k e -> p (k e)"), bank[6][:, 0:GS * E1]))
                settle()
                for k in range(GS):
                    do(v_.max(top_v[:, GS * g + k, :], logit_sb[:, k, :]))
                settle()
                for k in range(GS):
                    do(v_.max_index(top_i[:, k, :], top_v[:, GS * g + k, :], logit_sb[:, k, :]))
                settle()
                do(v_.tensor_copy(top_if[:], top_i[:, :, 0:2]))
                settle()
                for c in range(TOPK):
                    do(v_.tensor_tensor(pick[:, c, :, ts],
                                        col_f[:, 0:E1].rearrange("p (e o) -> p e o", o=1).to_broadcast([P, E1, GS]),
                                        top_if[:, :, c].rearrange("p (o t) -> p o t", o=1).to_broadcast([P, E1, GS]),
                                        ALU.is_equal))
                settle()
                v_.tensor_tensor(both[:, :, ts], pick[:, 0, :, ts], pick[:, 1, :, ts], ALU.add).then_inc(v_top, 1)

            for g in range(NG):
                if g + 1 < NG:
                    evac_xT(g + 1)
                if g >= 1:
                    l1_norm(g - 1)
                    row_stats(g - 1)
                l0_sum(g)
                if g >= 1:
                    film_h(g - 1)
                l0_norm(g)
                if g >= 2:
                    top2(g - 2)
                l1_stats(g)
            l1_norm(NG - 1)
            top2(NG - 2)
            row_stats(NG - 1)
            film_h(NG - 1)
            dve.wait_ge(l_w3, 16 * NB)
            dve.wait_ge(k_pool, 14)
            over_a = lambda v: v[0:A, :].rearrange("p (b o) -> p b o", o=1).to_broadcast([A, NB, A])
            do(v_.tensor_tensor(w3v[:], w3[:], over_a(valid), ALU.mult))
            do(v_.tensor_tensor(eye3[:], eye3[:], over_a(invalid), ALU.mult))
            settle()
            v_.tensor_tensor(w3v[:], w3v[:], eye3[:], ALU.add).then_inc(v_w3, 1)
            dve.wait_ge(p_pro, 8)
            v_.tensor_copy(bias3[:], q_bias3).then_inc(v_pro, 1)
            top2(NG - 1)

            dve.wait_ge(p_rank, 1)
            flat = lambda t: t[:].rearrange("p e t -> p (e t)")
            do(v_.tensor_copy(flat(tot), bank[6][:, 256:384]))
            settle()
            do(v_.tensor_tensor_scan(flat(run), flat(scan_mask), flat(tot), 0.0, ALU.mult, ALU.add))
            settle()
            do(v_.tensor_scalar(blk[:], run[:, :, NB - 1], float(P - 1) - (P - 1) / 2, 1.0 / P, ALU.add, ALU.mult))
            do(v_.tensor_tensor(flat(pos), flat(run), flat(tot), ALU.subtract))
            settle()
            do(v_.tensor_scalar(blk[:], blk[:], ROUND, -ROUND, ALU.add, ALU.add))
            do(v_.tensor_tensor(flat(pos), flat(pos), bank[6][:, 128:256], ALU.add))
            settle()
            do(v_.tensor_tensor_scan(blk_end[:], scan_mask[:, :, 1], blk[:], 0.0, ALU.mult, ALU.add))
            settle()
            do(v_.tensor_tensor(blk_start[:], blk_end[:], blk[:], ALU.subtract))
            do(v_.tensor_tensor(exp_cmp[:], col_f[0:1, 0:BLOCKS].rearrange("p (n o) -> p n o", o=1)
                                .to_broadcast([1, BLOCKS, E1]),
                                blk_end[0:1, :].rearrange("p (o e) -> p o e", o=1).to_broadcast([1, BLOCKS, E1]),
                                ALU.is_ge))
            settle()
            do(v_.scalar_tensor_tensor(out=pos[:], in0=blk_start[:].rearrange("p (e o) -> p e o", o=1)
                                       .to_broadcast([P, E1, NB]), scalar=float(P), in1=pos[:],
                                       op0=ALU.mult, op1=ALU.add))
            do(v_.tensor_reduce(exp_f[:], exp_cmp[:], AX.X, ALU.add))
            settle()
            v_.tensor_scalar(exp_i[:], exp_f[:], float(E1 - 1), None, ALU.min).then_inc(v_exp, 1)
            do(v_.tensor_tensor(slot_e[:].rearrange("p k e t -> p k (e t)"),
                                pick[:].rearrange("p k e t -> p k (e t)"),
                                pos[:].rearrange("p (o e) t -> p o (e t)", o=1).to_broadcast([P, TOPK, E1 * NB]),
                                ALU.mult))
            settle()
            do(v_.tensor_reduce(slot[:].rearrange("p (k t) -> p k t", k=TOPK),
                                slot_e[:].rearrange("p k e t -> p k t e"), AX.X, ALU.add))
            settle()
            do(v_.tensor_scalar(blk_of[:], slot[:], -(P - 1) / 2, 1.0 / P, ALU.add, ALU.mult))
            settle()
            do(v_.tensor_scalar(blk_of[:], blk_of[:], ROUND, -ROUND, ALU.add, ALU.add))
            settle()
            do(v_.scalar_tensor_tensor(out=in_blk[:], in0=blk_of[:], scalar=-float(P), in1=slot[:],
                                       op0=ALU.mult, op1=ALU.add))
            do(v_.tensor_copy(blk_of_bf[:], blk_of[:]))
            settle()
            do(v_.tensor_tensor(hot_tmp[:], col_bf[:, 0:BLOCKS].rearrange("p (o n) -> p o n", o=1)
                                .to_broadcast([P, KT, BLOCKS]),
                                blk_of_bf[:].rearrange("p (j o) -> p j o", o=1).to_broadcast([P, KT, BLOCKS]),
                                ALU.is_equal))
            settle()
            do(v_.tensor_scalar(hot_blk[:, :, 0, :], hot_tmp[:], part_f[:], None, ALU.mult))
            do(v_.tensor_tensor(hot_blk[:, :, 1, :], hot_tmp[:],
                                col_bf[:, 1:KT + 1].rearrange("p (j o) -> p j o", o=1).to_broadcast([P, KT, BLOCKS]),
                                ALU.mult))
            settle()
            for j in range(KT):
                last = v_.tensor_scalar(hot_in[:, j, :], col_bf[:], in_blk[:, j:j + 1], None, ALU.is_equal)
                if j % 8 == 7:
                    last.then_inc(v_hot, 1)
            dve.wait_ge(p_inv, 1)
            do(v_.tensor_copy(wrap[:], bank[5][:, 0:BLOCKS]))
            settle()
            do(v_.scalar_tensor_tensor(out=dest[:], in0=bank[5][:, BLOCKS:2 * BLOCKS], scalar=float(P),
                                       in1=wrap[:], op0=ALU.mult, op1=ALU.add))
            settle()
            do(v_.tensor_scalar(dest[:], dest[:], -float(P), None, ALU.add))
            settle()
            do(v_.tensor_scalar(wrap[:], dest[:], float(NROW), -float(NROW), ALU.is_ge, ALU.mult))
            do(v_.tensor_scalar(src_f[:], dest[:], 0.0, FAR, ALU.is_lt, ALU.mult))
            settle()
            do(v_.tensor_tensor(dest_i[:], dest[:], src_f[:], ALU.add))
            do(v_.tensor_tensor(dest[:], dest[:], wrap[:], ALU.add))
            settle()
            v_.tensor_scalar(src_i[:], dest[:], 0.0, None, ALU.max).then_inc(v_idx, 1)
            v_.tensor_tensor(soft_in[:], top_v[:], top_v[:, :, 0:1].to_broadcast([P, NB, 8]), ALU.subtract)\
                .then_inc(v_smax, 1)

            def gate_values():
                dve.wait_ge(a_sexp, 1)
                do(v_.tensor_reduce(soft_s[:, 0, :], soft[:], AX.X, ALU.add))
                settle()
                do(v_.reciprocal(soft_s[:, 1, :], soft_s[:, 0, :]))
                settle()
                do(v_.tensor_tensor(soft[:], soft[:], soft_s[:, 1, :].rearrange("p (t o) -> p t o", o=1)
                                    .to_broadcast([P, NB, 8]), ALU.mult))
                settle()
                do(v_.tensor_tensor(soft_s[:, 2, :], soft[:, :, 0], soft[:, :, 1], ALU.add))
                settle()
                do(v_.reciprocal(soft_s[:, 3, :], soft_s[:, 2, :]))
                settle()
                for c in range(TOPK):
                    last = v_.tensor_tensor(gates[:, c, :], soft[:, :, c], soft_s[:, 3, :], ALU.mult)
                    if c == 0:
                        do(last)
                last.then_inc(v_gate, 1)

            def rows_T(n):
                dve.wait_ge(p_gT, n + 1)
                if n >= 2:
                    dve.wait_ge(p_u, n - 1)
                v_.tensor_copy(gotT[:, n % 2, :], bank[6 + n % 2][:, 0:P]).then_inc(v_gT, 1)

            rows_T(0)
            for n in range(BLOCKS + 2):
                if n + 1 < BLOCKS:
                    rows_T(n + 1)
                if n < BLOCKS:
                    dve.wait_ge(p_u, n + 1)
                    if n >= 2:
                        dve.wait_ge(p_t, n - 1)
                    v_.tensor_copy(up_sb[:, n % 2, :], bank[n % 2][:]).then_inc(v_u, 1)
                if n >= 2:
                    m = n - 2
                    e = dve.value_load(exp_i[0:1, m:m + 1], min_val=0, max_val=E1 - 1)
                    dve.wait_ge(p_y, m + 1)
                    if m >= 4:
                        dve.wait_ge(sca[m % 4], 16 * (m // 4))
                    if m == 0:
                        dve.wait_ge(l_w1, 16 * (2 * E1 + 1))
                    v_.tensor_tensor(y_blk[:, m % 4, :], bank[4 + m % 2][:, 0:D],
                                     b2_tab[:, bass.ds(e, 1), :].rearrange("p o d -> p (o d)"), ALU.add)\
                        .then_inc(v_y, 1)
                if n == 4:
                    gate_values()

            def combine(g):
                dve.wait_ge(l_y[g], 32)
                if g == 0:
                    dve.wait_ge(v_gate, 1)
                    dve.wait_ge(v_rot, 1)
                for k in range(GS):
                    t = GS * g + k
                    do(v_.scalar_tensor_tensor(out=u_a[:, g % 2, k, :], in0=y_in[:, g, 0, k, :],
                                               scalar=gates[:, 0, t:t + 1], in1=x1[:, t, :],
                                               op0=ALU.mult, op1=ALU.add))
                settle()
                if g >= 2:
                    dve.wait_ge(g_swap, GS * (g - 1))
                for k in range(GS):
                    t = GS * g + k
                    v_.scalar_tensor_tensor(out=u_b[:, g % 2, k, :], in0=y_in[:, g, 1, k, :],
                                            scalar=gates[:, 1, t:t + 1], in1=u_a[:, g % 2, k, :],
                                            op0=ALU.mult, op1=ALU.add).then_inc(v_u3, 1)

            def rotate(g):
                for k in range(GS):
                    t = GS * g + k
                    dve.wait_ge(v_u3, t + 1)
                    do(v_.tensor_tensor(t_same[:, g % 2, k, :].rearrange("p (q j) -> p q j", j=4),
                                        u_b[:, g % 2, k, :].rearrange("p (q j) -> p q j", j=4),
                                        rot_same[:, t:t + 1, :].to_broadcast([P, D // 4, 4]), ALU.mult))
                settle()
                dve.wait_ge(g_swap, GS * (g + 1))
                if g >= 2:
                    dve.wait_ge(p_xrT, g - 1)
                pairs = lambda t: t[:, g % 2].rearrange("p k (q j) -> p (k q) j", j=2)
                v_.tensor_tensor(pairs(xr), pairs(t_same), pairs(t_swap)[:, :, ::-1], ALU.add).then_inc(v_xr, 1)

            def l3_sum(g):
                dve.wait_ge(p_up3, g + 1)
                dve.wait_ge(v_xr, g + 1)
                fl = lambda t: t[:, g % 2].rearrange("p k d -> p (k d)")
                v_.tensor_tensor(fl(r3), bank[4 + g % 2][:], fl(xr), ALU.add).then_inc(v_r3, 1)
                dve.wait_ge(v_r3, g + 1)
                for k in range(GS):
                    do(v_.bn_stats(st3[:, k, :], r3[:, g % 2, k, :]))
                settle()
                for k in range(GS):
                    do(v_.bn_aggr(mv3[:, g % 2, k, :], st3[:, k, :]))
                settle()
                v_.tensor_scalar(ve3[:, g % 2, :], mv3[:, g % 2, :, 1], 1e-5, None, ALU.add).then_inc(v_var3, 1)

            def l3_norm(g):
                dve.wait_ge(g_rstd3, g + 1)
                if g >= 2:
                    dve.wait_ge(g_o3, g - 1)
                for k in range(GS):
                    do(v_.tensor_scalar(z3[:, g % 2, k, :], r3[:, g % 2, k, :], mv3[:, g % 2, k, 0:1],
                                        rs3[:, g % 2, k:k + 1], ALU.subtract, ALU.mult))
                settle()
                v_.tensor_tensor(zg3[:, g % 2], z3[:, g % 2],
                                 g3[:].rearrange("p (o d) -> p o d", o=1).to_broadcast([P, GS, D]), ALU.mult)\
                    .then_inc(v_zg3, 1)

            combine(0)
            rotate(0)
            for g in range(NG):
                if g + 1 < NG:
                    combine(g + 1)
                    rotate(g + 1)
                l3_sum(g)
                l3_norm(g)


_INS = ['x', 'itok_B_0_7', 'itok_B_6_14', 'condB_theta', 'condB_phi', 'itok_B_0_15',
        'L0_cond_Wi', 'L0_cond_bi', 'L0_cond_Wo', 'L0_cond_bo', 'L0_cond_gamma', 'L0_cond_beta',
        'L1_cond_ln_g', 'L1_cond_ln_b', 'L1_cond_subj_emb', 'L1_cond_hyp_w1', 'L1_cond_hyp_b1',
        'L1_cond_hyp_w2', 'L1_cond_hyp_b2', 'L1_cond_sty_w1', 'L1_cond_sty_b1', 'L1_cond_sty_w2',
        'L1_cond_sty_b2', 'L1_cond_router_w', 'L1_cond_exp_w1', 'L1_cond_exp_b1', 'L1_cond_exp_w2',
        'L1_cond_exp_b2', 'L3_cond_down_W', 'L3_cond_down_b', 'L3_cond_up_W', 'L3_cond_up_b',
        'L3_cond_expert_W', 'L3_cond_expert_b', 'L3_cond_domain_emb', 'L3_cond_ln_gamma',
        'L3_cond_ln_beta']


def kernel(**inputs):
    import numpy as _np
    import concourse.bacc as _bacc
    from concourse import mybir as _mybir
    from concourse.bass_utils import run_bass_kernel_spmd as _run

    nc = _bacc.Bacc("TRN2", target_bir_lowering=False, num_devices=1)
    arrays, args = {}, []
    for name in _INS:
        a = _np.ascontiguousarray(inputs[name])
        arrays[f"in_{name}_dram"] = a
        args.append(nc.dram_tensor(f"in_{name}_dram", a.shape, _mybir.dt.from_np(a.dtype), kind="ExternalInput").ap())
    shape = tuple(inputs['x'].shape)
    args.append(nc.dram_tensor("out_dram", shape, _mybir.dt.float32, kind="ExternalOutput").ap())
    conditional_layers_kernel(nc, *args)
    r = _run(nc, [arrays], core_ids=[0])
    return r.results[0]["out_dram"]
```

```python
from contextlib import ExitStack

import concourse.bass as bass
from concourse import mybir

F32 = mybir.dt.float32
BF16 = mybir.dt.bfloat16
I32 = mybir.dt.int32
U32 = mybir.dt.uint32
ALU = mybir.AluOpType
ACT = mybir.ActivationFunctionType
AX = mybir.AxisListType

P = 128
ROUND = 12582912.0
TWO_PI_HI = 6.28125
TWO_PI_LO = 0.0019353071795864769
PI = 3.1415925
FAR = 1.0e6


def small_layout(sizes):
    at, cols = {}, 0
    for name, width in sizes:
        at[name] = (cols, width)
        cols += width
    return at, cols


SMALL = (("angle", 16), ("sign", 1), ("l0_bi", 32), ("exp_b1", 32), ("hyp_b1", 1), ("hyp_b2", 1), ("sty_b1", 1),
         ("sty_b2", 2), ("ln_g", 1), ("ln_b", 1), ("down_b", 1), ("emb", 64), ("hyp_w1", 128),
         ("hyp_w2", 128), ("sty_w1", 64), ("sty_w2", 256), ("router_w", 8),
         ("down_T", 32), ("down_T_swapped", 32), ("up_T", 128), ("l3_b", 32), ("l3_emb", 32))


def conditional_layers_kernel(nc, x, ids3, l0_wi, l0_wo, l0_rows, small_in, exp_w1, exp_w2, exp_b2,
                              l3_w, l3_rows, out):
    NB, S, D = x.shape
    E0, _, FF = l0_wi.shape
    E1 = exp_w1.shape[0]
    NS, SE, SH, SM = 32, 64, 128, 64
    E3, A, _ = l3_w.shape
    FC = FF // P
    GS = 4
    NG = NB // GS
    GW = GS * D
    TOPK = 2
    NROW = NB * S
    BLOCKS = (TOPK * NROW + E1 * (P - 1)) // P
    KT = TOPK * NB
    LAG = 2
    assert S == P and D == P and GW == 512 and FC * P == 512

    h_dram = nc.dram_tensor("h_rows", (NROW, D), F32, kind="Internal").ap()
    y_dram = nc.dram_tensor("expert_rows", (TOPK * NROW, D), F32, kind="Internal").ap()

    with ExitStack() as ctx:
        def sb(name, shape, dt=F32):
            return ctx.enter_context(nc.sbuf_tensor(name, shape, dt))

        def sem(name):
            return ctx.enter_context(nc.semaphore(name))

        bank = [ctx.enter_context(nc.psum_tensor(f"bank{i}", [P, 512], F32)) for i in range(8)]

        ident = sb("ident", [P, P])
        upper = sb("upper", [P, P], BF16)
        ones_bf = sb("ones_bf", [P, P], BF16)
        ones_row = sb("ones_row", [1, NB])
        minus_half = sb("minus_half", [P, 16])
        col_i = sb("col_i", [P, P], I32)
        col_f = sb("col_f", [P, P])
        col_bf = sb("col_bf", [P, P], BF16)
        part_i = sb("part_i", [P, 1], I32)
        part_f = sb("part_f", [P, 1])
        scan_mask = sb("scan_mask", [P, E1, NB])

        ids = sb("ids", [NS, 3, NB], I32)
        ids_f = sb("ids_f", [NS, 3, NB])
        id3_clip = sb("id3_clip", [NS, NB])
        id3_clip_i = sb("id3_clip_i", [1, NB], I32)
        valid = sb("valid", [NS, NB])
        invalid = sb("invalid", [NS, NB])
        pick_subj = sb("pick_subj", [NS, NB])
        pick_l3 = sb("pick_l3", [E3, NB])
        pick_l3_valid = sb("pick_l3_valid", [E3, NB])
        at, small_cols = small_layout(SMALL)
        assert small_cols == small_in.shape[1]
        small = sb("small", [P, small_cols])
        col = {name: first for name, (first, _) in at.items()}
        part = lambda name, rows: small[0:rows, at[name][0]:at[name][0] + at[name][1]]
        cols = small
        R_BI, R_B1, R_H1, R_H2, R_S1, R_S2, R_LG, R_LB, R_DB = (
            col[n] for n in ("l0_bi", "exp_b1", "hyp_b1", "hyp_b2", "sty_b1", "sty_b2", "ln_g", "ln_b", "down_b"))
        S_SIGN = col["sign"]
        angle = part("angle", P)
        arg = sb("arg", [P, 2, NB])
        turns = sb("turns", [P, 2, NB])
        trig = sb("trig", [P, 2, NB])
        rot_same = sb("rot_same", [P, NB])
        rot_swap = sb("rot_swap", [P, NB])
        emb_sb = part("emb", NS)
        hw1 = part("hyp_w1", SE)
        hw2 = part("hyp_w2", SH)
        sw1 = part("sty_w1", SH)
        sw2 = part("sty_w2", SM)
        hyp_a = sb("hyp_a", [SE, NB])
        hyp_b = sb("hyp_b", [SH, NB])
        hyp_c = sb("hyp_c", [SH, NB])
        hyp_d = sb("hyp_d", [SM, NB])
        g_pre = sb("g_pre", [P, NB])
        g_abs = sb("g_abs", [P, NB])
        g_exp = sb("g_exp", [P, NB])
        g_ln = sb("g_ln", [P, NB])
        g_pos = sb("g_pos", [P, NB])
        film_g = sb("film_g", [P, NB])
        film_b = sb("film_b", [P, NB])
        g_sq = sb("g_sq", [P, 1])
        rw = part("router_w", P)

        x_sb = sb("x_sb", [P, NB, D])
        xT = sb("xT", [P, 2, GW])
        w0_place = sb("w0_place", [P, 2, 4 * FF])
        wi = w0_place[:, 0].rearrange("p (s f) -> p s f", s=4)
        wo = w0_place[:, 1].rearrange("p (s c d) -> p s c d", s=4, c=FC)
        tab0 = sb("tab0", [P, 3, E0, D])
        act0 = sb("act0", [P, 2, FC, P])
        x_bo = sb("x_bo", [P, 2, GS, D])
        r0 = sb("r0", [P, 2, GS, D])
        z0 = sb("z0", [P, 2, GS, D])
        zg = sb("zg", [P, 2, GS, D])
        x1 = sb("x1", [P, NB, D])
        st = sb("st", [P, 4, GS, 6])
        mv = sb("mv", [P, 3, GS, 2])
        veps = sb("veps", [P, 3, GS])
        rstd = sb("rstd", [P, 3, GS])

        z1 = sb("z1", [P, 2, GS, D])
        film = sb("film", [P, 6, GS])
        hT = sb("hT", [P, 2, GW])
        h_row = sb("h_row", [P, 2, GS, D])
        top_v = sb("top_v", [P, NB, 8])
        top_i = sb("top_i", [P, GS, 8], U32)
        top_if = sb("top_if", [P, GS, 2])
        pick = sb("pick", [P, TOPK, E1, NB], BF16)
        both = sb("both", [P, E1, NB], BF16)
        logit_sb = sb("logit_sb", [P, GS, E1])
        tot = sb("tot", [P, E1, NB])
        run = sb("run", [P, E1, NB])
        pos = sb("pos", [P, E1, NB])
        blk = sb("blk", [P, E1])
        blk_end = sb("blk_end", [P, E1])
        blk_start = sb("blk_start", [P, E1])
        slot_e = sb("slot_e", [P, TOPK, E1, NB])
        slot = sb("slot", [P, KT])
        blk_of = sb("blk_of", [P, KT])
        in_blk = sb("in_blk", [P, KT])
        hot_in = sb("hot_in", [P, KT, P], BF16)
        hot_blk = sb("hot_blk", [P, KT, 2, BLOCKS], BF16)
        hot_tmp = sb("hot_tmp", [P, KT, BLOCKS], BF16)
        blk_of_bf = sb("blk_of_bf", [P, KT], BF16)
        dest = sb("dest", [P, BLOCKS])
        wrap = sb("wrap", [P, BLOCKS])
        src_f = sb("src_f", [P, BLOCKS])
        src_i = sb("src_i", [P, BLOCKS], I32)
        dest_i = sb("dest_i", [P, BLOCKS], I32)
        exp_cmp = sb("exp_cmp", [1, BLOCKS, E1])
        exp_f = sb("exp_f", [1, BLOCKS])
        exp_i = sb("exp_i", [1, BLOCKS], I32)
        soft = sb("soft", [P, NB, 8])
        soft_in = sb("soft_in", [P, NB, 8])
        soft_s = sb("soft_s", [P, 4, NB])
        gates = sb("gates", [P, TOPK, NB])
        w1 = sb("w1", [P, E1, FF])
        w2 = sb("w2", [P, E1, FC, D])
        b2_tab = sb("b2_tab", [P, E1, D])
        got = sb("got", [P, 4, D])
        gotT = sb("gotT", [P, 2, P])
        w1_now = sb("w1_now", [P, 2, FF])
        hid = sb("hid", [P, 2, FC, P])
        y_blk = sb("y_blk", [P, 4, D])

        dwT = part("down_T", P)
        dwT_sw = part("down_T_swapped", P)
        uwT = part("up_T", A)
        w3 = sb("w3", [A, NB, A])
        w3v = sb("w3v", [A, NB, A])
        eye3 = sb("eye3", [A, NB, A])
        b3 = part("l3_b", E3)
        e3 = part("l3_emb", E3)
        c3 = sb("c3", [A, NB])
        bias3 = sb("bias3", [NB, D])
        m3 = sb("m3", [A + 1, NB, D])
        rows3 = sb("rows3", [P, 3, D])
        g3, be3, ub = rows3[:, 0, :], rows3[:, 1, :], rows3[0:1, 2, :]
        assert NG * TOPK * GS * D == 2 * 4 * FF
        y_in = w0_place[:].rearrange("p a f -> p (a f)").rearrange("p (g k t d) -> p g k t d", g=NG, k=TOPK, t=GS)
        u_a, u_b, uT, rot = x_bo, z0, xT, x_sb
        rot_diag = sb("rot_diag", [P, D])
        dw_rot = sb("dw_rot", [P, NB, A])
        dw_tmp = sb("dw_tmp", [P, NB, A])
        a3 = sb("a3", [A + 1, 2, GW])
        z3 = sb("z3", [P, 2, GS, D])
        zg3 = sb("zg3", [P, 2, GS, D])
        o3 = sb("o3", [P, 2, GS, D])
        st3 = sb("st3", [P, GS, 6])
        mv3 = sb("mv3", [P, 2, GS, 2])
        ve3 = sb("ve3", [P, 2, GS])
        rs3 = sb("rs3", [P, 2, GS])
        nmr3 = sb("nmr3", [P, 2, GS])

        l_ids = sem("l_ids")
        l_x = [sem(f"l_x{g}") for g in range(NG)]
        l_w0 = [sem(f"l_w0_{s}") for s in range(4)]
        l_tab0 = sem("l_tab0")
        l_small = sem("l_small")
        l_rows3 = sem("l_rows3")
        l_w1 = sem("l_w1")
        l_w3 = sem("l_w3")
        l_m3 = sem("l_m3")
        l_y = [sem(f"l_y{g}") for g in range(NG)]
        k_pool = sem("k_pool")
        k_dve = sem("k_dve")
        v_ids = sem("v_ids")
        p_pro = sem("p_pro")
        v_pro = sem("v_pro")
        v_soft_in = sem("v_soft_in")
        a_soft = sem("a_soft")
        v_arg = sem("v_arg")
        a_trig = sem("a_trig")
        v_rot = sem("v_rot")
        vc = sem("vc")
        gc = sem("gc")
        ac = sem("ac")
        p_xT = sem("p_xT")
        v_xT = sem("v_xT")
        p_up = sem("p_up")
        a_gelu = sem("a_gelu")
        p_down = sem("p_down")
        g_xbo = sem("g_xbo")
        v_r0 = sem("v_r0")
        v_var = sem("v_var")
        g_rstd = sem("g_rstd")
        v_z0 = sem("v_z0")
        g_x1 = sem("g_x1")
        v_z1 = sem("v_z1")
        p_zT = sem("p_zT")
        v_hT = sem("v_hT")
        p_rt = sem("p_rt")
        v_top = sem("v_top")
        a_hrow = sem("a_hrow")
        st_h = [sem(f"st_h{i}") for i in range(2)]
        p_rank = sem("p_rank")
        v_hot = sem("v_hot")
        p_inv = sem("p_inv")
        v_idx = sem("v_idx")
        v_exp = sem("v_exp")
        v_w3 = sem("v_w3")
        p_m3 = sem("p_m3")
        a_m3 = sem("a_m3")
        v_smax = sem("v_smax")
        a_sexp = sem("a_sexp")
        v_gate = sem("v_gate")
        gat = [sem(f"gat{i}") for i in range(4)]
        sca = [sem(f"sca{i}") for i in range(4)]
        p_gT = sem("p_gT")
        v_gT = sem("v_gT")
        p_u = sem("p_u")
        v_w1 = sem("v_w1")
        a_hid = sem("a_hid")
        p_y = sem("p_y")
        v_y = sem("v_y")
        v_u3 = sem("v_u3")
        p_uT = sem("p_uT")
        a_uT = sem("a_uT")
        p_dn3 = sem("p_dn3")
        a_gelu3 = sem("a_gelu3")
        p_res3 = sem("p_res3")
        p_up3 = sem("p_up3")
        v_nmr3 = sem("v_nmr3")
        a_z3 = sem("a_z3")
        v_var3 = sem("v_var3")
        g_rstd3 = sem("g_rstd3")
        v_zg3 = sem("v_zg3")
        g_o3 = sem("g_o3")
        s_out = [sem(f"s_out{i}") for i in range(2)]

        class Chain:

            def __init__(self, eng, s):
                self.eng, self.s, self.n = eng, s, 0

            def do(self, ins):
                self.n += 1
                return ins.then_inc(self.s, 1)

            def settle(self):
                self.eng.wait_ge(self.s, self.n)

        block = ctx.enter_context(nc.Block())

        y_v = y_dram.rearrange("(k t p) d -> p k t d", k=TOPK, p=P)
        row = lambda ap: ap.rearrange("(o n) -> o n", o=1)
        pro = bank[7]
        c0 = 0
        q_se, q_h1, q_h2, q_s1, q_ga, q_be = (pro[:, c0 + NB * i:c0 + NB * (i + 1)] for i in range(6))
        q_c3 = bank[5][:, 0:NB]
        q_bias3 = bank[0][0:NB, 0:D]

        @block.sync
        def _(sp):
            sp.dma_start(ids[:].rearrange("p k b -> p (k b)"), row(ids3).to_broadcast([NS, 3 * NB])).then_inc(l_ids, 16)
            sp.wait_ge(l_ids, 16)
            for b in range(NB):
                e = sp.value_load(ids[0:1, 0, b:b + 1], min_val=0, max_val=E0 - 1)
                if b >= 4:
                    sp.wait_ge(p_down, b - 3)
                sp.dma_start(wi[:, b % 4, :], l0_wi[bass.ds(e, 1)].rearrange("o h i -> h (o i)"))\
                    .then_inc(l_w0[b % 4], 16)
                sp.dma_start(wo[:, b % 4, :, :], l0_wo[bass.ds(e, 1)].rearrange("o (c p) h -> p (o c) h", p=P))\
                    .then_inc(l_w0[b % 4], 16)
                if b >= NB - E1:
                    i = b - (NB - E1)
                    sp.dma_start(w1[:, i, :], exp_w1[i]).then_inc(l_w1, 16)
                    sp.dma_start(w2[:, i], exp_w2[i].rearrange("(c p) d -> p c d", p=P)).then_inc(l_w1, 16)
            sp.dma_start(b2_tab[:], exp_b2.rearrange("(o e) d -> o e d", o=1).to_broadcast([P, E1, D]))\
                .then_inc(l_w1, 16)
            sp.wait_ge(v_ids, 1)
            for b in range(NB):
                e = sp.value_load(id3_clip_i[0:1, b:b + 1], min_val=0, max_val=E3 - 1)
                sp.dma_start(w3[:, b, :], l3_w[bass.ds(e, 1)].rearrange("o p a -> p (o a)")).then_inc(l_w3, 16)
            sp.wait_ge(v_pro, 7)
            sp.dma_start(m3[A:A + 1, :, :], bias3[:]).then_inc(l_m3, 16)
            for i in range(4):
                sp.wait_ge(sca[i], 16 * len(range(i, BLOCKS, 4)))
            for g in range(NG):
                sp.dma_start(y_in[:, g, 0], y_v[:, 0, GS * g:GS * (g + 1), :]).then_inc(l_y[g], 16)
            for g in range(NG):
                sp.wait_ge(g_o3, g + 1)
                sp.dma_start(out[GS * g:GS * (g + 1)].rearrange("b s d -> s b d"), o3[:, g % 2])\
                    .then_inc(s_out[g % 2], 16)
            for i in range(2):
                sp.wait_ge(s_out[i], 16 * NG // 2)

        @block.gpsimd
        def _(pool):
            g_ = nc.gpsimd
            ch = Chain(pool, gc)
            g_.memset(ones_row[:], 1.0).then_inc(k_pool, 1)
            g_.memset(ident[:], 0.0).then_inc(k_pool, 1)
            g_.iota(col_i[:], [[1, P]], base=0, channel_multiplier=0).then_inc(k_pool, 1)
            g_.iota(part_i[:], [[0, 1]], base=0, channel_multiplier=1).then_inc(k_pool, 1)
            pool.wait_ge(k_pool, 4)
            g_.affine_select(out=ident[:], in_=ident[:], compare_op=ALU.not_equal, fill=1.0, base=0,
                             pattern=[[-1, P]], channel_multiplier=1).then_inc(k_pool, 1)
            g_.memset(minus_half[:], -0.5).then_inc(k_pool, 1)
            g_.memset(ones_bf[:], 1.0).then_inc(k_pool, 1)
            g_.memset(scan_mask[:], 1.0).then_inc(k_pool, 1)
            g_.memset(a3[:], 1.0).then_inc(k_pool, 1)
            pool.wait_ge(k_pool, 9)
            g_.affine_select(out=upper[:], in_=ones_bf[:], compare_op=ALU.is_gt, fill=0.0, base=0,
                             pattern=[[1, P]], channel_multiplier=-1).then_inc(k_pool, 1)
            g_.memset(scan_mask[:, :, 0:1], 0.0).then_inc(k_pool, 1)
            g_.memset(eye3[:], 0.0).then_inc(k_pool, 1)
            pool.wait_ge(k_pool, 12)
            g_.affine_select(out=eye3[:], in_=eye3[:], compare_op=ALU.not_equal, fill=1.0, base=0,
                             pattern=[[0, NB], [-1, A]], channel_multiplier=1).then_inc(k_pool, 1)

            pool.wait_ge(l_ids, 16)
            pool.wait_ge(l_tab0, 16)

            def expert_row(b):
                return pool.value_load(ids[0:1, 0, b:b + 1], min_val=0, max_val=E0 - 1)

            def add_bo(g):
                pool.wait_ge(l_x[g], 16)
                if g >= 2:
                    pool.wait_ge(v_r0, g - 1)
                for k in range(GS):
                    b = GS * g + k
                    e = expert_row(b)
                    last = g_.tensor_tensor(x_bo[:, g % 2, k, :], x_sb[:, b, :],
                                            tab0[:, 0, bass.ds(e, 1), :].rearrange("p o d -> p (o d)"), ALU.add)
                    last.then_inc(g_xbo, 1)

            turn = [0]

            def power(kind):
                turn[0] += 1
                pool.wait_ge(v_var, turn[0])
                g_.tensor_tensor(rstd[:, kind, :], veps[:, kind, :], minus_half[:, 0:GS], ALU.pow)\
                    .then_inc(g_rstd, 1)

            def scale_shift(g):
                for k in range(GS):
                    b = GS * g + k
                    e = expert_row(b)
                    pool.wait_ge(v_z0, b + 1)
                    ch.do(g_.tensor_tensor(zg[:, g % 2, k, :], z0[:, g % 2, k, :],
                                           tab0[:, 1, bass.ds(e, 1), :].rearrange("p o d -> p (o d)"), ALU.mult))
                    ch.settle()
                    g_.tensor_tensor(x1[:, b, :], zg[:, g % 2, k, :],
                                     tab0[:, 2, bass.ds(e, 1), :].rearrange("p o d -> p (o d)"), ALU.add)\
                        .then_inc(g_x1, 1)

            add_bo(0)
            for g in range(NG):
                if g >= 1:
                    power(2)
                power(0)
                if g + 1 < NG:
                    add_bo(g + 1)
                scale_shift(g)
                power(1)
            power(2)

            pool.wait_ge(v_idx, 1)
            for i in range(2):
                pool.wait_ge(st_h[i], 16 * NG // 2)

            def gather(n):
                if n >= 4:
                    pool.wait_ge(p_gT, n - 3)
                g_.indirect_dma_start(got[:, n % 4, :], None, h_dram,
                                      bass.IndirectOffsetOnAxis(ap=src_i[:, n:n + 1], axis=0))\
                    .then_inc(gat[n % 4], 16)

            def scatter(n):
                pool.wait_ge(v_y, n + 1)
                g_.indirect_dma_start(y_dram, bass.IndirectOffsetOnAxis(ap=dest_i[:, n:n + 1], axis=0),
                                      y_blk[:, n % 4, :], None,
                                      bounds_check=TOPK * NROW - 1, oob_is_err=False)\
                    .then_inc(sca[n % 4], 16)

            for n in range(3):
                gather(n)
            for n in range(BLOCKS + LAG):
                if n + 3 < BLOCKS:
                    gather(n + 3)
                if n >= LAG:
                    scatter(n - LAG)

            def power3(g):
                pool.wait_ge(v_var3, g + 1)
                g_.tensor_tensor(rs3[:, g % 2, :], ve3[:, g % 2, :], minus_half[:, 0:GS], ALU.pow)\
                    .then_inc(g_rstd3, 1)

            def shift3(g):
                pool.wait_ge(v_zg3, g + 1)
                if g >= 2:
                    pool.wait_ge(s_out[g % 2], 16 * (g // 2))
                g_.tensor_tensor(o3[:, g % 2], zg3[:, g % 2],
                                 be3.rearrange("p (o d) -> p o d", o=1).to_broadcast([P, GS, D]), ALU.add)\
                    .then_inc(g_o3, 1)

            pool.wait_ge(l_rows3, 16)
            power3(0)
            for g in range(NG):
                if g + 1 < NG:
                    power3(g + 1)
                shift3(g)

        @block.scalar
        def _(act):
            a_ = nc.scalar

            def store_rows(g):
                act.wait_ge(p_rt, g + 1)
                if g >= 2:
                    act.wait_ge(st_h[g % 2], 16 * (g // 2))
                a_.activation(h_row[:, g % 2], bank[7][:], ACT.Copy).then_inc(a_hrow, 1)
                act.wait_ge(a_hrow, g + 1)
                act.dma_start(h_dram.rearrange("(t p) d -> p t d", p=P)[:, GS * g:GS * (g + 1), :], h_row[:, g % 2])\
                    .then_inc(st_h[g % 2], 16)

            def load_x(g):
                act.dma_start(x_sb[:, GS * g:GS * (g + 1), :],
                              x[GS * g:GS * (g + 1)].rearrange("b s d -> s b d")).then_inc(l_x[g], 16)

            load_x(0)
            act.dma_start(small[:], small_in).then_inc(l_small, 16)
            act.dma_start(tab0[:].rearrange("p i e d -> p (i e d)"),
                          row(l0_rows.rearrange("i e d -> (i e d)")).to_broadcast([P, 3 * E0 * D])).then_inc(l_tab0, 16)
            for g in range(1, NG):
                load_x(g)
            act.dma_start(rows3[:].rearrange("p i d -> p (i d)"),
                          row(l3_rows.rearrange("i d -> (i d)")).to_broadcast([P, 3 * D])).then_inc(l_rows3, 16)
            act.wait_ge(v_arg, 1)
            a_.activation(trig[:], arg[:], ACT.Sin).then_inc(a_trig, 1)
            act.wait_ge(v_soft_in, 1)
            a_.activation(g_exp[:], g_abs[:], ACT.Exp, scale=-1.0).then_inc(ac, 1)
            act.wait_ge(ac, 1)
            a_.activation(g_ln[:], g_exp[:], ACT.Ln, bias=1.0).then_inc(a_soft, 1)

            act.wait_ge(l_ids, 16)
            for b in range(NB):
                e = act.value_load(ids[0:1, 0, b:b + 1], min_val=0, max_val=E0 - 1)
                act.wait_ge(p_up, b + 1)
                if b >= 2:
                    act.wait_ge(p_down, b - 1)
                for c in range(FC):
                    last = a_.activation(act0[:, b % 2, c, :], bank[1 + b % 2][:, c * P:(c + 1) * P], ACT.Gelu,
                                         bias=cols[:, bass.ds(e * FC + (R_BI + c), 1)])
                last.then_inc(a_gelu, 1)
                if b % GS == 1 and b >= 2 * GS + 1:
                    store_rows(b // GS - 2)
            for g in range(NG - 2, NG):
                store_rows(g)

            act.wait_ge(v_smax, 1)
            a_.activation(soft[:], soft_in[:], ACT.Exp).then_inc(a_sexp, 1)
            for i in range(4):
                act.wait_ge(p_m3, i + 1)
                a_.activation(m3[0:A, GS * i:GS * (i + 1), :], bank[1 + i][0:A, :], ACT.Copy).then_inc(a_m3, 1)

            for n in range(BLOCKS):
                if n == 0:
                    act.wait_ge(v_exp, 1)
                e = act.value_load(exp_i[0:1, n:n + 1], min_val=0, max_val=E1 - 1)
                act.wait_ge(p_u, n + 1)
                if n >= 2:
                    act.wait_ge(p_y, n - 1)
                for c in range(FC):
                    last = a_.activation(hid[:, n % 2, c, :], bank[n % 2][:, c * P:(c + 1) * P], ACT.Relu,
                                         bias=cols[:, bass.ds(e * FC + (R_B1 + c), 1)])
                last.then_inc(a_hid, 1)

            for i in range(4):
                act.wait_ge(sca[i], 16 * len(range(i, BLOCKS, 4)))
            for g in range(NG):
                act.dma_start(y_in[:, g, 1], y_v[:, 1, GS * g:GS * (g + 1), :]).then_inc(l_y[g], 16)

            def evac_uT(g):
                act.wait_ge(p_uT, g + 1)
                if g >= 2:
                    act.wait_ge(p_res3, g - 1)
                a_.activation(uT[:, g % 2, :], bank[g % 2][:], ACT.Copy).then_inc(a_uT, 1)

            def gelu3(g):
                act.wait_ge(p_dn3, g + 1)
                if g >= 2:
                    act.wait_ge(p_up3, g - 1)
                a_.activation(a3[0:A, g % 2, :], bank[2 + g % 2][0:A, :], ACT.Gelu,
                              bias=cols[0:A, R_DB:R_DB + 1]).then_inc(a_gelu3, 1)

            def norm3(g):
                act.wait_ge(v_nmr3, g + 1)
                if g >= 2:
                    act.wait_ge(v_zg3, g - 1)
                for k in range(GS):
                    last = a_.activation(z3[:, g % 2, k, :], bank[4 + g][:, k * P:(k + 1) * P], ACT.Identity,
                                         bias=nmr3[:, g % 2, k:k + 1], scale=rs3[:, g % 2, k:k + 1])
                last.then_inc(a_z3, 1)

            evac_uT(0)
            gelu3(0)
            for g in range(1, NG):
                evac_uT(g)
                gelu3(g)
                norm3(g - 1)
            norm3(NG - 1)

        @block.tensor
        def _(pe):
            t_ = nc.tensor

            def mm(out_, lhsT, rhs, start=True, stop=True):
                return t_.matmul(out_, lhsT, rhs, start=start, stop=stop)

            def x_transposes(g):
                pe.wait_ge(l_x[g], 16)
                if g >= 1:
                    pe.wait_ge(v_xT, g)
                for k in range(GS):
                    last = t_.transpose(bank[0][:, k * P:(k + 1) * P], x_sb[:, GS * g + k, :], ident[:])
                last.then_inc(p_xT, 1)

            pe.wait_ge(k_pool, 5)
            x_transposes(0)
            pe.wait_ge(l_small, 16)
            pe.wait_ge(v_ids, 1)
            mm(q_se[0:SE], emb_sb, pick_subj[:]).then_inc(p_pro, 1)
            pe.wait_ge(v_pro, 1)
            mm(q_h1[0:SH], hw1, hyp_a[:]).then_inc(p_pro, 1)
            pe.wait_ge(v_pro, 2)
            mm(q_h2[0:SH], hw2, hyp_b[:]).then_inc(p_pro, 1)
            pe.wait_ge(v_pro, 3)
            mm(q_s1[0:SM], sw1, hyp_c[:]).then_inc(p_pro, 1)
            pe.wait_ge(v_pro, 4)
            mm(q_ga, sw2[:, 0:D], hyp_d[:])
            mm(q_be, sw2[:, D:2 * D], hyp_d[:]).then_inc(p_pro, 1)
            mm(q_c3[0:A], b3, pick_l3_valid[:], stop=False)
            mm(q_c3[0:A], e3, pick_l3[:], start=False).then_inc(p_pro, 1)

            def up(b):
                pe.wait_ge(v_xT, b // GS + 1)
                pe.wait_ge(l_w0[b % 4], 32 * (b // 4 + 1))
                if b >= 2:
                    pe.wait_ge(a_gelu, b - 1)
                for c in range(FC):
                    last = mm(bank[1 + b % 2][:, c * P:(c + 1) * P], wi[:, b % 4, c * P:(c + 1) * P],
                              xT[:, (b // GS) % 2, (b % GS) * P:(b % GS + 1) * P])
                last.then_inc(p_up, 1)

            def down(b):
                g, k = divmod(b, GS)
                pe.wait_ge(a_gelu, b + 1)
                if k == 0 and g >= 2:
                    pe.wait_ge(v_r0, g - 1)
                for c in range(FC):
                    last = mm(bank[3 + g % 2][:, k * P:(k + 1) * P], act0[:, b % 2, c, :], wo[:, b % 4, c, :],
                              start=(c == 0), stop=(c == FC - 1))
                last.then_inc(p_down, 1)

            def z_transposes(g):
                pe.wait_ge(v_z1, GS * (g + 1))
                if g >= 1:
                    pe.wait_ge(v_hT, g)
                else:
                    pe.wait_ge(v_pro, 6)
                for k in range(GS):
                    last = t_.transpose(bank[5][:, k * P:(k + 1) * P], z1[:, g % 2, k, :], ident[:])
                last.then_inc(p_zT, 1)

            def route(g):
                pe.wait_ge(v_hT, g + 1)
                if g >= 1:
                    pe.wait_ge(a_hrow, g)
                    pe.wait_ge(v_top, g)
                else:
                    pe.wait_ge(v_pro, 6)
                for k in range(GS):
                    mm(bank[6][:, k * E1:(k + 1) * E1], hT[:, g % 2, k * P:(k + 1) * P], rw)
                for k in range(GS):
                    last = t_.transpose(bank[7][:, k * P:(k + 1) * P], hT[:, g % 2, k * P:(k + 1) * P], ident[:])
                last.then_inc(p_rt, 1)

            for b in range(NB):
                if b % GS == 2 and b // GS + 1 < NG:
                    x_transposes(b // GS + 1)
                up(b)
                if b >= 1:
                    down(b - 1)
                if b % GS == 3 and b >= 2 * GS - 1:
                    z_transposes(b // GS - 1)
                if b % GS == 1 and b >= 2 * GS + 1:
                    route(b // GS - 2)
            down(NB - 1)
            route(NG - 2)
            pe.wait_ge(v_pro, 6)
            pe.wait_ge(v_xT, NG)
            pe.wait_ge(l_rows3, 16)
            mm(q_bias3, c3[:], uwT, stop=False)
            mm(q_bias3, ones_row[:], ub, start=False).then_inc(p_pro, 1)
            z_transposes(NG - 1)
            route(NG - 1)
            pe.wait_ge(v_top, NG)
            mm(bank[6][:, 128:256], upper[:], both[:].rearrange("p e t -> p (e t)"))
            mm(bank[6][:, 256:384], ones_bf[:], both[:].rearrange("p e t -> p (e t)")).then_inc(p_rank, 1)
            pe.wait_ge(v_w3, 1)
            pe.wait_ge(v_r0, NG)
            for b in range(NB):
                last = mm(bank[1 + b // GS][0:A, (b % GS) * D:(b % GS + 1) * D], w3v[:, b, :], uwT)
                if b % GS == GS - 1:
                    last.then_inc(p_m3, 1)
            pe.wait_ge(v_hot, 1)
            pe.wait_ge(v_pro, 7)
            for j in range(KT):
                if j % 8 == 0 and j:
                    pe.wait_ge(v_hot, j // 8 + 1)
                last = mm(bank[5][:, 0:2 * BLOCKS], hot_in[:, j, :],
                          hot_blk[:, j].rearrange("p a n -> p (a n)"), start=(j == 0), stop=(j == KT - 1))
            last.then_inc(p_inv, 1)

            pe.wait_ge(a_m3, 4)
            pe.wait_ge(v_idx, 1)
            pe.wait_ge(a_hrow, NG)
            pe.wait_ge(l_w1, 16 * (2 * E1 + 1))

            def rows_T(n):
                pe.wait_ge(gat[n % 4], 16 * (n // 4 + 1))
                if n >= 2:
                    pe.wait_ge(v_gT, n - 1)
                t_.transpose(bank[6 + n % 2][:, 0:P], got[:, n % 4, :], ident[:]).then_inc(p_gT, 1)

            def blk_up(n):
                pe.wait_ge(v_gT, n + 1)
                pe.wait_ge(v_w1, n + 1)
                if n >= 2:
                    pe.wait_ge(a_hid, n - 1)
                for c in range(FC):
                    last = mm(bank[n % 2][:, c * P:(c + 1) * P], w1_now[:, n % 2, c * P:(c + 1) * P],
                              gotT[:, n % 2, :])
                last.then_inc(p_u, 1)

            def blk_down(n, e):
                pe.wait_ge(a_hid, n + 1)
                if n >= 2:
                    pe.wait_ge(v_y, n - 1)
                for c in range(FC):
                    last = mm(bank[4 + n % 2][:, 0:D], hid[:, n % 2, c, :],
                              w2[:, bass.ds(e, 1), c, :].rearrange("p o d -> p (o d)"),
                              start=(c == 0), stop=(c == FC - 1))
                last.then_inc(p_y, 1)

            rows_T(0)
            for n in range(BLOCKS + LAG):
                if n >= LAG:
                    e = pe.value_load(exp_i[0:1, n - LAG:n - LAG + 1], min_val=0, max_val=E1 - 1)
                if n < BLOCKS:
                    blk_up(n)
                if n + 1 < BLOCKS:
                    rows_T(n + 1)
                if n >= LAG:
                    blk_down(n - LAG, e)

            def l3_T(g):
                pe.wait_ge(v_u3, GS * (g + 1))
                if g >= 2:
                    pe.wait_ge(a_uT, g - 1)
                for k in range(GS):
                    last = t_.transpose(bank[g % 2][:, k * P:(k + 1) * P], u_b[:, g % 2, k, :], ident[:])
                last.then_inc(p_uT, 1)

            def l3_down(g):
                pe.wait_ge(a_uT, g + 1)
                if g >= 2:
                    pe.wait_ge(a_gelu3, g - 1)
                for k in range(GS):
                    last = mm(bank[2 + g % 2][0:A, k * P:(k + 1) * P], dw_rot[:, GS * g + k, :],
                              uT[:, g % 2, k * P:(k + 1) * P])
                last.then_inc(p_dn3, 1)

            def l3_up(g):
                for k in range(GS):
                    ks = slice(k * P, (k + 1) * P)
                    last = mm(bank[4 + g][:, ks], uT[:, g % 2, ks], rot[:, GS * g + k, :],
                              start=(k == 0), stop=False)
                last.then_inc(p_res3, 1)
                pe.wait_ge(a_gelu3, g + 1)
                for k in range(GS):
                    ks = slice(k * P, (k + 1) * P)
                    last = mm(bank[4 + g][:, ks], a3[:, g % 2, ks], m3[:, GS * g + k, :], start=False,
                              stop=(k == GS - 1))
                last.then_inc(p_up3, 1)

            pe.wait_ge(l_m3, 16)
            pe.wait_ge(v_y, BLOCKS)
            pe.wait_ge(v_rot, 1)
            l3_T(0)
            for g in range(NG):
                l3_down(g)
                l3_up(g)
                if g + 1 < NG:
                    l3_T(g + 1)

        @block.vector
        def _(dve):
            v_ = nc.vector
            ch = Chain(dve, vc)
            do, settle = ch.do, ch.settle
            dve.wait_ge(k_pool, 4)
            v_.tensor_copy(col_f[:], col_i[:]).then_inc(k_dve, 1)
            v_.tensor_copy(col_bf[:], col_i[:]).then_inc(k_dve, 1)
            v_.tensor_copy(part_f[:], part_i[:]).then_inc(k_dve, 1)
            dve.wait_ge(l_ids, 16)
            do(v_.tensor_copy(ids_f[:], ids[:]))
            settle()
            dve.wait_ge(k_dve, 3)
            do(v_.tensor_scalar(id3_clip[:], ids_f[:, 2, :], 0.0, float(E3 - 1), ALU.max, ALU.min))
            do(v_.tensor_scalar(invalid[:], ids_f[:, 2, :], 0.0, None, ALU.is_ge))
            do(v_.tensor_scalar(pick_subj[:], ids_f[:, 1, :], part_f[0:NS, 0:1], None, ALU.is_equal))
            do(v_.tensor_scalar(pick_l3_valid[:], ids_f[0:E3, 2, :], part_f[0:E3, 0:1], None, ALU.is_equal))
            settle()
            do(v_.tensor_copy(id3_clip_i[:], id3_clip[0:1, :]))
            do(v_.tensor_scalar(pick_l3[:], id3_clip[0:E3, :], part_f[0:E3, 0:1], None, ALU.is_equal))
            do(v_.scalar_tensor_tensor(out=valid[:], in0=ids_f[:, 2, :], scalar=float(E3), in1=invalid[:],
                                       op0=ALU.is_lt, op1=ALU.mult))
            settle()
            v_.tensor_scalar(invalid[:], valid[:], -1.0, 1.0, ALU.mult, ALU.add).then_inc(v_ids, 1)
            dve.wait_ge(l_small, 16)
            do(v_.tensor_copy(arg[:, 0, :], angle))
            do(v_.tensor_scalar(arg[:, 1, :], angle, 1.5707963267948966, None, ALU.add))
            settle()
            do(v_.tensor_scalar(turns[:], arg[:], 0.15915494309189535, ROUND, ALU.mult, ALU.add))
            settle()
            do(v_.tensor_scalar(turns[:], turns[:], -ROUND, None, ALU.add))
            settle()
            do(v_.scalar_tensor_tensor(out=arg[:], in0=turns[:], scalar=-TWO_PI_HI, in1=arg[:],
                                       op0=ALU.mult, op1=ALU.add))
            settle()
            do(v_.scalar_tensor_tensor(out=arg[:], in0=turns[:], scalar=-TWO_PI_LO, in1=arg[:],
                                       op0=ALU.mult, op1=ALU.add))
            settle()
            v_.tensor_scalar(arg[:], arg[:], PI, -PI, ALU.min, ALU.max).then_inc(v_arg, 1)

            def evac_xT(g):
                dve.wait_ge(p_xT, g + 1)
                if g >= 2:
                    dve.wait_ge(p_up, GS * (g - 1))
                v_.tensor_copy(xT[:, g % 2, :], bank[0][:]).then_inc(v_xT, 1)

            evac_xT(0)
            dve.wait_ge(p_pro, 1)
            v_.tensor_copy(hyp_a[:], q_se[0:SE]).then_inc(v_pro, 1)
            dve.wait_ge(p_pro, 2)
            v_.tensor_scalar(hyp_b[:], q_h1, cols[:, R_H1:R_H1 + 1], 0.0, ALU.add, ALU.max).then_inc(v_pro, 1)
            dve.wait_ge(p_pro, 3)
            v_.tensor_scalar(hyp_c[:], q_h2, cols[:, R_H2:R_H2 + 1], None, ALU.add).then_inc(v_pro, 1)
            dve.wait_ge(p_pro, 4)
            v_.tensor_scalar(hyp_d[:], q_s1[0:SM], cols[0:SM, R_S1:R_S1 + 1], 0.0, ALU.add, ALU.max)\
                .then_inc(v_pro, 1)
            dve.wait_ge(p_pro, 5)
            do(v_.tensor_scalar(g_pre[:], q_ga, cols[:, R_S2:R_S2 + 1], None, ALU.add))
            v_.tensor_scalar(film_b[:], q_be, cols[:, R_S2 + 1:R_S2 + 2], None, ALU.add).then_inc(v_pro, 1)
            settle()
            v_.scalar_tensor_tensor(out=g_abs[:], in0=g_pre[:], scalar=-1.0, in1=g_pre[:],
                                    op0=ALU.mult, op1=ALU.max).then_inc(v_soft_in, 1)
            do(v_.tensor_scalar(g_pos[:], g_pre[:], 0.0, 1e-8, ALU.max, ALU.add))
            do(v_.tensor_tensor(g_sq[:], cols[:, R_LG:R_LG + 1], cols[:, R_LG:R_LG + 1], ALU.mult))
            dve.wait_ge(p_pro, 6)
            v_.tensor_copy(c3[:], q_c3[0:A]).then_inc(v_pro, 1)
            settle()
            dve.wait_ge(a_soft, 1)
            do(v_.tensor_tensor(film_g[:], g_pos[:], g_ln[:], ALU.add))
            dve.wait_ge(a_trig, 1)
            do(v_.tensor_copy(rot_same[:], trig[:, 1, :]))
            do(v_.tensor_scalar(rot_swap[:], trig[:, 0, :], small[:, S_SIGN:S_SIGN + 1], None, ALU.mult))
            settle()

            def stats(kind, src):
                for k in range(GS):
                    do(v_.bn_stats(st[:, kind, k, :], src(k)))
                settle()
                for k in range(GS):
                    do(v_.bn_aggr(mv[:, kind, k, :], st[:, kind, k, :]))
                settle()

            def l0_sum(g):
                dve.wait_ge(p_down, GS * (g + 1))
                dve.wait_ge(g_xbo, GS * (g + 1))
                v_.tensor_tensor(r0[:, g % 2].rearrange("p k d -> p (k d)"), bank[3 + g % 2][:],
                                 x_bo[:, g % 2].rearrange("p k d -> p (k d)"), ALU.add).then_inc(v_r0, 1)
                dve.wait_ge(v_r0, g + 1)
                stats(0, lambda k: r0[:, g % 2, k, :])
                v_.tensor_scalar(veps[:, 0, :], mv[:, 0, :, 1], 1e-12, None, ALU.add).then_inc(v_var, 1)

            power = [0]

            def normalise(dst, src, kind, s):
                power[0] += 1
                dve.wait_ge(g_rstd, power[0])
                for k in range(GS):
                    v_.tensor_scalar(dst[:, k, :], src(k), mv[:, kind, k, 0:1], rstd[:, kind, k:k + 1],
                                     ALU.subtract, ALU.mult).then_inc(s, 1)

            def l0_norm(g):
                if g >= 2:
                    dve.wait_ge(g_x1, GS * (g - 1))
                normalise(z0[:, g % 2], lambda k: r0[:, g % 2, k, :], 0, v_z0)

            def l1_stats(g):
                dve.wait_ge(g_x1, GS * (g + 1))
                stats(1, lambda k: x1[:, GS * g + k, :])
                v_.tensor_scalar(veps[:, 1, :], mv[:, 1, :, 1], 1e-5, None, ALU.add).then_inc(v_var, 1)

            def l1_norm(g):
                if g >= 2:
                    dve.wait_ge(p_zT, g - 1)
                normalise(z1[:, g % 2], lambda k: x1[:, GS * g + k, :], 1, v_z1)

            g_col, b_col = cols[:, R_LG:R_LG + 1], cols[:, R_LB:R_LB + 1]

            def row_stats(g):
                dve.wait_ge(p_zT, g + 1)
                stats(2, lambda k: bank[5][:, k * P:(k + 1) * P])
                v_.tensor_scalar(veps[:, 2, :], mv[:, 2, :, 1], g_sq[:], 1e-8, ALU.mult, ALU.add)\
                    .then_inc(v_var, 1)
                do(v_.tensor_scalar(film[:, 2, :], mv[:, 2, :, 0], g_col, b_col, ALU.mult, ALU.add))
                settle()
                do(v_.tensor_scalar(film[:, 3, :], film[:, 2, :], -1.0, b_col, ALU.mult, ALU.add))

            def film_h(g):
                power[0] += 1
                dve.wait_ge(g_rstd, power[0])
                bs = slice(GS * g, GS * (g + 1))
                do(v_.tensor_tensor(film[:, 4, :], rstd[:, 2, :], film_g[:, bs], ALU.mult))
                settle()
                do(v_.tensor_scalar(film[:, 0, :], film[:, 4, :], g_col, None, ALU.mult))
                do(v_.tensor_tensor(film[:, 5, :], film[:, 4, :], film[:, 3, :], ALU.mult))
                settle()
                do(v_.tensor_tensor(film[:, 1, :], film[:, 5, :], film_b[:, bs], ALU.add))
                settle()
                if g >= 2:
                    dve.wait_ge(p_rt, g - 1)
                for k in range(GS):
                    last = v_.tensor_scalar(hT[:, g % 2, k * P:(k + 1) * P], bank[5][:, k * P:(k + 1) * P],
                                            film[:, 0, k:k + 1], film[:, 1, k:k + 1], ALU.mult, ALU.add)
                last.then_inc(v_hT, 1)

            def top2(g):
                dve.wait_ge(p_rt, g + 1)
                ts = slice(GS * g, GS * (g + 1))
                do(v_.tensor_copy(logit_sb[:].rearrange("p k e -> p (k e)"), bank[6][:, 0:GS * E1]))
                settle()
                for k in range(GS):
                    do(v_.max(top_v[:, GS * g + k, :], logit_sb[:, k, :]))
                settle()
                for k in range(GS):
                    do(v_.max_index(top_i[:, k, :], top_v[:, GS * g + k, :], logit_sb[:, k, :]))
                settle()
                do(v_.tensor_copy(top_if[:], top_i[:, :, 0:2]))
                settle()
                for c in range(TOPK):
                    do(v_.tensor_tensor(pick[:, c, :, ts],
                                        col_f[:, 0:E1].rearrange("p (e o) -> p e o", o=1).to_broadcast([P, E1, GS]),
                                        top_if[:, :, c].rearrange("p (o t) -> p o t", o=1).to_broadcast([P, E1, GS]),
                                        ALU.is_equal))
                settle()
                v_.tensor_tensor(both[:, :, ts], pick[:, 0, :, ts], pick[:, 1, :, ts], ALU.add).then_inc(v_top, 1)

            for g in range(NG):
                if g + 1 < NG:
                    evac_xT(g + 1)
                if g >= 1:
                    l1_norm(g - 1)
                    row_stats(g - 1)
                l0_sum(g)
                if g >= 1:
                    film_h(g - 1)
                l0_norm(g)
                if g >= 2:
                    top2(g - 2)
                l1_stats(g)
            l1_norm(NG - 1)
            top2(NG - 2)
            row_stats(NG - 1)
            film_h(NG - 1)
            dve.wait_ge(l_w3, 16 * NB)
            dve.wait_ge(k_pool, 13)
            over_a = lambda v: v[0:A, :].rearrange("p (b o) -> p b o", o=1).to_broadcast([A, NB, A])
            do(v_.tensor_tensor(w3v[:], w3[:], over_a(valid), ALU.mult))
            do(v_.tensor_tensor(eye3[:], eye3[:], over_a(invalid), ALU.mult))
            settle()
            v_.tensor_tensor(w3v[:], w3v[:], eye3[:], ALU.add).then_inc(v_w3, 1)
            dve.wait_ge(p_pro, 7)
            v_.tensor_copy(bias3[:], q_bias3).then_inc(v_pro, 1)
            top2(NG - 1)

            dve.wait_ge(p_rank, 1)
            flat = lambda t: t[:].rearrange("p e t -> p (e t)")
            do(v_.tensor_copy(flat(tot), bank[6][:, 256:384]))
            settle()
            do(v_.tensor_tensor_scan(flat(run), flat(scan_mask), flat(tot), 0.0, ALU.mult, ALU.add))
            settle()
            do(v_.tensor_scalar(blk[:], run[:, :, NB - 1], float(P - 1) - (P - 1) / 2, 1.0 / P, ALU.add, ALU.mult))
            do(v_.tensor_tensor(flat(pos), flat(run), flat(tot), ALU.subtract))
            settle()
            do(v_.tensor_scalar(blk[:], blk[:], ROUND, -ROUND, ALU.add, ALU.add))
            do(v_.tensor_tensor(flat(pos), flat(pos), bank[6][:, 128:256], ALU.add))
            settle()
            do(v_.tensor_tensor_scan(blk_end[:], scan_mask[:, :, 1], blk[:], 0.0, ALU.mult, ALU.add))
            settle()
            do(v_.tensor_tensor(blk_start[:], blk_end[:], blk[:], ALU.subtract))
            do(v_.tensor_tensor(exp_cmp[:], col_f[0:1, 0:BLOCKS].rearrange("p (n o) -> p n o", o=1)
                                .to_broadcast([1, BLOCKS, E1]),
                                blk_end[0:1, :].rearrange("p (o e) -> p o e", o=1).to_broadcast([1, BLOCKS, E1]),
                                ALU.is_ge))
            settle()
            do(v_.scalar_tensor_tensor(out=pos[:], in0=blk_start[:].rearrange("p (e o) -> p e o", o=1)
                                       .to_broadcast([P, E1, NB]), scalar=float(P), in1=pos[:],
                                       op0=ALU.mult, op1=ALU.add))
            do(v_.tensor_reduce(exp_f[:], exp_cmp[:], AX.X, ALU.add))
            settle()
            v_.tensor_scalar(exp_i[:], exp_f[:], float(E1 - 1), None, ALU.min).then_inc(v_exp, 1)
            do(v_.tensor_tensor(slot_e[:].rearrange("p k e t -> p k (e t)"),
                                pick[:].rearrange("p k e t -> p k (e t)"),
                                pos[:].rearrange("p (o e) t -> p o (e t)", o=1).to_broadcast([P, TOPK, E1 * NB]),
                                ALU.mult))
            settle()
            do(v_.tensor_reduce(slot[:].rearrange("p (k t) -> p k t", k=TOPK),
                                slot_e[:].rearrange("p k e t -> p k t e"), AX.X, ALU.add))
            settle()
            do(v_.tensor_scalar(blk_of[:], slot[:], -(P - 1) / 2, 1.0 / P, ALU.add, ALU.mult))
            settle()
            do(v_.tensor_scalar(blk_of[:], blk_of[:], ROUND, -ROUND, ALU.add, ALU.add))
            settle()
            do(v_.scalar_tensor_tensor(out=in_blk[:], in0=blk_of[:], scalar=-float(P), in1=slot[:],
                                       op0=ALU.mult, op1=ALU.add))
            do(v_.tensor_copy(blk_of_bf[:], blk_of[:]))
            settle()
            do(v_.tensor_tensor(hot_tmp[:], col_bf[:, 0:BLOCKS].rearrange("p (o n) -> p o n", o=1)
                                .to_broadcast([P, KT, BLOCKS]),
                                blk_of_bf[:].rearrange("p (j o) -> p j o", o=1).to_broadcast([P, KT, BLOCKS]),
                                ALU.is_equal))
            settle()
            do(v_.tensor_scalar(hot_blk[:, :, 0, :], hot_tmp[:], part_f[:], None, ALU.mult))
            do(v_.tensor_tensor(hot_blk[:, :, 1, :], hot_tmp[:],
                                col_bf[:, 1:KT + 1].rearrange("p (j o) -> p j o", o=1).to_broadcast([P, KT, BLOCKS]),
                                ALU.mult))
            settle()
            for j in range(KT):
                last = v_.tensor_scalar(hot_in[:, j, :], col_bf[:], in_blk[:, j:j + 1], None, ALU.is_equal)
                if j % 8 == 7:
                    last.then_inc(v_hot, 1)
            dve.wait_ge(p_inv, 1)
            do(v_.tensor_copy(wrap[:], bank[5][:, 0:BLOCKS]))
            settle()
            do(v_.scalar_tensor_tensor(out=dest[:], in0=bank[5][:, BLOCKS:2 * BLOCKS], scalar=float(P),
                                       in1=wrap[:], op0=ALU.mult, op1=ALU.add))
            settle()
            do(v_.tensor_scalar(dest[:], dest[:], -float(P), None, ALU.add))
            settle()
            do(v_.tensor_scalar(wrap[:], dest[:], float(NROW), -float(NROW), ALU.is_ge, ALU.mult))
            do(v_.tensor_scalar(src_f[:], dest[:], 0.0, FAR, ALU.is_lt, ALU.mult))
            settle()
            do(v_.tensor_tensor(dest_i[:], dest[:], src_f[:], ALU.add))
            do(v_.tensor_tensor(dest[:], dest[:], wrap[:], ALU.add))
            settle()
            v_.tensor_scalar(src_i[:], dest[:], 0.0, None, ALU.max).then_inc(v_idx, 1)
            v_.tensor_tensor(soft_in[:], top_v[:], top_v[:, :, 0:1].to_broadcast([P, NB, 8]), ALU.subtract)\
                .then_inc(v_smax, 1)

            def gate_values():
                dve.wait_ge(a_sexp, 1)
                do(v_.tensor_reduce(soft_s[:, 0, :], soft[:], AX.X, ALU.add))
                settle()
                do(v_.reciprocal(soft_s[:, 1, :], soft_s[:, 0, :]))
                settle()
                do(v_.tensor_tensor(soft[:], soft[:], soft_s[:, 1, :].rearrange("p (t o) -> p t o", o=1)
                                    .to_broadcast([P, NB, 8]), ALU.mult))
                settle()
                do(v_.tensor_tensor(soft_s[:, 2, :], soft[:, :, 0], soft[:, :, 1], ALU.add))
                settle()
                do(v_.reciprocal(soft_s[:, 3, :], soft_s[:, 2, :]))
                settle()
                for c in range(TOPK):
                    last = v_.tensor_tensor(gates[:, c, :], soft[:, :, c], soft_s[:, 3, :], ALU.mult)
                    if c == 0:
                        do(last)
                last.then_inc(v_gate, 1)

            swapped = lambda ap: ap.rearrange("p (q j) -> p q j", j=2)[:, :, ::-1]
            paired = lambda ap: ap.rearrange("p (q j) -> p q j", j=2)

            def rotation(b):
                settle()
                do(v_.tensor_scalar(rot_diag[:], ident[:], rot_same[:, b:b + 1], None, ALU.mult))
                settle()
                last = v_.scalar_tensor_tensor(out=paired(rot[:, b, :]), in0=swapped(ident[:]),
                                               scalar=rot_swap[:, b:b + 1], in1=paired(rot_diag[:]),
                                               op0=ALU.mult, op1=ALU.add)
                if b == NB - 1:
                    last.then_inc(v_rot, 1)
                else:
                    do(last)

            def down_rotated():
                over_b = lambda t: t.rearrange("p (o a) -> p o a", o=1).to_broadcast([P, NB, A])
                over_a_ = lambda t: t[:].rearrange("p (b o) -> p b o", o=1).to_broadcast([P, NB, A])
                do(v_.tensor_tensor(dw_rot[:], over_b(dwT), over_a_(rot_same), ALU.mult))
                do(v_.tensor_tensor(dw_tmp[:], over_b(dwT_sw), over_a_(rot_swap), ALU.mult))
                settle()
                do(v_.tensor_tensor(dw_rot[:], dw_rot[:], dw_tmp[:], ALU.add))
                settle()

            def rows_T(n):
                dve.wait_ge(p_gT, n + 1)
                if n >= 2:
                    dve.wait_ge(p_u, n - 1)
                v_.tensor_copy(gotT[:, n % 2, :], bank[6 + n % 2][:, 0:P]).then_inc(v_gT, 1)

            ex = {}

            def load_expert(n):
                ex[n] = dve.value_load(exp_i[0:1, n:n + 1], min_val=0, max_val=E1 - 1)

            def stage_w1(n):
                if n >= 2:
                    dve.wait_ge(p_u, n - 1)
                v_.tensor_copy(w1_now[:, n % 2, :], w1[:, bass.ds(ex[n], 1), :].rearrange("p o f -> p (o f)"))\
                    .then_inc(v_w1, 1)

            load_expert(0)
            load_expert(1)

            dve.wait_ge(l_w1, 16 * (2 * E1 + 1))
            stage_w1(0)
            rows_T(0)
            for n in range(BLOCKS + LAG):
                if n + 1 < BLOCKS:
                    stage_w1(n + 1)
                    rows_T(n + 1)
                if n + 2 < BLOCKS:
                    load_expert(n + 2)
                if n >= LAG:
                    m = n - LAG
                    dve.wait_ge(p_y, m + 1)
                    if m >= 4:
                        dve.wait_ge(sca[m % 4], 16 * (m // 4))
                    v_.tensor_tensor(y_blk[:, m % 4, :], bank[4 + m % 2][:, 0:D],
                                     b2_tab[:, bass.ds(ex.pop(m), 1), :].rearrange("p o d -> p (o d)"), ALU.add)\
                        .then_inc(v_y, 1)
                if n == 2:
                    gate_values()
                if n == 3:
                    down_rotated()
                if 4 <= n < 4 + NB:
                    rotation(n - 4)

            def combine(g):
                dve.wait_ge(l_y[g], 32)
                for k in range(GS):
                    t = GS * g + k
                    do(v_.scalar_tensor_tensor(out=u_a[:, g % 2, k, :], in0=y_in[:, g, 0, k, :],
                                               scalar=gates[:, 0, t:t + 1], in1=x1[:, t, :],
                                               op0=ALU.mult, op1=ALU.add))
                settle()
                if g >= 2:
                    dve.wait_ge(p_uT, g - 1)
                for k in range(GS):
                    t = GS * g + k
                    v_.scalar_tensor_tensor(out=u_b[:, g % 2, k, :], in0=y_in[:, g, 1, k, :],
                                            scalar=gates[:, 1, t:t + 1], in1=u_a[:, g % 2, k, :],
                                            op0=ALU.mult, op1=ALU.add).then_inc(v_u3, 1)

            def stats3(g):
                dve.wait_ge(p_up3, g + 1)
                for k in range(GS):
                    do(v_.bn_stats(st3[:, k, :], bank[4 + g][:, k * P:(k + 1) * P]))
                settle()
                for k in range(GS):
                    do(v_.bn_aggr(mv3[:, g % 2, k, :], st3[:, k, :]))
                settle()
                v_.tensor_scalar(ve3[:, g % 2, :], mv3[:, g % 2, :, 1], 1e-5, None, ALU.add).then_inc(v_var3, 1)

            def shift_of_norm3(g):
                dve.wait_ge(g_rstd3, g + 1)
                if g >= 2:
                    dve.wait_ge(a_z3, g - 1)
                v_.scalar_tensor_tensor(out=nmr3[:, g % 2, :], in0=mv3[:, g % 2, :, 0], scalar=-1.0,
                                        in1=rs3[:, g % 2, :], op0=ALU.mult, op1=ALU.mult).then_inc(v_nmr3, 1)

            def scale3(g):
                dve.wait_ge(a_z3, g + 1)
                if g >= 2:
                    dve.wait_ge(g_o3, g - 1)
                v_.tensor_tensor(zg3[:, g % 2], z3[:, g % 2],
                                 g3.rearrange("p (o d) -> p o d", o=1).to_broadcast([P, GS, D]), ALU.mult)\
                    .then_inc(v_zg3, 1)

            dve.wait_ge(l_rows3, 16)
            dve.wait_ge(v_gate, 1)
            combine(0)
            combine(1)
            combine(2)
            stats3(0)
            shift_of_norm3(0)
            combine(3)
            for g in range(1, NG):
                stats3(g)
                shift_of_norm3(g)
                scale3(g - 1)
            scale3(NG - 1)


def kernel(**inputs):
    import numpy as _np
    import concourse.bacc as _bacc
    from concourse import mybir as _mybir
    from concourse.bass_utils import run_bass_kernel_spmd as _run

    a = {name: _np.asarray(v) for name, v in inputs.items()}
    nb, _, d = a["x"].shape

    def columns(v):
        v = v.reshape(-1, min(v.shape[-1], P))
        return _np.pad(v.T, ((0, P - v.shape[1]), (0, 0)))

    def down(m):
        return _np.pad(m, ((0, P - m.shape[0]), (0, 0)))

    th, ph = a["condB_theta"], a["condB_phi"]
    down_t = a["L3_cond_down_W"].T
    swapped = down_t.reshape(d // 2, 2, -1)[:, ::-1].reshape(d, -1)
    small = _np.concatenate([
        _np.tile(_np.stack([th, th, ph, ph]), (d // 4, 1)),
        _np.tile(_np.array([[-1.0], [1.0]], _np.float32), (d // 2, 1)),
        columns(a["L0_cond_bi"]), columns(a["L1_cond_exp_b1"]), columns(a["L1_cond_hyp_b1"]),
        columns(a["L1_cond_hyp_b2"]), columns(a["L1_cond_sty_b1"]), columns(a["L1_cond_sty_b2"]),
        columns(a["L1_cond_ln_g"]), columns(a["L1_cond_ln_b"]), columns(a["L3_cond_down_b"]),
        down(a["L1_cond_subj_emb"]), down(a["L1_cond_hyp_w1"]), down(a["L1_cond_hyp_w2"]),
        down(a["L1_cond_sty_w1"]), down(a["L1_cond_sty_w2"]), down(a["L1_cond_router_w"]),
        down_t, swapped, down(a["L3_cond_up_W"].T), down(a["L3_cond_expert_b"]), down(a["L3_cond_domain_emb"]),
    ], axis=1)
    laid_out = [
        ("x", a["x"]),
        ("ids3", _np.concatenate([a["itok_B_0_7"], a["itok_B_6_14"], a["itok_B_0_15"]])),
        ("l0_wi", a["L0_cond_Wi"]),
        ("l0_wo", a["L0_cond_Wo"]),
        ("l0_rows", _np.stack([a["L0_cond_bo"], a["L0_cond_gamma"], a["L0_cond_beta"]])),
        ("small", small),
        ("exp_w1", a["L1_cond_exp_w1"]),
        ("exp_w2", a["L1_cond_exp_w2"]),
        ("exp_b2", a["L1_cond_exp_b2"]),
        ("l3_w", a["L3_cond_expert_W"]),
        ("l3_rows", _np.stack([a["L3_cond_ln_gamma"], a["L3_cond_ln_beta"], a["L3_cond_up_b"]])),
    ]
    nc = _bacc.Bacc("TRN2", target_bir_lowering=False, num_devices=1)
    arrays, args = {}, []
    for name, v in laid_out:
        v = _np.ascontiguousarray(v)
        arrays[f"in_{name}"] = v
        args.append(nc.dram_tensor(f"in_{name}", v.shape, _mybir.dt.from_np(v.dtype), kind="ExternalInput").ap())
    args.append(nc.dram_tensor("out_dram", a["x"].shape, _mybir.dt.float32, kind="ExternalOutput").ap())
    conditional_layers_kernel(nc, *args)
    r = _run(nc, [arrays], core_ids=[0])
    return r.results[0]["out_dram"]
```

```python
from contextlib import ExitStack

import concourse.bass as bass
from concourse import mybir

F32 = mybir.dt.float32
BF16 = mybir.dt.bfloat16
I32 = mybir.dt.int32
U32 = mybir.dt.uint32
ALU = mybir.AluOpType
ACT = mybir.ActivationFunctionType
AX = mybir.AxisListType

P = 128
ROUND = 12582912.0
TWO_PI_HI = 6.28125
TWO_PI_LO = 0.0019353071795864769
PI = 3.1415925
FAR = 1.0e6


def small_layout(sizes):
    at, cols = {}, 0
    for name, width in sizes:
        at[name] = (cols, width)
        cols += width
    return at, cols


def conditional_layers_kernel(nc, x, ids3, l0_wi, l0_wo, l0_rows, small_in, exp_w1, exp_w2, exp_b2,
                              l3_w, l3_rows, out, small_sizes, subjects):
    NB, S, D = x.shape
    E0, _, FF = l0_wi.shape
    E1 = exp_w1.shape[0]
    at, small_cols = small_layout(small_sizes)
    NS = subjects
    SE, SH, SM = (at[name][1] for name in ("emb", "hyp_w1", "sty_w1"))
    E3, A, _ = l3_w.shape
    FC = FF // P
    GS = 4
    NG = NB // GS
    GW = GS * D
    TOPK = 2
    NROW = NB * S
    BLOCKS = (TOPK * NROW + E1 * (P - 1)) // P
    KT = TOPK * NB
    ACT_HOTS = 12
    WARM_BLOCKS, WARM_L3 = 3, 10
    W0_SLOTS = 6
    WARM_START = 4
    LOOPS = 3
    RING, AHEAD = 8, 7
    EARLY = 2
    LAG = 2
    assert S == P and D == P and GW == 512 and FC * P == 512

    h_dram = nc.dram_tensor("h_rows", (NROW, D), F32, kind="Internal").ap()
    y_dram = nc.dram_tensor("expert_rows", (TOPK * NROW, D), F32, kind="Internal").ap()

    with ExitStack() as ctx:
        def sb(name, shape, dt=F32):
            return ctx.enter_context(nc.sbuf_tensor(name, shape, dt))

        def sem(name):
            return ctx.enter_context(nc.semaphore(name))

        bank = [ctx.enter_context(nc.psum_tensor(f"bank{i}", [P, 512], F32)) for i in range(8)]

        ident = sb("ident", [P, P])
        behind = sb("behind", [P, P], BF16)
        ones_bf = sb("ones_bf", [P, P], BF16)
        ones_row = sb("ones_row", [1, NB])
        warm = sb("warm", [1, NB])
        minus_half = sb("minus_half", [P, 16])
        col_i = sb("col_i", [P, P], I32)
        col_f = sb("col_f", [P, P])
        col_bf = sb("col_bf", [P, P], BF16)
        part_i = sb("part_i", [P, 1], I32)
        part_f = sb("part_f", [P, 1])
        scan_mask = sb("scan_mask", [P, E1, NB])

        ids = sb("ids", [NS, 3, NB], I32)
        ids_f = sb("ids_f", [NS, 3, NB])
        id3_clip = sb("id3_clip", [NS, NB])
        id3_clip_i = sb("id3_clip_i", [1, NB], I32)
        valid = sb("valid", [NS, NB])
        invalid = sb("invalid", [NS, NB])
        pick_subj = sb("pick_subj", [NS, NB])
        pick_l3 = sb("pick_l3", [E3, NB])
        pick_l3_valid = sb("pick_l3_valid", [E3, NB])
        assert small_cols == small_in.shape[1]
        small = sb("small", [P, small_cols])
        col = {name: first for name, (first, _) in at.items()}
        part = lambda name, rows: small[0:rows, at[name][0]:at[name][0] + at[name][1]]
        cols = small
        R_BI, R_B1, R_H1, R_H2, R_S1, R_S2, R_LG, R_LB, R_DB = (
            col[n] for n in ("l0_bi", "exp_b1", "hyp_b1", "hyp_b2", "sty_b1", "sty_b2", "ln_g", "ln_b", "down_b"))
        S_SIGN = col["sign"]
        angle = part("angle", P)
        arg = sb("arg", [P, 2, NB])
        turns = sb("turns", [P, 2, NB])
        trig = sb("trig", [P, 2, NB])
        rot_same = sb("rot_same", [P, NB])
        rot_swap = sb("rot_swap", [P, NB])
        emb_sb = part("emb", NS)
        hw1 = part("hyp_w1", SE)
        hw2 = part("hyp_w2", SH)
        sw1 = part("sty_w1", SH)
        sw2 = part("sty_w2", SM)
        hyp_a = sb("hyp_a", [SE, NB])
        hyp_b = sb("hyp_b", [SH, NB])
        hyp_c = sb("hyp_c", [SH, NB])
        hyp_d = sb("hyp_d", [SM, NB])
        g_pre = sb("g_pre", [P, NB])
        g_abs = sb("g_abs", [P, NB])
        g_exp = sb("g_exp", [P, NB])
        g_ln = sb("g_ln", [P, NB])
        g_pos = sb("g_pos", [P, NB])
        film_g = sb("film_g", [P, NB])
        film_b = sb("film_b", [P, NB])
        g_sq = sb("g_sq", [P, 1])
        rw = part("router_w", P)

        x_sb = sb("x_sb", [P, NB, D])
        xT = sb("xT", [P, 2, GW])
        w0_place = sb("w0_place", [P, 2 * W0_SLOTS * FF])
        wi = w0_place[:, 0:W0_SLOTS * FF].rearrange("p (s f) -> p s f", s=W0_SLOTS)
        wo = w0_place[:, W0_SLOTS * FF:].rearrange("p (s c d) -> p s c d", s=W0_SLOTS, c=FC)
        rows0 = sb("rows0", [P, NB, 3, D])
        act0 = sb("act0", [P, 2, FC, P])
        x_bo = sb("x_bo", [P, 2, GS, D])
        z0 = sb("z0", [P, 2, GS, D])
        zg = sb("zg", [P, 2, GS, D])
        x1 = sb("x1", [P, NB, D])
        st = sb("st", [P, 4, GS, 6])
        mv = sb("mv", [P, 3, GS, 2])
        veps = sb("veps", [P, 3, GS])
        rstd = sb("rstd", [P, 3, GS])

        z1 = sb("z1", [P, 2, GS, D])
        film = sb("film", [P, 2, 6, GS])
        hT = sb("hT", [P, 2, GW])
        h_row = sb("h_row", [P, 2, GS, D])
        top_v = sb("top_v", [P, NB, 8])
        top_i = sb("top_i", [P, GS, 8], U32)
        pick = sb("pick", [P, TOPK, E1, NB], BF16)
        both = sb("both", [P, E1, NB], BF16)
        run = sb("run", [P, E1, NB])
        pos = sb("pos", [P, E1, NB])
        blk = sb("blk", [P, E1])
        blk_end = sb("blk_end", [P, E1])
        blk_start = sb("blk_start", [P, E1])
        slot_e = sb("slot_e", [P, TOPK, E1, NB])
        slot = sb("slot", [P, KT])
        blk_of = sb("blk_of", [P, KT])
        in_blk = sb("in_blk", [P, KT])
        hot_in = sb("hot_in", [P, KT, P], BF16)
        hot_blk = sb("hot_blk", [P, KT, 2, BLOCKS], BF16)
        hot_tmp = sb("hot_tmp", [P, KT, BLOCKS], BF16)
        minus_in_blk = sb("minus_in_blk", [P, ACT_HOTS])
        hot_off = sb("hot_off", [P, ACT_HOTS, P])
        blk_of_bf = sb("blk_of_bf", [P, KT], BF16)
        dest = sb("dest", [P, BLOCKS])
        wrap = sb("wrap", [P, BLOCKS])
        src_f = sb("src_f", [P, BLOCKS])
        pad = sb("pad", [P, BLOCKS])
        src_i = sb("src_i", [P, BLOCKS], I32)
        dest_i = sb("dest_i", [P, BLOCKS], I32)
        exp_cmp = sb("exp_cmp", [1, BLOCKS, E1])
        exp_f = sb("exp_f", [1, BLOCKS])
        exp_i = sb("exp_i", [1, BLOCKS], I32)
        soft = sb("soft", [P, NB, 8])
        soft_in = sb("soft_in", [P, NB, 8])
        soft_s = sb("soft_s", [P, 4, NB])
        gates = sb("gates", [P, TOPK, NB])
        w1 = sb("w1", [P, E1, FF])
        w2 = sb("w2", [P, E1, FC, D])
        b2_tab = sb("b2_tab", [P, E1, D])
        got = sb("got", [P, RING, D])
        gotT = sb("gotT", [P, 2, P])

        flat0 = rows0[:].rearrange("p b i d -> p (b i d)")
        taken = [0]

        def of_rows0(size):
            first = taken[0]
            taken[0] += size
            assert taken[0] <= NB * 3 * D
            return flat0[:, first:first + size]

        w1_now = of_rows0(2 * FF).rearrange("p (i f) -> p i f", i=2)
        hid = of_rows0(2 * FF).rearrange("p (i c d) -> p i c d", i=2, c=FC)
        y_blk = of_rows0(4 * D).rearrange("p (i d) -> p i d", i=4)
        rot_diag = of_rows0(D)
        dw_rot = of_rows0(NB * A).rearrange("p (b a) -> p b a", b=NB)
        dw_tmp = of_rows0(NB * A).rearrange("p (b a) -> p b a", b=NB)

        dwT = part("down_T", P)
        dwT_sw = part("down_T_swapped", P)
        uwT = part("up_T", A)
        w3 = sb("w3", [A, NB, A])
        w3v = sb("w3v", [A, NB, A])
        eye3 = sb("eye3", [A, NB, A])
        b3 = part("l3_b", E3)
        e3 = part("l3_emb", E3)
        c3 = sb("c3", [A, NB])
        bias3 = sb("bias3", [NB, D])
        m3 = sb("m3", [A + 1, NB, D])
        rows3 = sb("rows3", [P, 3, D])
        g3, be3, ub = rows3[:, 0, :], rows3[:, 1, :], rows3[0:1, 2, :]
        assert NG * TOPK * GS * D <= 2 * W0_SLOTS * FF
        y_in = w0_place[:, 0:NG * TOPK * GS * D].rearrange("p (g k t d) -> p g k t d", g=NG, k=TOPK, t=GS)
        u_a, u_b, uT, rot, z3, o3 = x_bo, z0, xT, x_sb, zg, z1
        zg3 = sb("zg3", [P, 2, GS, D])
        a3 = sb("a3", [A + 1, 2, GW])
        st3 = sb("st3", [P, GS, 6])
        mv3 = sb("mv3", [P, 2, GS, 2])
        ve3 = sb("ve3", [P, 2, GS])
        rs3 = sb("rs3", [P, 2, GS])
        nmr3 = sb("nmr3", [P, 2, GS])

        l_ids = sem("l_ids")
        l_x = [sem(f"l_x{g}") for g in range(NG)]
        l_w0 = [sem(f"l_w0_{s}") for s in range(W0_SLOTS)]
        l_rows0 = [sem(f"l_rows0_{g}") for g in range(NG)]
        l_small = sem("l_small")
        l_rows3 = sem("l_rows3")
        l_w1 = sem("l_w1")
        l_w3 = sem("l_w3")
        l_m3 = sem("l_m3")
        l_y = [sem(f"l_y{g}") for g in range(NG)]
        k_pool = sem("k_pool")
        k_dve = sem("k_dve")
        v_ids = sem("v_ids")
        p_pro = sem("p_pro")
        v_pro = sem("v_pro")
        v_soft_in = sem("v_soft_in")
        a_soft = sem("a_soft")
        v_arg = sem("v_arg")
        a_trig = sem("a_trig")
        v_diag = sem("v_diag")
        v_rot = sem("v_rot")
        vc = sem("vc")
        gc = sem("gc")
        ac = sem("ac")
        p_xT = sem("p_xT")
        a_xT = sem("a_xT")
        p_up = sem("p_up")
        a_gelu = sem("a_gelu")
        p_down = sem("p_down")
        g_xbo = sem("g_xbo")
        p_sum = sem("p_sum")
        v_var = sem("v_var")
        g_rstd = sem("g_rstd")
        v_z0 = sem("v_z0")
        g_x1 = sem("g_x1")
        v_z1 = sem("v_z1")
        p_zT = sem("p_zT")
        v_film = sem("v_film")
        a_hT = sem("a_hT")
        p_warm = sem("p_warm")
        p_logit = sem("p_logit")
        p_rt = sem("p_rt")
        v_top = sem("v_top")
        a_hrow = sem("a_hrow")
        st_h = [sem(f"st_h{i}") for i in range(2)]
        p_rank = sem("p_rank")
        v_tmp = sem("v_tmp")
        v_min = sem("v_min")
        a_off = sem("a_off")
        a_hot = sem("a_hot")
        v_hot = sem("v_hot")
        g_hot = sem("g_hot")
        p_inv = sem("p_inv")
        v_idx = sem("v_idx")
        v_exp = sem("v_exp")
        g_w3 = sem("g_w3")
        p_m3 = sem("p_m3")
        a_m3 = sem("a_m3")
        v_smax = sem("v_smax")
        a_sexp = sem("a_sexp")
        v_gate = sem("v_gate")
        gat = [sem(f"gat{i}") for i in range(RING)]
        sca = [sem(f"sca{i}") for i in range(4)]
        p_gT = sem("p_gT")
        v_gT = sem("v_gT")
        p_u = sem("p_u")
        v_w1 = sem("v_w1")
        a_hid = sem("a_hid")
        p_y = sem("p_y")
        v_y = sem("v_y")
        v_u3 = sem("v_u3")
        p_uT = sem("p_uT")
        a_uT = sem("a_uT")
        p_dn3 = sem("p_dn3")
        a_gelu3 = sem("a_gelu3")
        p_res3 = sem("p_res3")
        p_up3 = sem("p_up3")
        v_nmr3 = sem("v_nmr3")
        a_z3 = sem("a_z3")
        v_var3 = sem("v_var3")
        g_rstd3 = sem("g_rstd3")
        v_zg3 = sem("v_zg3")
        v_o3 = sem("v_o3")
        g_o3 = sem("g_o3")
        s_out = [sem(f"s_out{i}") for i in range(2)]

        class Chain:

            def __init__(self, eng, s):
                self.eng, self.s, self.n = eng, s, 0

            def do(self, ins):
                self.n += 1
                return ins.then_inc(self.s, 1)

            def settle(self):
                self.eng.wait_ge(self.s, self.n)

            def wait_for(self, count):
                self.eng.wait_ge(self.s, count)

        block = ctx.enter_context(nc.Block())

        y_v = y_dram.rearrange("(k t p) d -> p k t d", k=TOPK, p=P)
        row = lambda ap: ap.rearrange("(o n) -> o n", o=1)
        pro = bank[7]
        c0 = 0
        q_se, q_h1, q_h2, q_s1, q_ga, q_be = (pro[:, c0 + NB * i:c0 + NB * (i + 1)] for i in range(6))
        q_c3 = bank[5][:, 0:NB]
        q_bias3 = bank[0][0:NB, 0:D]

        @block.sync
        def _(sp):
            sp.dma_start(ids[:].rearrange("p k b -> p (k b)"), row(ids3).to_broadcast([NS, 3 * NB])).then_inc(l_ids, 16)
            sp.wait_ge(l_ids, 16)
            for b in range(NB):
                e = sp.value_load(ids[0:1, 0, b:b + 1], min_val=0, max_val=E0 - 1)
                slot_ = b % W0_SLOTS
                if b >= W0_SLOTS:
                    sp.wait_ge(p_down, b - W0_SLOTS + 1)
                sp.dma_start(wi[:, slot_, :], l0_wi[bass.ds(e, 1)].rearrange("o h i -> h (o i)"))\
                    .then_inc(l_w0[slot_], 16)
                sp.dma_start(wo[:, slot_, :, :], l0_wo[bass.ds(e, 1)].rearrange("o (c p) h -> p (o c) h", p=P))\
                    .then_inc(l_w0[slot_], 16)
                sp.dma_start(rows0[:, b].rearrange("p i d -> p (i d)"),
                             l0_rows[bass.ds(e, 1)].rearrange("o i d -> o (i d)").to_broadcast([P, 3 * D]))\
                    .then_inc(l_rows0[b // GS], 16)
            sp.wait_ge(v_ids, 1)
            for b in range(NB):
                e = sp.value_load(id3_clip_i[0:1, b:b + 1], min_val=0, max_val=E3 - 1)
                sp.dma_start(w3[:, b, :], l3_w[bass.ds(e, 1)].rearrange("o p a -> p (o a)")).then_inc(l_w3, 16)
            for i in range(E1):
                sp.dma_start(w1[:, i, :], exp_w1[i]).then_inc(l_w1, 16)
                sp.dma_start(w2[:, i], exp_w2[i].rearrange("(c p) d -> p c d", p=P)).then_inc(l_w1, 16)
            sp.dma_start(b2_tab[:], exp_b2.rearrange("(o e) d -> o e d", o=1).to_broadcast([P, E1, D]))\
                .then_inc(l_w1, 16)
            sp.wait_ge(v_pro, 7)
            sp.dma_start(m3[A:A + 1, :, :], bias3[:]).then_inc(l_m3, 16)
            for i in range(4):
                sp.wait_ge(sca[i], 16 * len(range(i, BLOCKS, 4)))
            for g in range(NG):
                sp.dma_start(y_in[:, g, 0], y_v[:, 0, GS * g:GS * (g + 1), :]).then_inc(l_y[g], 16)
            for g in range(NG):
                if g < NG - 1:
                    sp.wait_ge(g_o3, g + 1)
                else:
                    sp.wait_ge(v_o3, 1)
                sp.dma_start(out[GS * g:GS * (g + 1)].rearrange("b s d -> s b d"), o3[:, g % 2])\
                    .then_inc(s_out[g % 2], 16)
            for i in range(2):
                sp.wait_ge(s_out[i], 16 * NG // 2)

        @block.gpsimd
        def _(pool):
            g_ = nc.gpsimd
            ch = Chain(pool, gc)
            g_.memset(ones_row[:], 1.0).then_inc(k_pool, 1)
            g_.memset(ident[:], 0.0).then_inc(k_pool, 1)
            g_.iota(col_i[:], [[1, P]], base=0, channel_multiplier=0).then_inc(k_pool, 1)
            g_.iota(part_i[:], [[0, 1]], base=0, channel_multiplier=1).then_inc(k_pool, 1)
            pool.wait_ge(k_pool, 4)
            g_.affine_select(out=ident[:], in_=ident[:], compare_op=ALU.not_equal, fill=1.0, base=0,
                             pattern=[[-1, P]], channel_multiplier=1).then_inc(k_pool, 1)
            g_.memset(minus_half[:], -0.5).then_inc(k_pool, 1)
            g_.memset(ones_bf[:], 1.0).then_inc(k_pool, 1)
            g_.memset(behind[:], -1.0).then_inc(k_pool, 1)
            g_.memset(scan_mask[:], 1.0).then_inc(k_pool, 1)
            g_.memset(a3[:], 1.0).then_inc(k_pool, 1)
            pool.wait_ge(k_pool, 10)
            g_.affine_select(out=behind[:], in_=behind[:], compare_op=ALU.is_ge, fill=0.0, base=0,
                             pattern=[[-1, P]], channel_multiplier=1).then_inc(k_pool, 1)
            g_.memset(scan_mask[:, :, 0:1], 0.0).then_inc(k_pool, 1)
            g_.memset(eye3[:], 0.0).then_inc(k_pool, 1)
            pool.wait_ge(k_pool, 13)
            g_.affine_select(out=eye3[:], in_=eye3[:], compare_op=ALU.not_equal, fill=1.0, base=0,
                             pattern=[[0, NB], [-1, A]], channel_multiplier=1).then_inc(k_pool, 1)

            def add_bo(g):
                pool.wait_ge(l_x[g], 16)
                pool.wait_ge(l_rows0[g], 16 * GS)
                if g >= 2:
                    pool.wait_ge(p_sum, g - 1)
                bs = slice(GS * g, GS * (g + 1))
                g_.tensor_tensor(x_bo[:, g % 2], x_sb[:, bs, :], rows0[:, bs, 0, :], ALU.add).then_inc(g_xbo, 1)

            turn = [0]

            def power(kind):
                turn[0] += 1
                pool.wait_ge(v_var, turn[0])
                g_.tensor_tensor(rstd[:, kind, :], veps[:, kind, :], minus_half[:, 0:GS], ALU.pow)\
                    .then_inc(g_rstd, 1)

            def scale_shift(g):
                pool.wait_ge(v_z0, g + 1)
                bs = slice(GS * g, GS * (g + 1))
                ch.do(g_.tensor_tensor(zg[:, g % 2], z0[:, g % 2], rows0[:, bs, 1, :], ALU.mult))
                ch.settle()
                g_.tensor_tensor(x1[:, bs, :], zg[:, g % 2], rows0[:, bs, 2, :], ALU.add).then_inc(g_x1, 1)

            add_bo(0)
            for g in range(NG):
                power(0)
                if g + 1 < NG:
                    add_bo(g + 1)
                scale_shift(g)
                if g >= 1:
                    power(2)
                power(1)
            pool.wait_ge(l_w3, 16 * NB)
            pool.wait_ge(v_ids, 1)
            over_a = lambda v: v[0:A, :].rearrange("p (b o) -> p b o", o=1).to_broadcast([A, NB, A])
            ch.do(g_.tensor_tensor(w3v[:], w3[:], over_a(valid), ALU.mult))
            ch.do(g_.tensor_tensor(eye3[:], eye3[:], over_a(invalid), ALU.mult))
            ch.settle()
            g_.tensor_tensor(w3v[:], w3v[:], eye3[:], ALU.add).then_inc(g_w3, 1)
            power(2)

            pool.wait_ge(v_tmp, 1)
            g_.tensor_tensor(hot_blk[:, :, 1, :], hot_tmp[:],
                             col_bf[:, 1:KT + 1].rearrange("p (j o) -> p j o", o=1).to_broadcast([P, KT, BLOCKS]),
                             ALU.mult).then_inc(g_hot, 1)
            pool.wait_ge(v_idx, 1)
            for i in range(2):
                pool.wait_ge(st_h[i], 16 * NG // 2)

            def gather(n):
                if n >= RING:
                    pool.wait_ge(p_gT, n - RING + 1)
                g_.indirect_dma_start(got[:, n % RING, :], None, h_dram,
                                      bass.IndirectOffsetOnAxis(ap=src_i[:, n:n + 1], axis=0))\
                    .then_inc(gat[n % RING], 16)

            def scatter(n):
                if n == 0:
                    pool.wait_ge(v_idx, 2)
                pool.wait_ge(v_y, n + 1)
                g_.indirect_dma_start(y_dram, bass.IndirectOffsetOnAxis(ap=dest_i[:, n:n + 1], axis=0),
                                      y_blk[:, n % 4, :], None,
                                      bounds_check=TOPK * NROW - 1, oob_is_err=False)\
                    .then_inc(sca[n % 4], 16)

            for n in range(AHEAD):
                gather(n)
            for n in range(BLOCKS):
                if n + AHEAD < BLOCKS:
                    gather(n + AHEAD)
                scatter(n)

            def power3(g):
                pool.wait_ge(v_var3, g + 1)
                g_.tensor_tensor(rs3[:, g % 2, :], ve3[:, g % 2, :], minus_half[:, 0:GS], ALU.pow)\
                    .then_inc(g_rstd3, 1)

            def shift3(g):
                if g == 1:
                    pool.wait_ge(v_zg3, 1)
                else:
                    pool.wait_ge(a_z3, g + 1)
                    ch.do(g_.tensor_tensor(zg3[:, g % 2], z3[:, g % 2],
                                           g3.rearrange("p (o d) -> p o d", o=1).to_broadcast([P, GS, D]), ALU.mult))
                    ch.settle()
                if g >= 2:
                    pool.wait_ge(s_out[g % 2], 16 * (g // 2))
                g_.tensor_tensor(o3[:, g % 2], zg3[:, g % 2],
                                 be3.rearrange("p (o d) -> p o d", o=1).to_broadcast([P, GS, D]), ALU.add)\
                    .then_inc(g_o3, 1)

            pool.wait_ge(l_rows3, 16)
            power3(0)
            for g in range(NG):
                if g + 1 < NG:
                    power3(g + 1)
                    shift3(g)

        @block.scalar
        def _(act):
            a_ = nc.scalar

            def store_rows(g):
                act.wait_ge(p_rt, g + 1)
                if g >= 2:
                    act.wait_ge(st_h[g % 2], 16 * (g // 2))
                a_.activation(h_row[:, g % 2], bank[7][:], ACT.Copy).then_inc(a_hrow, 1)
                act.wait_ge(a_hrow, g + 1)
                act.dma_start(h_dram.rearrange("(t p) d -> p t d", p=P)[:, GS * g:GS * (g + 1), :], h_row[:, g % 2])\
                    .then_inc(st_h[g % 2], 16)

            def load_x(g):
                act.dma_start(x_sb[:, GS * g:GS * (g + 1), :],
                              x[GS * g:GS * (g + 1)].rearrange("b s d -> s b d")).then_inc(l_x[g], 16)

            load_x(0)
            act.dma_start(small[:], small_in).then_inc(l_small, 16)
            act.wait_ge(k_pool, 9)
            a_.activation(warm[:], ones_row[:], ACT.Gelu).then_inc(ac, 1)
            def evac_xT(g):
                act.wait_ge(p_xT, g + 1)
                if g >= 2:
                    act.wait_ge(p_up, GS * (g - 1))
                a_.activation(xT[:, g % 2, :], bank[0][:], ACT.Copy).then_inc(a_xT, 1)

            def film_h(g):
                act.wait_ge(v_film, g + 1)
                if g >= 2:
                    act.wait_ge(p_rt, g - 1)
                for k in range(GS):
                    a_.activation(hT[:, g % 2, k * P:(k + 1) * P], bank[5][:, k * P:(k + 1) * P],
                                  ACT.Identity, bias=film[:, g % 2, 1, k:k + 1],
                                  scale=film[:, g % 2, 0, k:k + 1]).then_inc(a_hT, 1)

            evac_xT(0)
            load_x(1)
            act.wait_ge(l_ids, 16)
            act.wait_ge(l_small, 16)

            def expert0(b):
                return act.value_load(ids[0:1, 0, b:b + 1], min_val=0, max_val=E0 - 1)

            e = expert0(0)
            for b in range(NB):
                act.wait_ge(p_up, b + 1)
                if b >= 2:
                    act.wait_ge(p_down, b - 1)
                for c in range(FC):
                    last = a_.activation(act0[:, b % 2, c, :], bank[1 + b % 2][:, c * P:(c + 1) * P], ACT.Gelu,
                                         bias=cols[:, bass.ds(e * FC + (R_BI + c), 1)])
                last.then_inc(a_gelu, 1)
                if b + 1 < NB:
                    e = expert0(b + 1)
                g, k = divmod(b, GS)
                if k == 1 and g + 1 < NG:
                    evac_xT(g + 1)
                if k == 2 and g + 2 < NG:
                    load_x(g + 2)
                if b == GS + 3:
                    act.dma_start(rows3[:].rearrange("p i d -> p (i d)"),
                                  row(l3_rows.rearrange("i d -> (i d)")).to_broadcast([P, 3 * D]))\
                        .then_inc(l_rows3, 16)
                if b == GS + 3:
                    act.wait_ge(v_soft_in, 1)
                    a_.activation(g_exp[:], g_abs[:], ACT.Exp, scale=-1.0).then_inc(ac, 1)
                    act.wait_ge(ac, 2)
                    a_.activation(g_ln[:], g_exp[:], ACT.Ln, bias=1.0).then_inc(a_soft, 1)
                if k == 0 and g >= 3:
                    film_h(g - 3)
                if k == 2 and g >= 3:
                    store_rows(g - 3)
            act.wait_ge(v_arg, 1)
            a_.activation(trig[:], arg[:], ACT.Sin).then_inc(a_trig, 1)
            for g in range(NG - 3, NG):
                film_h(g)
                store_rows(g)
            act.wait_ge(v_min, 1)
            for j in range(ACT_HOTS):
                last = a_.activation(hot_off[:, j, :], col_f[:], ACT.Abs, bias=minus_in_blk[:, j:j + 1])
            last.then_inc(a_off, 1)
            act.wait_ge(a_off, 1)
            a_.activation(hot_in[:, KT - ACT_HOTS:KT, :], hot_off[:], ACT.Relu, bias=1.0, scale=-1.0)\
                .then_inc(a_hot, 1)
            for i in range(4):
                act.wait_ge(p_m3, i + 1)
                a_.activation(m3[0:A, GS * i:GS * (i + 1), :], bank[1 + i][0:A, :], ACT.Copy).then_inc(a_m3, 1)
            act.wait_ge(v_smax, 1)
            a_.activation(soft[:], soft_in[:], ACT.Exp).then_inc(a_sexp, 1)

            def hidden(turn, k):
                n = turn * RING + k
                e = act.value_load(exp_i[0:1, bass.ds(n, 1)], min_val=0, max_val=E1 - 1)
                act.wait_ge(p_u, n + 1)
                if k >= 2:
                    act.wait_ge(p_y, n - 1)
                for c in range(FC):
                    last = a_.activation(hid[:, k % 2, c, :], bank[k % 2][:, c * P:(c + 1) * P], ACT.Relu,
                                         bias=cols[:, bass.ds(e * FC + (R_B1 + c), 1)])
                last.then_inc(a_hid, 1)

            act.wait_ge(v_exp, 1)
            for k in range(RING):
                hidden(0, k)
            with act.Fori(0, LOOPS) as turn:
                for k in range(RING, 2 * RING):
                    hidden(turn, k)
            for k in range((LOOPS + 1) * RING, BLOCKS):
                hidden(0, k)

            a_.activation(warm[:], ones_row[:], ACT.Gelu).then_inc(ac, 1)
            for i in range(4):
                act.wait_ge(sca[i], 16 * len(range(i, BLOCKS, 4)))
            for g in range(NG):
                act.dma_start(y_in[:, g, 1], y_v[:, 1, GS * g:GS * (g + 1), :]).then_inc(l_y[g], 16)

            def evac_uT(g):
                act.wait_ge(p_uT, g + 1)
                if g >= 2:
                    act.wait_ge(p_res3, g - 1)
                a_.activation(uT[:, g % 2, :], bank[g % 2][:], ACT.Copy).then_inc(a_uT, 1)

            def gelu3(g):
                act.wait_ge(p_dn3, g + 1)
                if g >= 2:
                    act.wait_ge(p_up3, g - 1)
                a_.activation(a3[0:A, g % 2, :], bank[2 + g % 2][0:A, :], ACT.Gelu,
                              bias=cols[0:A, R_DB:R_DB + 1]).then_inc(a_gelu3, 1)

            def norm3(g):
                act.wait_ge(v_nmr3, g + 1)
                if g >= 2:
                    act.wait_ge(g_o3, g - 1)
                for k in range(GS if g < NG - 1 else GS // 2):
                    last = a_.activation(z3[:, g % 2, k, :], bank[4 + g][:, k * P:(k + 1) * P], ACT.Identity,
                                         bias=nmr3[:, g % 2, k:k + 1], scale=rs3[:, g % 2, k:k + 1])
                last.then_inc(a_z3, 1)

            evac_uT(0)
            for g in range(NG):
                gelu3(g)
                if g + 1 < NG:
                    evac_uT(g + 1)
                if g >= 1:
                    norm3(g - 1)
            norm3(NG - 1)

        @block.tensor
        def _(pe):
            t_ = nc.tensor

            def mm(out_, lhsT, rhs, start=True, stop=True):
                return t_.matmul(out_, lhsT, rhs, start=start, stop=stop)

            def x_transposes(g):
                pe.wait_ge(l_x[g], 16)
                if g >= 1:
                    pe.wait_ge(a_xT, g)
                for k in range(GS):
                    last = t_.transpose(bank[0][:, k * P:(k + 1) * P], x_sb[:, GS * g + k, :], ident[:])
                last.then_inc(p_xT, 1)

            def keep_warm(n, rhs):
                for _ in range(n):
                    mm(bank[6][:, 0:rhs.shape[1]], ident[:], rhs).then_inc(p_warm, 1)

            pe.wait_ge(k_pool, 5)
            keep_warm(WARM_START, ident[:])
            x_transposes(0)

            def hypernetwork(i):
                if i == 0:
                    pe.wait_ge(l_small, 16)
                    pe.wait_ge(v_ids, 1)
                    mm(q_se[0:SE], emb_sb, pick_subj[:]).then_inc(p_pro, 1)
                else:
                    pe.wait_ge(v_pro, i)
                if i == 1:
                    mm(q_h1[0:SH], hw1, hyp_a[:]).then_inc(p_pro, 1)
                if i == 2:
                    mm(q_h2[0:SH], hw2, hyp_b[:]).then_inc(p_pro, 1)
                if i == 3:
                    mm(q_s1[0:SM], sw1, hyp_c[:]).then_inc(p_pro, 1)
                if i == 4:
                    mm(q_ga, sw2[:, 0:D], hyp_d[:])
                    mm(q_be, sw2[:, D:2 * D], hyp_d[:]).then_inc(p_pro, 1)
                    mm(q_c3[0:A], b3, pick_l3_valid[:], stop=False)
                    mm(q_c3[0:A], e3, pick_l3[:], start=False).then_inc(p_pro, 1)

            def up(b):
                pe.wait_ge(a_xT, b // GS + 1)
                pe.wait_ge(l_w0[b % W0_SLOTS], 32 * (b // W0_SLOTS + 1))
                if b >= 2:
                    pe.wait_ge(a_gelu, b - 1)
                for c in range(FC):
                    last = mm(bank[1 + b % 2][:, c * P:(c + 1) * P], wi[:, b % W0_SLOTS, c * P:(c + 1) * P],
                              xT[:, (b // GS) % 2, (b % GS) * P:(b % GS + 1) * P])
                last.then_inc(p_up, 1)

            def down(b):
                g, k = divmod(b, GS)
                pe.wait_ge(a_gelu, b + 1)
                if k == 0 and g >= 2:
                    pe.wait_ge(v_z0, g - 1)
                for c in range(FC):
                    last = mm(bank[3 + g % 2][:, k * P:(k + 1) * P], act0[:, b % 2, c, :], wo[:, b % W0_SLOTS, c, :],
                              start=(k == 0 and c == 0), stop=False)
                last.then_inc(p_down, 1)
                if k == GS - 1:
                    pe.wait_ge(g_xbo, g + 1)
                    mm(bank[3 + g % 2][:], ident[:], x_bo[:, g % 2].rearrange("p k d -> p (k d)"), start=False)\
                        .then_inc(p_sum, 1)

            def z_transposes(g):
                if g >= 1:
                    pe.wait_ge(a_hT, GS * g)
                else:
                    pe.wait_ge(v_pro, 6)
                for k in range(GS):
                    pe.wait_ge(v_z1, GS * g + k + 1)
                    last = t_.transpose(bank[5][:, k * P:(k + 1) * P], z1[:, g % 2, k, :], ident[:])
                last.then_inc(p_zT, 1)

            def route(g):
                if g >= 1:
                    pe.wait_ge(a_hrow, g)
                    pe.wait_ge(v_top, g)
                else:
                    pe.wait_ge(v_pro, 6)
                for k in range(GS):
                    pe.wait_ge(a_hT, GS * g + k + 1)
                    last = mm(bank[6][:, k * E1:(k + 1) * E1], hT[:, g % 2, k * P:(k + 1) * P], rw)
                last.then_inc(p_logit, 1)
                for k in range(GS):
                    last = t_.transpose(bank[7][:, k * P:(k + 1) * P], hT[:, g % 2, k * P:(k + 1) * P], ident[:])
                last.then_inc(p_rt, 1)

            hypernetwork(0)
            keep_warm(WARM_START, ident[:])
            for b in range(NB):
                g, k = divmod(b, GS)
                if k == 1 and g + 1 < NG:
                    x_transposes(g + 1)
                up(b)
                if b < 4:
                    hypernetwork(b + 1)
                if b >= 1:
                    down(b - 1)
                if k == 1 and g >= 3:
                    route(g - 3)
                if k == 1 and g >= 2:
                    z_transposes(g - 2)
            down(NB - 1)
            def l3_matrix(b):
                last = mm(bank[1 + b // GS][0:A, (b % GS) * D:(b % GS + 1) * D], w3v[:, b, :], uwT)
                if b % GS == GS - 1:
                    last.then_inc(p_m3, 1)

            pe.wait_ge(v_pro, 6)
            pe.wait_ge(a_xT, NG)
            pe.wait_ge(l_rows3, 16)
            mm(q_bias3, c3[:], uwT, stop=False)
            mm(q_bias3, ones_row[:], ub, start=False).then_inc(p_pro, 1)
            route(NG - 3)
            z_transposes(NG - 2)
            route(NG - 2)
            z_transposes(NG - 1)
            pe.wait_ge(g_w3, 1)
            pe.wait_ge(v_z0, NG)
            for b in range(NB // 4):
                l3_matrix(b)
            route(NG - 1)
            pe.wait_ge(v_top, NG)
            mm(bank[6][:, 128:256], behind[:], both[:].rearrange("p e t -> p (e t)"))
            mm(bank[6][:, 256:384], ones_bf[:], both[:].rearrange("p e t -> p (e t)")).then_inc(p_rank, 1)
            for b in range(NB // 4, NB):
                l3_matrix(b)
            pe.wait_ge(v_hot, 1)
            pe.wait_ge(g_hot, 1)
            pe.wait_ge(v_pro, 7)
            for j in range(KT):
                if j == KT - ACT_HOTS:
                    pe.wait_ge(a_hot, 1)
                if j % 4 == 0 and j < KT - ACT_HOTS:
                    pe.wait_ge(v_hot, j // 4 + 2)
                last = mm(bank[5][:, 0:2 * BLOCKS], hot_in[:, j, :],
                          hot_blk[:, j].rearrange("p a n -> p (a n)"), start=(j == 0), stop=(j == KT - 1))
            last.then_inc(p_inv, 1)

            pe.wait_ge(l_w1, 16 * (2 * E1 + 1))
            keep_warm(WARM_BLOCKS, w1[:, 0, :])
            pe.wait_ge(a_m3, 4)
            pe.wait_ge(v_idx, 1)
            pe.wait_ge(a_hrow, NG)

            def rows_T(turn, k):
                pe.wait_ge(gat[k % RING], 16 * (turn + (k // RING + 1)))
                if k >= 2:
                    pe.wait_ge(v_gT, turn * RING + (k - 1))
                t_.transpose(bank[6 + k % 2][:, 0:P], got[:, k % RING, :], ident[:]).then_inc(p_gT, 1)

            def blk_up(turn, k):
                n = turn * RING + k
                pe.wait_ge(v_gT, n + 1)
                pe.wait_ge(v_w1, n + 1)
                if k >= 2:
                    pe.wait_ge(a_hid, n - 1)
                for c in range(FC):
                    last = mm(bank[k % 2][:, c * P:(c + 1) * P], w1_now[:, k % 2, c * P:(c + 1) * P],
                              gotT[:, k % 2, :])
                last.then_inc(p_u, 1)

            def blk_down(turn, k, e):
                n = turn * RING + k
                pe.wait_ge(a_hid, n + 1)
                if k >= 2:
                    pe.wait_ge(v_y, n - 1)
                for c in range(FC):
                    last = mm(bank[4 + k % 2][:, 0:D], hid[:, k % 2, c, :],
                              w2[:, bass.ds(e, 1), c, :].rearrange("p o d -> p (o d)"),
                              start=(c == 0), stop=(c == FC - 1))
                last.then_inc(p_y, 1)

            def blk_step(turn, k):
                if k >= LAG + EARLY:
                    e = pe.value_load(exp_i[0:1, bass.ds(turn * RING + (k - LAG), 1)], min_val=0, max_val=E1 - 1)
                if k < BLOCKS:
                    blk_up(turn, k)
                if k + 1 < BLOCKS:
                    rows_T(turn, k + 1)
                if 1 <= k <= EARLY:
                    blk_down(0, k - 1, pe.value_load(exp_i[0:1, k - 1:k], min_val=0, max_val=E1 - 1))
                elif k >= LAG + EARLY:
                    blk_down(turn, k - LAG, e)

            rows_T(0, 0)
            for k in range(RING):
                blk_step(0, k)
            with pe.Fori(0, LOOPS) as turn:
                for k in range(RING, 2 * RING):
                    blk_step(turn, k)
            for k in range((LOOPS + 1) * RING, BLOCKS + LAG):
                blk_step(0, k)

            keep_warm(WARM_L3, w1[:, 0, :])

            def l3_T(g):
                pe.wait_ge(v_u3, GS * (g + 1))
                if g >= 2:
                    pe.wait_ge(a_uT, g - 1)
                for k in range(GS):
                    last = t_.transpose(bank[g % 2][:, k * P:(k + 1) * P], u_b[:, g % 2, k, :], ident[:])
                last.then_inc(p_uT, 1)

            def l3_down(g):
                pe.wait_ge(a_uT, g + 1)
                if g >= 2:
                    pe.wait_ge(a_gelu3, g - 1)
                for k in range(GS):
                    last = mm(bank[2 + g % 2][0:A, k * P:(k + 1) * P], dw_rot[:, GS * g + k, :],
                              uT[:, g % 2, k * P:(k + 1) * P])
                last.then_inc(p_dn3, 1)

            def l3_residual(g):
                for k in range(GS):
                    ks = slice(k * P, (k + 1) * P)
                    last = mm(bank[4 + g][:, ks], uT[:, g % 2, ks], rot[:, GS * g + k, :],
                              start=(k == 0), stop=False)
                last.then_inc(p_res3, 1)

            def l3_up(g):
                pe.wait_ge(a_gelu3, g + 1)
                for k in range(GS):
                    ks = slice(k * P, (k + 1) * P)
                    last = mm(bank[4 + g][:, ks], a3[:, g % 2, ks], m3[:, GS * g + k, :], start=False,
                              stop=(k == GS - 1))
                last.then_inc(p_up3, 1)

            pe.wait_ge(l_m3, 16)
            pe.wait_ge(v_y, BLOCKS)
            pe.wait_ge(v_rot, NB + 1)
            l3_T(0)
            for g in range(NG):
                l3_down(g)
                l3_residual(g)
                if g + 1 < NG:
                    l3_T(g + 1)
                l3_up(g)

        @block.vector
        def _(dve):
            v_ = nc.vector
            ch = Chain(dve, vc)
            do, settle = ch.do, ch.settle
            dve.wait_ge(k_pool, 4)
            v_.tensor_copy(col_f[:], col_i[:]).then_inc(k_dve, 1)
            v_.tensor_copy(col_bf[:], col_i[:]).then_inc(k_dve, 1)
            v_.tensor_copy(part_f[:], part_i[:]).then_inc(k_dve, 1)
            dve.wait_ge(l_ids, 16)
            do(v_.tensor_copy(ids_f[:], ids[:]))
            settle()
            dve.wait_ge(k_dve, 3)
            do(v_.tensor_scalar(id3_clip[:], ids_f[:, 2, :], 0.0, float(E3 - 1), ALU.max, ALU.min))
            do(v_.tensor_scalar(invalid[:], ids_f[:, 2, :], 0.0, None, ALU.is_ge))
            do(v_.tensor_scalar(pick_subj[:], ids_f[:, 1, :], part_f[0:NS, 0:1], None, ALU.is_equal))
            do(v_.tensor_scalar(pick_l3_valid[:], ids_f[0:E3, 2, :], part_f[0:E3, 0:1], None, ALU.is_equal))
            settle()
            do(v_.tensor_copy(id3_clip_i[:], id3_clip[0:1, :]))
            do(v_.tensor_scalar(pick_l3[:], id3_clip[0:E3, :], part_f[0:E3, 0:1], None, ALU.is_equal))
            do(v_.scalar_tensor_tensor(out=valid[:], in0=ids_f[:, 2, :], scalar=float(E3), in1=invalid[:],
                                       op0=ALU.is_lt, op1=ALU.mult))
            settle()
            v_.tensor_scalar(invalid[:], valid[:], -1.0, 1.0, ALU.mult, ALU.add).then_inc(v_ids, 1)
            dve.wait_ge(l_small, 16)
            do(v_.tensor_copy(arg[:, 0, :], angle))
            do(v_.tensor_scalar(arg[:, 1, :], angle, 1.5707963267948966, None, ALU.add))
            settle()
            do(v_.tensor_scalar(turns[:], arg[:], 0.15915494309189535, ROUND, ALU.mult, ALU.add))
            settle()
            do(v_.tensor_scalar(turns[:], turns[:], -ROUND, None, ALU.add))
            settle()
            do(v_.scalar_tensor_tensor(out=arg[:], in0=turns[:], scalar=-TWO_PI_HI, in1=arg[:],
                                       op0=ALU.mult, op1=ALU.add))
            settle()
            do(v_.scalar_tensor_tensor(out=arg[:], in0=turns[:], scalar=-TWO_PI_LO, in1=arg[:],
                                       op0=ALU.mult, op1=ALU.add))
            settle()
            v_.tensor_scalar(arg[:], arg[:], PI, -PI, ALU.min, ALU.max).then_inc(v_arg, 1)

            dve.wait_ge(p_pro, 1)
            v_.tensor_copy(hyp_a[:], q_se[0:SE]).then_inc(v_pro, 1)
            dve.wait_ge(p_pro, 2)
            v_.tensor_scalar(hyp_b[:], q_h1, cols[:, R_H1:R_H1 + 1], 0.0, ALU.add, ALU.max).then_inc(v_pro, 1)
            dve.wait_ge(p_pro, 3)
            v_.tensor_scalar(hyp_c[:], q_h2, cols[:, R_H2:R_H2 + 1], None, ALU.add).then_inc(v_pro, 1)
            dve.wait_ge(p_pro, 4)
            v_.tensor_scalar(hyp_d[:], q_s1[0:SM], cols[0:SM, R_S1:R_S1 + 1], 0.0, ALU.add, ALU.max)\
                .then_inc(v_pro, 1)
            dve.wait_ge(p_pro, 5)
            do(v_.tensor_scalar(g_pre[:], q_ga, cols[:, R_S2:R_S2 + 1], None, ALU.add))
            v_.tensor_scalar(film_b[:], q_be, cols[:, R_S2 + 1:R_S2 + 2], None, ALU.add).then_inc(v_pro, 1)
            settle()
            v_.scalar_tensor_tensor(out=g_abs[:], in0=g_pre[:], scalar=-1.0, in1=g_pre[:],
                                    op0=ALU.mult, op1=ALU.max).then_inc(v_soft_in, 1)
            do(v_.tensor_scalar(g_pos[:], g_pre[:], 0.0, 1e-8, ALU.max, ALU.add))
            do(v_.tensor_tensor(g_sq[:], cols[:, R_LG:R_LG + 1], cols[:, R_LG:R_LG + 1], ALU.mult))
            dve.wait_ge(p_pro, 6)
            v_.tensor_copy(c3[:], q_c3[0:A]).then_inc(v_pro, 1)
            settle()

            def film_gain():
                dve.wait_ge(a_soft, 1)
                do(v_.tensor_tensor(film_g[:], g_pos[:], g_ln[:], ALU.add))
                settle()

            def stats(kind, src):
                before = ch.n
                for k in range(GS):
                    do(v_.bn_stats(st[:, kind, k, :], src(k)))
                for k in range(GS):
                    ch.wait_for(before + k + 1)
                    do(v_.bn_aggr(mv[:, kind, k, :], st[:, kind, k, :]))
                settle()

            def l0_stats(g):
                dve.wait_ge(p_sum, g + 1)
                stats(0, lambda k: bank[3 + g % 2][:, k * P:(k + 1) * P])
                v_.tensor_scalar(veps[:, 0, :], mv[:, 0, :, 1], 1e-12, None, ALU.add).then_inc(v_var, 1)

            turns_of_power = [(0, 0), (1, 0)]
            for g in range(1, NG):
                turns_of_power += [(0, g), (2, g - 1), (1, g)]
            turns_of_power.append((2, NG - 1))

            def normalise(dst, src, kind, g):
                dve.wait_ge(g_rstd, turns_of_power.index((kind, g)) + 1)
                return [v_.tensor_scalar(dst[:, k, :], src(k), mv[:, kind, k, 0:1], rstd[:, kind, k:k + 1],
                                         ALU.subtract, ALU.mult) for k in range(GS)]

            def l0_norm(g):
                if g >= 2:
                    dve.wait_ge(g_x1, g - 1)
                normalise(z0[:, g % 2], lambda k: bank[3 + g % 2][:, k * P:(k + 1) * P], 0, g)[-1].then_inc(v_z0, 1)

            def l1_stats(g):
                dve.wait_ge(g_x1, g + 1)
                stats(1, lambda k: x1[:, GS * g + k, :])
                v_.tensor_scalar(veps[:, 1, :], mv[:, 1, :, 1], 1e-5, None, ALU.add).then_inc(v_var, 1)

            def l1_norm(g):
                if g >= 2:
                    dve.wait_ge(p_zT, g - 1)
                for ins in normalise(z1[:, g % 2], lambda k: x1[:, GS * g + k, :], 1, g):
                    ins.then_inc(v_z1, 1)

            g_col, b_col = cols[:, R_LG:R_LG + 1], cols[:, R_LB:R_LB + 1]

            def row_stats(g):
                dve.wait_ge(p_zT, g + 1)
                stats(2, lambda k: bank[5][:, k * P:(k + 1) * P])
                v_.tensor_scalar(veps[:, 2, :], mv[:, 2, :, 1], g_sq[:], 1e-8, ALU.mult, ALU.add)\
                    .then_inc(v_var, 1)
                if g >= 2:
                    dve.wait_ge(a_hT, GS * (g - 1))
                f = film[:, g % 2]
                do(v_.tensor_scalar(f[:, 2, :], mv[:, 2, :, 0], g_col, b_col, ALU.mult, ALU.add))
                settle()
                do(v_.tensor_scalar(f[:, 3, :], f[:, 2, :], -1.0, b_col, ALU.mult, ALU.add))

            def film_factors(g):
                dve.wait_ge(g_rstd, turns_of_power.index((2, g)) + 1)
                bs = slice(GS * g, GS * (g + 1))
                f = film[:, g % 2]
                do(v_.tensor_tensor(f[:, 4, :], rstd[:, 2, :], film_g[:, bs], ALU.mult))
                settle()
                do(v_.tensor_scalar(f[:, 0, :], f[:, 4, :], g_col, None, ALU.mult))
                do(v_.tensor_tensor(f[:, 5, :], f[:, 4, :], f[:, 3, :], ALU.mult))
                settle()
                v_.tensor_tensor(f[:, 1, :], f[:, 5, :], film_b[:, bs], ALU.add).then_inc(v_film, 1)

            def top2(g):
                dve.wait_ge(p_logit, g + 1)
                ts = slice(GS * g, GS * (g + 1))
                before = ch.n
                for k in range(GS):
                    do(v_.max(top_v[:, GS * g + k, :], bank[6][:, k * E1:(k + 1) * E1]))
                for k in range(GS):
                    ch.wait_for(before + k + 1)
                    do(v_.max_index(top_i[:, k, :], top_v[:, GS * g + k, :], bank[6][:, k * E1:(k + 1) * E1]))
                settle()
                for c in range(TOPK):
                    do(v_.tensor_tensor(pick[:, c, :, ts],
                                        col_f[:, 0:E1].rearrange("p (e o) -> p e o", o=1).to_broadcast([P, E1, GS]),
                                        top_i[:, :, c].rearrange("p (o t) -> p o t", o=1).to_broadcast([P, E1, GS]),
                                        ALU.is_equal))
                settle()
                v_.tensor_tensor(both[:, :, ts], pick[:, 0, :, ts], pick[:, 1, :, ts], ALU.add).then_inc(v_top, 1)

            for g in range(NG):
                l0_stats(g)
                if g >= 1:
                    l1_norm(g - 1)
                l0_norm(g)
                if g >= 1:
                    row_stats(g - 1)
                if g == 1:
                    film_gain()
                if g >= 2:
                    top2(g - 2)
                if g >= 1:
                    film_factors(g - 1)
                l1_stats(g)
            l1_norm(NG - 1)
            row_stats(NG - 1)
            film_factors(NG - 1)
            top2(NG - 2)
            dve.wait_ge(p_pro, 7)
            v_.tensor_copy(bias3[:], q_bias3).then_inc(v_pro, 1)
            top2(NG - 1)

            dve.wait_ge(p_rank, 1)
            flat = lambda t: t[:].rearrange("p e t -> p (e t)")
            do(v_.tensor_tensor_scan(flat(run), flat(scan_mask), bank[6][:, 256:384], 0.0, ALU.mult, ALU.add))
            settle()
            do(v_.tensor_scalar(blk[:], run[:, :, NB - 1], float(P - 1) - (P - 1) / 2, 1.0 / P, ALU.add, ALU.mult))
            do(v_.tensor_tensor(flat(pos), flat(run), bank[6][:, 128:256], ALU.add))
            settle()
            do(v_.tensor_scalar(blk[:], blk[:], ROUND, -ROUND, ALU.add, ALU.add))
            settle()
            do(v_.tensor_tensor_scan(blk_end[:], scan_mask[:, :, 1], blk[:], 0.0, ALU.mult, ALU.add))
            settle()
            do(v_.tensor_tensor(blk_start[:], blk_end[:], blk[:], ALU.subtract))
            settle()
            do(v_.scalar_tensor_tensor(out=pos[:], in0=blk_start[:].rearrange("p (e o) -> p e o", o=1)
                                       .to_broadcast([P, E1, NB]), scalar=float(P), in1=pos[:],
                                       op0=ALU.mult, op1=ALU.add))
            settle()
            do(v_.tensor_tensor(slot_e[:].rearrange("p k e t -> p k (e t)"),
                                pick[:].rearrange("p k e t -> p k (e t)"),
                                pos[:].rearrange("p (o e) t -> p o (e t)", o=1).to_broadcast([P, TOPK, E1 * NB]),
                                ALU.mult))
            settle()
            do(v_.tensor_reduce(slot[:].rearrange("p (k t) -> p k t", k=TOPK),
                                slot_e[:].rearrange("p k e t -> p k t e"), AX.X, ALU.add))
            settle()
            do(v_.tensor_scalar(blk_of[:], slot[:], -(P - 1) / 2, 1.0 / P, ALU.add, ALU.mult))
            settle()
            do(v_.tensor_scalar(blk_of[:], blk_of[:], ROUND, -ROUND, ALU.add, ALU.add))
            settle()
            do(v_.scalar_tensor_tensor(out=in_blk[:], in0=blk_of[:], scalar=-float(P), in1=slot[:],
                                       op0=ALU.mult, op1=ALU.add))
            do(v_.tensor_copy(blk_of_bf[:], blk_of[:]))
            settle()
            v_.tensor_scalar(minus_in_blk[:], in_blk[:, KT - ACT_HOTS:KT], -1.0, None, ALU.mult).then_inc(v_min, 1)
            settle()
            v_.tensor_tensor(hot_tmp[:], col_bf[:, 0:BLOCKS].rearrange("p (o n) -> p o n", o=1)
                                .to_broadcast([P, KT, BLOCKS]),
                                blk_of_bf[:].rearrange("p (j o) -> p j o", o=1).to_broadcast([P, KT, BLOCKS]),
                                ALU.is_equal).then_inc(v_tmp, 1)
            dve.wait_ge(v_tmp, 1)
            v_.tensor_scalar(hot_blk[:, :, 0, :], hot_tmp[:], part_f[:], None, ALU.mult).then_inc(v_hot, 1)
            for j in range(KT - ACT_HOTS):
                last = v_.tensor_scalar(hot_in[:, j, :], col_bf[:], in_blk[:, j:j + 1], None, ALU.is_equal)
                if j % 4 == 3:
                    last.then_inc(v_hot, 1)
            do(v_.tensor_tensor(exp_cmp[:], col_f[0:1, 0:BLOCKS].rearrange("p (n o) -> p n o", o=1)
                                .to_broadcast([1, BLOCKS, E1]),
                                blk_end[0:1, :].rearrange("p (o e) -> p o e", o=1).to_broadcast([1, BLOCKS, E1]),
                                ALU.is_ge))
            settle()
            do(v_.tensor_reduce(exp_f[:], exp_cmp[:], AX.X, ALU.add))
            settle()
            v_.tensor_scalar(exp_i[:], exp_f[:], float(E1 - 1), None, ALU.min).then_inc(v_exp, 1)
            dve.wait_ge(p_inv, 1)
            do(v_.tensor_copy(wrap[:], bank[5][:, 0:BLOCKS]))
            settle()
            do(v_.scalar_tensor_tensor(out=dest[:], in0=bank[5][:, BLOCKS:2 * BLOCKS], scalar=float(P),
                                       in1=wrap[:], op0=ALU.mult, op1=ALU.add))
            settle()
            do(v_.tensor_scalar(wrap[:], dest[:], float(NROW + P), -float(NROW), ALU.is_ge, ALU.mult))
            do(v_.tensor_scalar(pad[:], dest[:], float(P), FAR, ALU.is_lt, ALU.mult))
            settle()
            do(v_.scalar_tensor_tensor(out=src_f[:], in0=dest[:], scalar=-float(P), in1=wrap[:],
                                       op0=ALU.add, op1=ALU.add))
            settle()
            v_.tensor_scalar(src_i[:], src_f[:], 0.0, None, ALU.max).then_inc(v_idx, 1)
            v_.scalar_tensor_tensor(out=dest_i[:], in0=dest[:], scalar=-float(P), in1=pad[:],
                                    op0=ALU.add, op1=ALU.add).then_inc(v_idx, 1)
            v_.tensor_tensor(soft_in[:], top_v[:], top_v[:, :, 0:1].to_broadcast([P, NB, 8]), ALU.subtract)\
                .then_inc(v_smax, 1)

            def gate_values():
                dve.wait_ge(a_sexp, 1)
                do(v_.tensor_reduce(soft_s[:, 0, :], soft[:], AX.X, ALU.add))
                settle()
                do(v_.reciprocal(soft_s[:, 1, :], soft_s[:, 0, :]))
                settle()
                do(v_.tensor_tensor(soft[:], soft[:], soft_s[:, 1, :].rearrange("p (t o) -> p t o", o=1)
                                    .to_broadcast([P, NB, 8]), ALU.mult))
                settle()
                do(v_.tensor_tensor(soft_s[:, 2, :], soft[:, :, 0], soft[:, :, 1], ALU.add))
                settle()
                do(v_.reciprocal(soft_s[:, 3, :], soft_s[:, 2, :]))
                settle()
                for c in range(TOPK):
                    last = v_.tensor_tensor(gates[:, c, :], soft[:, :, c], soft_s[:, 3, :], ALU.mult)
                    if c == 0:
                        do(last)
                last.then_inc(v_gate, 1)

            swapped = lambda ap: ap.rearrange("p (q j) -> p q j", j=2)[:, :, ::-1]
            paired = lambda ap: ap.rearrange("p (q j) -> p q j", j=2)

            def rotation(b):
                dve.wait_ge(v_rot, b + 1)
                v_.tensor_scalar(rot_diag, ident[:], rot_same[:, b:b + 1], None, ALU.mult).then_inc(v_diag, 1)
                dve.wait_ge(v_diag, b + 1)
                v_.scalar_tensor_tensor(out=paired(rot[:, b, :]), in0=swapped(ident[:]),
                                        scalar=rot_swap[:, b:b + 1], in1=paired(rot_diag),
                                        op0=ALU.mult, op1=ALU.add).then_inc(v_rot, 1)

            def rotation_factors():
                dve.wait_ge(a_trig, 1)
                do(v_.tensor_copy(rot_same[:], trig[:, 1, :]))
                v_.tensor_scalar(rot_swap[:], trig[:, 0, :], small[:, S_SIGN:S_SIGN + 1], None, ALU.mult)\
                    .then_inc(v_rot, 1)
                settle()
                dve.wait_ge(v_rot, 1)

            def down_rotated(step):
                over_b = lambda t: t.rearrange("p (o a) -> p o a", o=1).to_broadcast([P, NB, A])
                over_a_ = lambda t: t[:].rearrange("p (b o) -> p b o", o=1).to_broadcast([P, NB, A])
                if step == 0:
                    do(v_.tensor_tensor(dw_rot, over_b(dwT), over_a_(rot_same), ALU.mult))
                if step == 1:
                    do(v_.tensor_tensor(dw_tmp, over_b(dwT_sw), over_a_(rot_swap), ALU.mult))
                if step == 2:
                    settle()
                    do(v_.tensor_tensor(dw_rot, dw_rot, dw_tmp, ALU.add))

            expert = {}

            def load_expert(n):
                expert[n] = dve.value_load(exp_i[0:1, n:n + 1], min_val=0, max_val=E1 - 1)

            def rows_T(n):
                dve.wait_ge(p_gT, n + 1)
                if n >= 2:
                    dve.wait_ge(p_u, n - 1)
                v_.tensor_copy(gotT[:, n % 2, :], bank[6 + n % 2][:, 0:P]).then_inc(v_gT, 1)

            def stage_w1(n):
                if n >= 2:
                    dve.wait_ge(p_u, n - 1)
                v_.tensor_copy(w1_now[:, n % 2, :], w1[:, bass.ds(expert[n], 1), :].rearrange("p o f -> p (o f)"))\
                    .then_inc(v_w1, 1)

            def add_b2(n):
                dve.wait_ge(p_y, n + 1)
                if n >= 4:
                    dve.wait_ge(sca[n % 4], 16 * (n // 4))
                v_.tensor_tensor(y_blk[:, n % 4, :], bank[4 + n % 2][:, 0:D],
                                 b2_tab[:, bass.ds(expert.pop(n), 1), :].rearrange("p o d -> p (o d)"), ALU.add)\
                    .then_inc(v_y, 1)

            dve.wait_ge(l_w1, 16 * (2 * E1 + 1))
            load_expert(0)
            load_expert(1)
            gate_values()
            stage_w1(0)
            rows_T(0)
            for k in range(BLOCKS + LAG):
                if k + 1 < BLOCKS:
                    stage_w1(k + 1)
                    rows_T(k + 1)
                if k + 2 < BLOCKS:
                    load_expert(k + 2)
                if 1 <= k <= EARLY:
                    add_b2(k - 1)
                elif k >= LAG + EARLY:
                    add_b2(k - LAG)
                if k == 3:
                    rotation_factors()
                elif 4 <= k < 7:
                    down_rotated(k - 4)
                elif RING <= k < RING + NB:
                    rotation(k - RING)

            def combine(g):
                dve.wait_ge(l_y[g], 32)
                before = ch.n
                for k in range(GS):
                    t = GS * g + k
                    do(v_.scalar_tensor_tensor(out=u_a[:, g % 2, k, :], in0=y_in[:, g, 0, k, :],
                                               scalar=gates[:, 0, t:t + 1], in1=x1[:, t, :],
                                               op0=ALU.mult, op1=ALU.add))
                if g >= 2:
                    dve.wait_ge(p_uT, g - 1)
                for k in range(GS):
                    ch.wait_for(before + k + 1)
                    t = GS * g + k
                    v_.scalar_tensor_tensor(out=u_b[:, g % 2, k, :], in0=y_in[:, g, 1, k, :],
                                            scalar=gates[:, 1, t:t + 1], in1=u_a[:, g % 2, k, :],
                                            op0=ALU.mult, op1=ALU.add).then_inc(v_u3, 1)

            def stats3(g):
                dve.wait_ge(p_up3, g + 1)
                before = ch.n
                for k in range(GS):
                    do(v_.bn_stats(st3[:, k, :], bank[4 + g][:, k * P:(k + 1) * P]))
                for k in range(GS):
                    ch.wait_for(before + k + 1)
                    do(v_.bn_aggr(mv3[:, g % 2, k, :], st3[:, k, :]))
                settle()
                v_.tensor_scalar(ve3[:, g % 2, :], mv3[:, g % 2, :, 1], 1e-5, None, ALU.add).then_inc(v_var3, 1)

            def shift_of_norm3(g):
                dve.wait_ge(g_rstd3, g + 1)
                if g >= 2:
                    dve.wait_ge(a_z3, g - 1)
                v_.scalar_tensor_tensor(out=nmr3[:, g % 2, :], in0=mv3[:, g % 2, :, 0], scalar=-1.0,
                                        in1=rs3[:, g % 2, :], op0=ALU.mult, op1=ALU.mult).then_inc(v_nmr3, 1)

            def scale3():
                g = 1
                dve.wait_ge(a_z3, g + 1)
                v_.tensor_tensor(zg3[:, g % 2], z3[:, g % 2],
                                 g3.rearrange("p (o d) -> p o d", o=1).to_broadcast([P, GS, D]), ALU.mult)\
                    .then_inc(v_zg3, 1)

            def last_scale_shift():
                g = NG - 1
                over_k = lambda v: v.rearrange("p (o d) -> p o d", o=1).to_broadcast([P, GS, D])
                dve.wait_ge(g_o3, g - 1)
                dve.wait_ge(a_z3, g + 1)
                for k in range(GS // 2, GS):
                    do(v_.tensor_scalar(z3[:, g % 2, k, :], bank[4 + g][:, k * P:(k + 1) * P],
                                        rs3[:, g % 2, k:k + 1], nmr3[:, g % 2, k:k + 1], ALU.mult, ALU.add))
                settle()
                do(v_.tensor_tensor(zg3[:, g % 2], z3[:, g % 2], over_k(g3), ALU.mult))
                settle()
                dve.wait_ge(s_out[g % 2], 16 * (g // 2))
                v_.tensor_tensor(o3[:, g % 2], zg3[:, g % 2], over_k(be3), ALU.add).then_inc(v_o3, 1)

            dve.wait_ge(l_rows3, 16)
            dve.wait_ge(v_gate, 1)
            combine(0)
            combine(1)
            combine(2)
            stats3(0)
            combine(3)
            shift_of_norm3(0)
            for g in range(1, NG):
                stats3(g)
                if g == 2:
                    scale3()
                shift_of_norm3(g)
            last_scale_shift()


def kernel(**inputs):
    import numpy as _np
    import concourse.bacc as _bacc
    from concourse import mybir as _mybir
    from concourse.bass_utils import run_bass_kernel_spmd as _run

    a = {name: _np.asarray(v) for name, v in inputs.items()}
    nb, _, d = a["x"].shape

    def columns(v):
        v = v.reshape(-1, min(v.shape[-1], P))
        return _np.pad(v.T, ((0, P - v.shape[1]), (0, 0)))

    def down(m):
        return _np.pad(m, ((0, P - m.shape[0]), (0, 0)))

    th, ph = a["condB_theta"], a["condB_phi"]
    down_t = a["L3_cond_down_W"].T
    swapped = down_t.reshape(d // 2, 2, -1)[:, ::-1].reshape(d, -1)
    small = [
        ("angle", _np.tile(_np.stack([th, th, ph, ph]), (d // 4, 1))),
        ("sign", _np.tile(_np.array([[-1.0], [1.0]], _np.float32), (d // 2, 1))),
        ("l0_bi", columns(a["L0_cond_bi"])),
        ("exp_b1", columns(a["L1_cond_exp_b1"])),
        ("hyp_b1", columns(a["L1_cond_hyp_b1"])),
        ("hyp_b2", columns(a["L1_cond_hyp_b2"])),
        ("sty_b1", columns(a["L1_cond_sty_b1"])),
        ("sty_b2", columns(a["L1_cond_sty_b2"])),
        ("ln_g", columns(a["L1_cond_ln_g"])),
        ("ln_b", columns(a["L1_cond_ln_b"])),
        ("down_b", columns(a["L3_cond_down_b"])),
        ("emb", down(a["L1_cond_subj_emb"])),
        ("hyp_w1", down(a["L1_cond_hyp_w1"])),
        ("hyp_w2", down(a["L1_cond_hyp_w2"])),
        ("sty_w1", down(a["L1_cond_sty_w1"])),
        ("sty_w2", down(a["L1_cond_sty_w2"])),
        ("router_w", down(a["L1_cond_router_w"])),
        ("down_T", down_t),
        ("down_T_swapped", swapped),
        ("up_T", down(a["L3_cond_up_W"].T)),
        ("l3_b", down(a["L3_cond_expert_b"])),
        ("l3_emb", down(a["L3_cond_domain_emb"])),
    ]
    laid_out = [
        ("x", a["x"]),
        ("ids3", _np.concatenate([a["itok_B_0_7"], a["itok_B_6_14"], a["itok_B_0_15"]])),
        ("l0_wi", a["L0_cond_Wi"]),
        ("l0_wo", a["L0_cond_Wo"]),
        ("l0_rows", _np.stack([a["L0_cond_bo"], a["L0_cond_gamma"], a["L0_cond_beta"]], axis=1)),
        ("small", _np.concatenate([v for _, v in small], axis=1)),
        ("exp_w1", a["L1_cond_exp_w1"]),
        ("exp_w2", a["L1_cond_exp_w2"]),
        ("exp_b2", a["L1_cond_exp_b2"]),
        ("l3_w", a["L3_cond_expert_W"]),
        ("l3_rows", _np.stack([a["L3_cond_ln_gamma"], a["L3_cond_ln_beta"], a["L3_cond_up_b"]])),
    ]
    nc = _bacc.Bacc("TRN2", target_bir_lowering=False, num_devices=1)
    arrays, args = {}, []
    for name, v in laid_out:
        v = _np.ascontiguousarray(v)
        arrays[f"in_{name}"] = v
        args.append(nc.dram_tensor(f"in_{name}", v.shape, _mybir.dt.from_np(v.dtype), kind="ExternalInput").ap())
    args.append(nc.dram_tensor("out_dram", a["x"].shape, _mybir.dt.float32, kind="ExternalOutput").ap())
    conditional_layers_kernel(nc, *args, small_sizes=[(name, v.shape[1]) for name, v in small],
                              subjects=a["L1_cond_subj_emb"].shape[0])
    r = _run(nc, [arrays], core_ids=[0])
    return r.results[0]["out_dram"]
```
